# Optimizing a Trainium2 kernel written in Bass

```python
import numpy as np
import jax
import jax.numpy as jnp

def _softmax(x, axis=-1):
    return jax.nn.softmax(x, axis=axis)
def _gelu(x):
    return jax.nn.gelu(x, approximate=True)
def _silu(x):
    return jax.nn.silu(x)
def _sigmoid(x):
    return jax.nn.sigmoid(x)
def _layernorm(x, axis=-1, eps=1e-5):
    m = jnp.mean(x, axis=axis, keepdims=True)
    v = jnp.var(x, axis=axis, keepdims=True)
    return (x - m) / jnp.sqrt(v + eps)
def _scatter_add(tgt, idx, src, axis=0):
    return tgt.at[idx].add(src)
def _segment_sum(src, seg, n):
    return jax.ops.segment_sum(src, seg, n)

kernel_name = 'mk_metaformer_d1_conv_nhwc128_2ec4f1'

def setup_inputs(seed: int = 0):
    np.random.seed(seed)
    _w = jnp.asarray
    def _rec_inputs():
        import jax
        import jax.numpy as jnp
        _gk = jax.random.key(seed)
        x = -0.0005207 + 1.001 * jax.random.normal(jax.random.fold_in(_gk, 1), (4, 32, 128, 128), jnp.float32)
        return x
    x = _rec_inputs()
    def _L0_conv_setup():
        import jax, jax.numpy as jnp
        import numpy as np
        N_HEADS = 16
        TEMPERATURE = 1.0
        EPS = 1e-05

        def _gelu(z):
            return jax.nn.gelu(z, approximate=False)

        def instance_norm(x, g, b):
            mu = jnp.mean(x, axis=(-2, -1), keepdims=True)
            var = jnp.var(x, axis=(-2, -1), keepdims=True)
            return (x - mu) * jax.lax.rsqrt(var + EPS) * g[:, None, None] + b[:, None, None]

        def conv1x1(x, w, b):
            return jnp.einsum('bihw,io->bohw', x, w) + b[None, :, None, None]

        def fourier_resample(x, out_shape):
            if tuple(x.shape[-2:]) == tuple(out_shape):
                return x
            Ho, Wo = out_shape
            xft = jnp.fft.rfftn(x, axes=(-2, -1), norm='forward')
            out = jnp.zeros(x.shape[:-2] + (Ho, Wo // 2 + 1), dtype=xft.dtype)
            hk = min(x.shape[-2], Ho) // 2
            wk = min(xft.shape[-1], Wo // 2 + 1)
            out = out.at[..., :hk, :wk].set(xft[..., :hk, :wk])
            out = out.at[..., -hk:, :wk].set(xft[..., -hk:, :wk])
            return jnp.fft.irfftn(out, s=out_shape, axes=(-2, -1), norm='forward')

        def spectral_conv(x, w, out_shape):
            wc = w[..., 0] + 1j * w[..., 1]
            mh = wc.shape[2] // 2
            mw = wc.shape[3]
            Ho, Wo = out_shape
            xft = jnp.fft.rfftn(x, axes=(-2, -1), norm='forward')
            top = jnp.einsum('bihw,iohw->bohw', xft[:, :, :mh, :mw], wc[:, :, :mh])
            bot = jnp.einsum('bihw,iohw->bohw', xft[:, :, -mh:, :mw], wc[:, :, mh:])
            out_ft = jnp.zeros((x.shape[0], wc.shape[1], Ho, Wo // 2 + 1), dtype=xft.dtype)
            out_ft = out_ft.at[:, :, :mh, :mw].set(top)
            out_ft = out_ft.at[:, :, -mh:, :mw].set(bot)
            return jnp.fft.irfftn(out_ft, s=out_shape, axes=(-2, -1), norm='forward')

        def fno_layer(x, spec_w, skip_w, skip_b, out_shape, norm=None, act=None):
            xs = fourier_resample(conv1x1(x, skip_w, skip_b), out_shape)
            xf = spectral_conv(x, spec_w, out_shape)
            if norm is not None:
                xf = instance_norm(xf, *norm)
            y = xf + xs
            return act(y) if act is not None else y

        def codano_forward(x, key_w, key_skip_w, key_skip_b, query_w, query_skip_w, query_skip_b, value_w, value_skip_w, value_skip_b, proj_w, proj_skip_w, proj_skip_b, norm1_g, norm1_b, attn_norm_g, attn_norm_b, norm2_g, norm2_b, mixer_w1, mixer_skip_w1, mixer_skip_b1, mixer_norm_g1, mixer_norm_b1, mixer_w2, mixer_skip_w2, mixer_skip_b2, mixer_norm_g2, mixer_norm_b2, mixer_out_g, mixer_out_b):
            b, t, H, W = x.shape
            tokens = x.reshape(b * t, 1, H, W)
            tokens_norm = instance_norm(tokens, norm1_g, norm1_b)
            Hs, Ws = (H // 2, W // 2)
            k = fno_layer(tokens_norm, key_w, key_skip_w, key_skip_b, (Hs, Ws))
            q = fno_layer(tokens_norm, query_w, query_skip_w, query_skip_b, (Hs, Ws))
            v = fno_layer(tokens_norm, value_w, value_skip_w, value_skip_b, (H, W))

            def heads_flat(z):
                hh, ww = z.shape[-2:]
                return z.reshape(b, t, N_HEADS, hh * ww).transpose(0, 2, 1, 3)
            kf, qf, vf = (heads_flat(k), heads_flat(q), heads_flat(v))
            scale = jnp.sqrt(jnp.asarray(kf.shape[-1], jnp.float32)) * TEMPERATURE
            dprod = jax.nn.softmax(jnp.einsum('bhtd,bhsd->bhts', qf, kf) / scale, axis=-1)
            attn = jnp.einsum('bhts,bhsd->bhtd', dprod, vf)
            attn = attn.transpose(0, 2, 1, 3).reshape(b * t, N_HEADS, H, W)
            attn = fno_layer(attn, proj_w, proj_skip_w, proj_skip_b, (H, W))
            attn = instance_norm(attn + tokens, attn_norm_g, attn_norm_b)
            m = instance_norm(attn, norm2_g, norm2_b)
            m = fno_layer(m, mixer_w1, mixer_skip_w1, mixer_skip_b1, (H, W), norm=(mixer_norm_g1, mixer_norm_b1), act=_gelu)
            m = fno_layer(m, mixer_w2, mixer_skip_w2, mixer_skip_b2, (H, W), norm=(mixer_norm_g2, mixer_norm_b2))
            out = instance_norm(m, mixer_out_g, mixer_out_b) + attn
            return out.reshape(b, t, H, W)
        key = jax.random.key(seed)
        ks = list(jax.random.split(key, 32))
        f32 = jnp.float32

        def W_(k, shape, s=0.02):
            return (s * jax.random.normal(k, shape)).astype(f32)
        B, T, H, Wd = (4, 32, 128, 128)
        mh_s, mw_s = (16, 9)
        mh_f, mw_f = (32, 17)
        return {'x': jax.random.normal(ks[0], (B, T, H, Wd), dtype=f32), 'key_w': W_(ks[1], (1, N_HEADS, mh_s, mw_s, 2)), 'key_skip_w': W_(ks[2], (1, N_HEADS), 0.5), 'key_skip_b': W_(ks[3], (N_HEADS,)), 'query_w': W_(ks[4], (1, N_HEADS, mh_s, mw_s, 2)), 'query_skip_w': W_(ks[5], (1, N_HEADS), 0.5), 'query_skip_b': W_(ks[6], (N_HEADS,)), 'value_w': W_(ks[7], (1, N_HEADS, mh_s, mw_s, 2)), 'value_skip_w': W_(ks[8], (1, N_HEADS), 0.5), 'value_skip_b': W_(ks[9], (N_HEADS,)), 'proj_w': W_(ks[10], (N_HEADS, 1, mh_f, mw_f, 2)), 'proj_skip_w': W_(ks[11], (N_HEADS, 1), 0.25), 'proj_skip_b': W_(ks[12], (1,)), 'norm1_g': jnp.ones((1,), f32), 'norm1_b': jnp.zeros((1,), f32), 'attn_norm_g': jnp.ones((1,), f32), 'attn_norm_b': jnp.zeros((1,), f32), 'norm2_g': jnp.ones((1,), f32), 'norm2_b': jnp.zeros((1,), f32), 'mixer_w1': W_(ks[13], (1, 1, mh_f, mw_f, 2)), 'mixer_skip_w1': W_(ks[14], (1, 1), 0.5), 'mixer_skip_b1': W_(ks[15], (1,)), 'mixer_norm_g1': jnp.ones((1,), f32), 'mixer_norm_b1': jnp.zeros((1,), f32), 'mixer_w2': W_(ks[16], (1, 1, mh_f, mw_f, 2)), 'mixer_skip_w2': W_(ks[17], (1, 1), 0.5), 'mixer_skip_b2': W_(ks[18], (1,)), 'mixer_norm_g2': jnp.ones((1,), f32), 'mixer_norm_b2': jnp.zeros((1,), f32), 'mixer_out_g': jnp.ones((1,), f32), 'mixer_out_b': jnp.zeros((1,), f32)}
    _L0_conv_all = _L0_conv_setup()
    _L0_conv_in = {k: v for k, v in _L0_conv_all.items() if k in ('key_w', 'key_skip_w', 'key_skip_b', 'query_w', 'query_skip_w', 'query_skip_b', 'value_w', 'value_skip_w', 'value_skip_b', 'proj_w', 'proj_skip_w', 'proj_skip_b', 'norm1_g', 'norm1_b', 'attn_norm_g', 'attn_norm_b', 'norm2_g', 'norm2_b', 'mixer_w1', 'mixer_skip_w1', 'mixer_skip_b1', 'mixer_norm_g1', 'mixer_norm_b1', 'mixer_w2', 'mixer_skip_w2', 'mixer_skip_b2', 'mixer_norm_g2', 'mixer_norm_b2', 'mixer_out_g', 'mixer_out_b', )}
    del _L0_conv_all

    def _L0_ffn_setup():
        import jax, jax.numpy as jnp
        import numpy as np
        BN_EPS = 1e-05
        key = jax.random.key(seed)
        k1, k2, k3 = jax.random.split(key, 3)
        B, T, I, H = (64, 2048, 128, 128)
        x = jax.random.normal(k1, (B, T, I), dtype=jnp.float32)
        W = jax.random.normal(k2, (H, I), dtype=jnp.float32) * (1.0 / np.sqrt(I))
        V = jnp.linalg.qr(jax.random.normal(k3, (H, H), dtype=jnp.float32))[0]
        gamma = jnp.ones((H,), dtype=jnp.float32)
        beta = jnp.zeros((H,), dtype=jnp.float32)
        return {'x': x, 'W': W, 'V': V, 'gamma': gamma, 'beta': beta}
    _L0_ffn_all = _L0_ffn_setup()
    _L0_ffn_in = {k: v for k, v in _L0_ffn_all.items() if k in ('W', 'V', 'gamma', 'beta', )}
    del _L0_ffn_all

    return {
        "x": x,
        "L0_conv_key_w": _L0_conv_in["key_w"],
        "L0_conv_key_skip_w": _L0_conv_in["key_skip_w"],
        "L0_conv_key_skip_b": _L0_conv_in["key_skip_b"],
        "L0_conv_query_w": _L0_conv_in["query_w"],
        "L0_conv_query_skip_w": _L0_conv_in["query_skip_w"],
        "L0_conv_query_skip_b": _L0_conv_in["query_skip_b"],
        "L0_conv_value_w": _L0_conv_in["value_w"],
        "L0_conv_value_skip_w": _L0_conv_in["value_skip_w"],
        "L0_conv_value_skip_b": _L0_conv_in["value_skip_b"],
        "L0_conv_proj_w": _L0_conv_in["proj_w"],
        "L0_conv_proj_skip_w": _L0_conv_in["proj_skip_w"],
        "L0_conv_proj_skip_b": _L0_conv_in["proj_skip_b"],
        "L0_conv_norm1_g": _L0_conv_in["norm1_g"],
        "L0_conv_norm1_b": _L0_conv_in["norm1_b"],
        "L0_conv_attn_norm_g": _L0_conv_in["attn_norm_g"],
        "L0_conv_attn_norm_b": _L0_conv_in["attn_norm_b"],
        "L0_conv_norm2_g": _L0_conv_in["norm2_g"],
        "L0_conv_norm2_b": _L0_conv_in["norm2_b"],
        "L0_conv_mixer_w1": _L0_conv_in["mixer_w1"],
        "L0_conv_mixer_skip_w1": _L0_conv_in["mixer_skip_w1"],
        "L0_conv_mixer_skip_b1": _L0_conv_in["mixer_skip_b1"],
        "L0_conv_mixer_norm_g1": _L0_conv_in["mixer_norm_g1"],
        "L0_conv_mixer_norm_b1": _L0_conv_in["mixer_norm_b1"],
        "L0_conv_mixer_w2": _L0_conv_in["mixer_w2"],
        "L0_conv_mixer_skip_w2": _L0_conv_in["mixer_skip_w2"],
        "L0_conv_mixer_skip_b2": _L0_conv_in["mixer_skip_b2"],
        "L0_conv_mixer_norm_g2": _L0_conv_in["mixer_norm_g2"],
        "L0_conv_mixer_norm_b2": _L0_conv_in["mixer_norm_b2"],
        "L0_conv_mixer_out_g": _L0_conv_in["mixer_out_g"],
        "L0_conv_mixer_out_b": _L0_conv_in["mixer_out_b"],
        "L0_ffn_W": _L0_ffn_in["W"],
        "L0_ffn_V": _L0_ffn_in["V"],
        "L0_ffn_gamma": _L0_ffn_in["gamma"],
        "L0_ffn_beta": _L0_ffn_in["beta"],
    }

def reference(x, L0_conv_key_w, L0_conv_key_skip_w, L0_conv_key_skip_b, L0_conv_query_w, L0_conv_query_skip_w, L0_conv_query_skip_b, L0_conv_value_w, L0_conv_value_skip_w, L0_conv_value_skip_b, L0_conv_proj_w, L0_conv_proj_skip_w, L0_conv_proj_skip_b, L0_conv_norm1_g, L0_conv_norm1_b, L0_conv_attn_norm_g, L0_conv_attn_norm_b, L0_conv_norm2_g, L0_conv_norm2_b, L0_conv_mixer_w1, L0_conv_mixer_skip_w1, L0_conv_mixer_skip_b1, L0_conv_mixer_norm_g1, L0_conv_mixer_norm_b1, L0_conv_mixer_w2, L0_conv_mixer_skip_w2, L0_conv_mixer_skip_b2, L0_conv_mixer_norm_g2, L0_conv_mixer_norm_b2, L0_conv_mixer_out_g, L0_conv_mixer_out_b, L0_ffn_W, L0_ffn_V, L0_ffn_gamma, L0_ffn_beta):
    import jax
    import jax.numpy as jnp
    def _L0_conv_ref(x, key_w, key_skip_w, key_skip_b, query_w, query_skip_w, query_skip_b, value_w, value_skip_w, value_skip_b, proj_w, proj_skip_w, proj_skip_b, norm1_g, norm1_b, attn_norm_g, attn_norm_b, norm2_g, norm2_b, mixer_w1, mixer_skip_w1, mixer_skip_b1, mixer_norm_g1, mixer_norm_b1, mixer_w2, mixer_skip_w2, mixer_skip_b2, mixer_norm_g2, mixer_norm_b2, mixer_out_g, mixer_out_b):
        import jax, jax.numpy as jnp
        import numpy as np
        N_HEADS = 16
        TEMPERATURE = 1.0
        EPS = 1e-05

        def _gelu(z):
            return jax.nn.gelu(z, approximate=False)

        def instance_norm(x, g, b):
            mu = jnp.mean(x, axis=(-2, -1), keepdims=True)
            var = jnp.var(x, axis=(-2, -1), keepdims=True)
            return (x - mu) * jax.lax.rsqrt(var + EPS) * g[:, None, None] + b[:, None, None]

        def conv1x1(x, w, b):
            return jnp.einsum('bihw,io->bohw', x, w) + b[None, :, None, None]

        def fourier_resample(x, out_shape):
            if tuple(x.shape[-2:]) == tuple(out_shape):
                return x
            Ho, Wo = out_shape
            xft = jnp.fft.rfftn(x, axes=(-2, -1), norm='forward')
            out = jnp.zeros(x.shape[:-2] + (Ho, Wo // 2 + 1), dtype=xft.dtype)
            hk = min(x.shape[-2], Ho) // 2
            wk = min(xft.shape[-1], Wo // 2 + 1)
            out = out.at[..., :hk, :wk].set(xft[..., :hk, :wk])
            out = out.at[..., -hk:, :wk].set(xft[..., -hk:, :wk])
            return jnp.fft.irfftn(out, s=out_shape, axes=(-2, -1), norm='forward')

        def spectral_conv(x, w, out_shape):
            wc = w[..., 0] + 1j * w[..., 1]
            mh = wc.shape[2] // 2
            mw = wc.shape[3]
            Ho, Wo = out_shape
            xft = jnp.fft.rfftn(x, axes=(-2, -1), norm='forward')
            top = jnp.einsum('bihw,iohw->bohw', xft[:, :, :mh, :mw], wc[:, :, :mh])
            bot = jnp.einsum('bihw,iohw->bohw', xft[:, :, -mh:, :mw], wc[:, :, mh:])
            out_ft = jnp.zeros((x.shape[0], wc.shape[1], Ho, Wo // 2 + 1), dtype=xft.dtype)
            out_ft = out_ft.at[:, :, :mh, :mw].set(top)
            out_ft = out_ft.at[:, :, -mh:, :mw].set(bot)
            return jnp.fft.irfftn(out_ft, s=out_shape, axes=(-2, -1), norm='forward')

        def fno_layer(x, spec_w, skip_w, skip_b, out_shape, norm=None, act=None):
            xs = fourier_resample(conv1x1(x, skip_w, skip_b), out_shape)
            xf = spectral_conv(x, spec_w, out_shape)
            if norm is not None:
                xf = instance_norm(xf, *norm)
            y = xf + xs
            return act(y) if act is not None else y

        def codano_forward(x, key_w, key_skip_w, key_skip_b, query_w, query_skip_w, query_skip_b, value_w, value_skip_w, value_skip_b, proj_w, proj_skip_w, proj_skip_b, norm1_g, norm1_b, attn_norm_g, attn_norm_b, norm2_g, norm2_b, mixer_w1, mixer_skip_w1, mixer_skip_b1, mixer_norm_g1, mixer_norm_b1, mixer_w2, mixer_skip_w2, mixer_skip_b2, mixer_norm_g2, mixer_norm_b2, mixer_out_g, mixer_out_b):
            b, t, H, W = x.shape
            tokens = x.reshape(b * t, 1, H, W)
            tokens_norm = instance_norm(tokens, norm1_g, norm1_b)
            Hs, Ws = (H // 2, W // 2)
            k = fno_layer(tokens_norm, key_w, key_skip_w, key_skip_b, (Hs, Ws))
            q = fno_layer(tokens_norm, query_w, query_skip_w, query_skip_b, (Hs, Ws))
            v = fno_layer(tokens_norm, value_w, value_skip_w, value_skip_b, (H, W))

            def heads_flat(z):
                hh, ww = z.shape[-2:]
                return z.reshape(b, t, N_HEADS, hh * ww).transpose(0, 2, 1, 3)
            kf, qf, vf = (heads_flat(k), heads_flat(q), heads_flat(v))
            scale = jnp.sqrt(jnp.asarray(kf.shape[-1], jnp.float32)) * TEMPERATURE
            dprod = jax.nn.softmax(jnp.einsum('bhtd,bhsd->bhts', qf, kf) / scale, axis=-1)
            attn = jnp.einsum('bhts,bhsd->bhtd', dprod, vf)
            attn = attn.transpose(0, 2, 1, 3).reshape(b * t, N_HEADS, H, W)
            attn = fno_layer(attn, proj_w, proj_skip_w, proj_skip_b, (H, W))
            attn = instance_norm(attn + tokens, attn_norm_g, attn_norm_b)
            m = instance_norm(attn, norm2_g, norm2_b)
            m = fno_layer(m, mixer_w1, mixer_skip_w1, mixer_skip_b1, (H, W), norm=(mixer_norm_g1, mixer_norm_b1), act=_gelu)
            m = fno_layer(m, mixer_w2, mixer_skip_w2, mixer_skip_b2, (H, W), norm=(mixer_norm_g2, mixer_norm_b2))
            out = instance_norm(m, mixer_out_g, mixer_out_b) + attn
            return out.reshape(b, t, H, W)
        return codano_forward(x, key_w, key_skip_w, key_skip_b, query_w, query_skip_w, query_skip_b, value_w, value_skip_w, value_skip_b, proj_w, proj_skip_w, proj_skip_b, norm1_g, norm1_b, attn_norm_g, attn_norm_b, norm2_g, norm2_b, mixer_w1, mixer_skip_w1, mixer_skip_b1, mixer_norm_g1, mixer_norm_b1, mixer_w2, mixer_skip_w2, mixer_skip_b2, mixer_norm_g2, mixer_norm_b2, mixer_out_g, mixer_out_b)

    def _L0_ffn_ref(x, W, V, gamma, beta):
        import jax, jax.numpy as jnp
        import numpy as np
        BN_EPS = 1e-05
        B, T, H = (x.shape[0], x.shape[1], W.shape[0])
        Wx = jnp.einsum('bti,hi->bth', x, W)
        flat = Wx.reshape(B * T, H)
        mean = jnp.mean(flat, axis=0)
        var = jnp.var(flat, axis=0)
        Wx = ((flat - mean) * jax.lax.rsqrt(var + BN_EPS) * gamma + beta).reshape(B, T, H)
        Vt = V.T

        def step(yt, wx_t):
            yt = jax.nn.sigmoid(wx_t + yt @ Vt)
            return (yt, yt)
        y0 = jnp.zeros((B, H), dtype=Wx.dtype)
        _, ys = jax.lax.scan(step, y0, jnp.swapaxes(Wx, 0, 1))
        return jnp.swapaxes(ys, 0, 1)

    def _gn(v, G=32, eps=1e-5):
        B_, H_, W_, C_ = v.shape
        g = v.reshape(B_, H_, W_, G, C_ // G)
        m = jnp.mean(g, axis=(1, 2, 4), keepdims=True)
        s = jnp.var(g, axis=(1, 2, 4), keepdims=True)
        return ((g - m) / jnp.sqrt(s + eps)).reshape(v.shape)

    def _ln_c(v, eps=1e-6):
        m = jnp.mean(v, axis=-1, keepdims=True)
        s = jnp.var(v, axis=-1, keepdims=True)
        return (v - m) / jnp.sqrt(s + eps)

    def _ln_t(v, eps=1e-5):
        m = jnp.mean(v, axis=-1, keepdims=True)
        s = jnp.var(v, axis=-1, keepdims=True)
        return (v - m) / jnp.sqrt(s + eps)

    def _to_tokens(v):
        B_, H_, W_, C_ = v.shape
        return v.reshape(B_, H_ * W_, C_)
    def _from_tokens(t, like):
        return t.reshape(like.shape)

    x = x + _L0_conv_ref(_ln_c(x), L0_conv_key_w, L0_conv_key_skip_w, L0_conv_key_skip_b, L0_conv_query_w, L0_conv_query_skip_w, L0_conv_query_skip_b, L0_conv_value_w, L0_conv_value_skip_w, L0_conv_value_skip_b, L0_conv_proj_w, L0_conv_proj_skip_w, L0_conv_proj_skip_b, L0_conv_norm1_g, L0_conv_norm1_b, L0_conv_attn_norm_g, L0_conv_attn_norm_b, L0_conv_norm2_g, L0_conv_norm2_b, L0_conv_mixer_w1, L0_conv_mixer_skip_w1, L0_conv_mixer_skip_b1, L0_conv_mixer_norm_g1, L0_conv_mixer_norm_b1, L0_conv_mixer_w2, L0_conv_mixer_skip_w2, L0_conv_mixer_skip_b2, L0_conv_mixer_norm_g2, L0_conv_mixer_norm_b2, L0_conv_mixer_out_g, L0_conv_mixer_out_b)
    t = _to_tokens(x)
    t = t + _L0_ffn_ref(_ln_t(t), L0_ffn_W, L0_ffn_V, L0_ffn_gamma, L0_ffn_beta)
    x = _from_tokens(t, x)
    return x


_drawn_inputs = setup_inputs


def setup_inputs(seed=0):
    import zlib

    import numpy as np

    out = dict(_drawn_inputs(seed))
    spreads = {'L0_ffn_gamma': (1.0, 0.6), 'L0_ffn_beta': (0.0, 0.8)}
    factors = {'L0_conv_key_w': 64.0,
     'L0_conv_key_skip_w': 6.009,
     'L0_conv_key_skip_b': 64.0,
     'L0_conv_query_w': 64.0,
     'L0_conv_query_skip_b': 64.0,
     'L0_conv_value_w': 8.0,
     'L0_conv_value_skip_b': 64.0,
     'L0_conv_proj_w': 5.252}
    for name, (base, spread) in spreads.items():
        noise = np.random.default_rng([zlib.crc32(name.encode()), seed]).standard_normal(out[name].shape)
        drawn = base * np.exp(spread * noise) if base else spread * noise
        out[name] = jnp.asarray(drawn.astype(out[name].dtype))
    for name, factor in factors.items():
        out[name] = (out[name] * factor).astype(out[name].dtype)
    return out
```

```python
from contextlib import ExitStack

import numpy as np
import concourse.bass as bass
from concourse import mybir

F32 = mybir.dt.float32
I32 = mybir.dt.int32
ALU = mybir.AluOpType
ACT = mybir.ActivationFunctionType
AX = mybir.AxisListType

NT, H, W = 128, 128, 128
NB, TB = 4, 32
NH, HG = 16, 4
MH, MW = 32, 16
MODES = MW * 2 * MH
LH, LW = 16, 8
NF = 65
PIX = H * W
LN_C_EPS, EPS = 1e-6, 1e-5
XC = 8
XR = H // XC
LN_DVE = 6
G4 = NT // 4
STEPS, BURN = 32, 10
Q = H // STEPS
CHUNKS = TB * Q
TOL = 1e-6

FUNCS = [("c", 0), ("c", 32)] + [("c", k) for k in range(1, 32)] + [("s", k) for k in range(1, 33)]
COS = {k: i for i, (f, k) in enumerate(FUNCS) if f == "c"}
SIN = {k: i for i, (f, k) in enumerate(FUNCS) if f == "s"}

SCALARS = ["norm1_g", "attn_norm_g", "attn_norm_b", "norm2_g", "norm2_b", "mixer_norm_g1",
           "mixer_norm_b1", "mixer_norm_g2", "mixer_out_g", "mixer_out_b", "mixer_skip_w1",
           "mixer_skip_b1", "mixer_skip_w2"]
ROW_AT = {n: (i, 1) for i, n in enumerate(SCALARS)}
for _i, _n in enumerate(["query_skip_w", "key_skip_w", "value_skip_w", "proj_skip_w"]):
    ROW_AT[_n] = (len(SCALARS) + NH * _i, NH)
ROW_W = len(SCALARS) + 4 * NH
ROW_AT["mixer_w1"] = (ROW_W, MH * 17 * 2)
ROW_AT["mixer_w2"] = (ROW_W + MH * 17 * 2, MH * 17 * 2)
ROW_N = ROW_W + 2 * MH * 17 * 2


def constants():
    n = np.arange(128)

    def func(f, k):
        a = 2 * np.pi * n * k / 128
        return np.cos(a) if f == "c" else np.sin(a)

    basis = np.stack([func(f, k) for f, k in FUNCS], 1) / 128
    g = np.zeros((128, 64))
    for k in range(32):
        g[:, k] = func("c", k) * (1 if k == 0 else 2 ** 0.5)
    for k in range(1, 32):
        g[:, 31 + k] = func("s", k) * 2 ** 0.5
    g = g * 8 / 128
    gram = np.concatenate([g, g * 2 ** 0.5], 1)
    edge = np.stack([func("c", 32), func("s", 32)], 1) * 8 / 128 * 2 ** 0.5
    h = np.concatenate([np.arange(16), np.arange(-16, 0)])
    ah = 2 * np.pi * np.outer(n, h) / 128
    ch, sh = np.cos(ah), np.sin(ah)
    row_modes = np.concatenate([ch, -sh, -sh, -ch], 1) / 128
    aw = 2 * np.pi * np.outer(n, np.arange(17)) / 128
    cw, sw = np.cos(aw), np.sin(aw)
    col_modes = np.concatenate([cw, -sw, -sw, -cw, sw, cw], 1) / 128
    basis17 = np.concatenate([cw, sw[:, 1:]], 1) / 128
    fr = np.zeros((128, 128))
    fr[:64] = np.concatenate([ch.T, -sh.T], 0)
    block = np.zeros((128, 512))
    for j in range(4):
        block[32 * j:32 * j + 16, 128 * j:128 * j + 128] = 2 * cw.T[1:17]
        block[32 * j + 16:32 * j + 32, 128 * j:128 * j + 128] = 2 * sw.T[1:17]
    at, out, x = {}, [], 0
    for name, p in (("ident", np.eye(128)), ("basis", basis), ("gram", gram), ("edge", edge),
                    ("row_modes", row_modes), ("col_modes", col_modes), ("basis17", basis17),
                    ("fr", fr), ("block", block), ("ones", np.ones((128, 128)))):
        at[name] = (x, p.shape[1])
        out.append(p)
        x += p.shape[1]
    return np.concatenate(out, 1).astype(np.float32), at


CONST, CONST_AT = constants()


def metaformer(nc, t, out):
    x_tok = t["x"].rearrange("b s h w -> (b s) h w")
    x_row = t["x"].rearrange("b s h w -> h (b s) w")
    out_row = out.rearrange("b s h w -> h (b s) w")
    ctx = ExitStack()
    with ctx:
        def sb(name, shape, dt=F32):
            return ctx.enter_context(nc.sbuf_tensor(name, shape, dt))

        def sem(name):
            return ctx.enter_context(nc.semaphore(name))

        PS = ctx.enter_context(nc.psum_tensor("PS", [128, 8, 512], F32))
        CST = sb("CST", [128, CONST.shape[1]])

        def const(name):
            a, n = CONST_AT[name]
            return CST[:, a:a + n]

        ident, basis, gram_fn, edge_fn = const("ident"), const("basis"), const("gram"), const("edge")
        row_modes, col_modes, basis17 = const("row_modes"), const("col_modes"), const("basis17")
        fr, block_w, ones = const("fr"), const("block"), const("ones")

        BIG1 = sb("BIG1", [128, PIX])
        BIG2 = sb("BIG2", [128, PIX])
        BIG3 = sb("BIG3", [128, PIX])
        SML = sb("SML", [128, 2624])
        FLAG = sb("FLAG", [1, 1], I32)

        def flat(a):
            n = 1
            for k in a.shape:
                n *= k
            names = "abcde"[:len(a.shape)]
            v = a.rearrange(" ".join(names) + " -> (" + " ".join(names) + ")") if len(names) > 1 else a
            return v.unsqueeze(0)

        x_t = BIG1[:, :].rearrange("t (h w) -> t h w", w=W)
        m1 = BIG1[:, :].rearrange("h (t w) -> h t w", w=W)
        z_s = BIG1[:, :].rearrange("d (q j t) -> d q j t", q=Q, t=NT)
        x_w = BIG2[:, :].rearrange("w (h t) -> w h t", t=NT)
        a0 = BIG2[:, :].rearrange("h (t w) -> h t w", w=W)
        rx = BIG2[:, 0:4096].rearrange("f (j t) -> f j t", t=NT)
        u_re = BIG2[:, 4096:6144].rearrange("m (n t) -> m n t", t=NT)
        u_im = BIG2[:, 6144:8192].rearrange("m (n t) -> m n t", t=NT)
        u_p = BIG2[:, 8192:10240].rearrange("m (n t) -> m n t", t=NT)
        u_q = BIG2[:, 10240:12288].rearrange("m (n t) -> m n t", t=NT)
        scr = BIG2[:, 12288:12800].rearrange("t (n s) -> t n s", s=TB)
        prob = BIG2[:, 12800:13312].rearrange("t (n s) -> t n s", s=TB)
        stmp = BIG2[:, 13312:13824].rearrange("t (n s) -> t n s", s=TB)
        edge_s = BIG2[:, 13824:13954].rearrange("t (f k) -> t f k", k=2)
        edge_p = BIG2[:, 13954:14018]
        edge_t = BIG2[0:64, 14020:14148]
        g_s = BIG2[:, 14148:14276]
        xlow = BIG2[:, 14276:14532].rearrange("t (v w h) -> t v w h", v=2, w=LW)
        xlow_t = BIG2[:, 14532:14788].rearrange("m (v t) -> m v t", v=2)
        cbd = BIG2[:, 14788:14916]
        cf = BIG2[:, 14916:15044]
        k1x = BIG2[:, 15044:15172]
        c32 = BIG2[:, 15172:15204]
        g_c = BIG2[:, 15204:15236]
        sel_x = BIG2[:, 15272:15784].rearrange("t (b p) -> t b p", b=NB)
        sel_w = BIG2[0:NH, 15784:16296].rearrange("n (g p) -> n g p", g=4)
        sq_dump = BIG2[:, 12288:13312]
        smax = BIG2[:, 15236:15252]
        ssum = BIG2[:, 15252:15268]

        row1 = BIG3[0:1, 0:ROW_N]
        row_var = BIG3[:, 2816:2944]
        vr = BIG3[:, 2944:3072]
        p1 = BIG3[:, 0:NF * NT].rearrange("h (f t) -> h f t", t=NT)
        wcp = BIG3[0:NH, 8320:8320 + 1088 + 3 * 288 + 2]
        w_proj = wcp[:, 0:1088].rearrange("n (h w v) -> n h w v", h=MH, v=2)
        w_val = wcp[:, 1088:1376].rearrange("n (h w v) -> n h w v", h=LH, v=2)
        w_key = wcp[:, 1376:1664].rearrange("n (h w v) -> n h w v", h=LH, v=2)
        w_qry = wcp[:, 1664:1952].rearrange("n (h w v) -> n h w v", h=LH, v=2)
        wy = BIG3[0:NH, 10276:11300].rearrange("n (w v h) -> n w v h", v=2, h=MH)
        wtmp = BIG3[0:NH, 11300:11812].rearrange("n (w h) -> n w h", h=MH)
        aqk = BIG3[:, 11812:11876].rearrange("m (k n) -> m k n", n=NH)
        mqk = BIG3[:, 11876:11908].rearrange("m (k n) -> m k n", n=NH)
        wqk = BIG3[:, 11908:11924]
        qk_c = BIG3[0:NH, 7600:8112].rearrange("n (k w h) -> n k w h", k=4, h=LH)
        mqt = BIG3[:, 11940:11956]
        pswv = BIG3[:, 11924:11940]
        PRM = BIG3[:, 12544:12544 + ROW_N]
        gf = BIG3[:, 12416:12544]
        t0 = BIG3[:, 14800:15824]
        prob_t = BIG3[:, 15824:16336].rearrange("p (g t) -> p g t", g=4)
        rep = BIG3[:, 0:8192]
        wr = BIG3[:, 0:4096].rearrange("p (g w v h) -> p g w v h", g=4, v=2, h=MH)
        xrep = BIG3[:, 4096:8192].rearrange("p (b w v h) -> p b w v h", b=4, v=2, h=MH)
        prod = BIG3[:, 8192:12288].rearrange("p (k a w v h) -> p k a w v h", k=2, a=2, v=2, h=MH)
        zt = BIG3[0:64, 0:4096].rearrange("k (t p) -> k t p", p=32)
        ta1 = BIG3[:, 4096:8192].rearrange("k (g n) -> k g n", n=H)
        y_m = BIG3[:, 8192:9216]
        ma = BIG3[:, 9216:10240]
        zw = BIG3[:, 10240:11264]
        ztmp = BIG3[:, 11264:12288]
        stage = BIG3[:, 14800:16336].rearrange("h (k t w) -> h k t w", k=3, w=W)
        p2 = BIG3[:, 0:33 * NT].rearrange("w (f t) -> w f t", t=NT)
        x1m = BIG3[:, 4352:5440].rearrange("t (h v w) -> t h v w", v=2, w=17)
        z2 = BIG3[:, 5440:6528].rearrange("t (h v w) -> t h v w", v=2, w=17)
        z2q = BIG3[:, 0:1024]
        z2g = BIG3[:, 1024:1056]
        z2t = BIG3[:, 6528:7616].rearrange("t (h v w) -> t h v w", v=2, w=17)
        ta2 = BIG3[:, 12288:16384].rearrange("k (g n) -> k g n", n=H)
        st2 = BIG3[:, 10240:10240 + NT * 6].rearrange("h (t k) -> h t k", k=6)
        wx = BIG3[:, :].rearrange("d (t h) -> d t h", h=H)
        y_s = BIG3[:, :].rearrange("d (q j t) -> d q j t", q=Q, t=NT)

        ts = SML[:, 0:1024]
        ln_w = SML[:, 0:1024].rearrange("w (k t h) -> w k t h", k=2, h=H)
        start_a = SML[:, 0:512].rearrange("d (q t) -> d q t", q=Q)
        start_b = SML[:, 512:1024].rearrange("d (q t) -> d q t", q=Q)
        cft = SML[:, 1024:1152]
        acft = SML[:, 1152:1280]
        ln_r = SML[:, 1024:1152]
        ln_b = SML[:, 1152:1280]
        w_t = SML[:, 1280:1408]
        v_t = SML[:, 1408:1536]
        sc = SML[:, 1536:1600]
        kap = SML[:, 1600:1728]
        bet = SML[:, 1728:1856]
        g0 = SML[:, 1856:1984]
        dg = SML[:, 1984:2112]
        z0 = SML[:, 2112:2176]
        z0t = SML[0:64, 2176:2304]
        ln_st = SML[:, 2304:2496].rearrange("p (k v c) -> p k v c", k=2, c=6)
        ln_tmp = SML[:, 2496:2624].rearrange("p (k v) -> p k v", v=16)
        bn_st = SML[:, 1984:2176].rearrange("p (g c) -> p g c", c=6)
        scn = {}

        def s(name):
            if name not in scn:
                scn[name] = len(scn)
                assert len(scn) <= 64
            return sc[:, scn[name]:scn[name] + 1]

        def prm(name):
            a, n = ROW_AT[name]
            return PRM[:, a:a + n]

        def modes(a):
            return a.rearrange("t (w v h) -> t w v h", v=2, h=MH)
        z3_1 = BIG3[:, 4096:5632].rearrange("t (w k h) -> t w k h", k=3, h=MH)
        z3_2 = BIG3[:, 9216:10752].rearrange("t (w k h) -> t w k h", k=3, h=MH)

        sems = {}

        def S(name):
            if name not in sems:
                sems[name] = sem(name)
            return sems[name]

        def bank(k):
            return PS[:, k, :]

        cx_ps = PS[:, 0:2, :].rearrange("t a n -> t (a n)")
        y_ps = PS[:, 2:4, :].rearrange("t a n -> t (a n)")
        modes_ps = PS[:, 4:6, :].rearrange("t a n -> t (a n)")

        P1_N = [min(7, NT - 7 * g) for g in range((NT + 6) // 7)]
        P2_N = [min(15, NT - 15 * g) for g in range((NT + 14) // 15)]
        X1_N = [15, 15, 2]

        def emptied(e, name, n):
            if (n + 1) // 2:
                e.wait_ge(S(name + "_act"), (n + 1) // 2)
            if n // 2:
                e.wait_ge(S(name + "_dve"), n // 2)

        def empty(e, name, n0, n1, move):
            act = e is scalar_engine
            for n in range(n0, n1):
                if (n % 2 == 0) == act:
                    e.wait_ge(S(name + "_filled"), n + 1)
                    move(e, n).then_inc(S(name + ("_act" if act else "_dve")), 1)

        def copy(e, o, i):
            return e.activation(o, i, ACT.Copy) if e is scalar_engine else e.tensor_copy(o, i)

        def move_col(e, n):
            return copy(e, x_w[:, 4 * n:4 * n + 4, :].rearrange("w h t -> w (h t)"), bank(n % 4))

        def move_p1(e, n):
            k = P1_N[n]
            return copy(e, p1[:, :, 7 * n:7 * n + k],
                        PS[:, n % 4, 0:NF * k].rearrange("h (t f) -> h f t", f=NF))

        def move_rx(e, n):
            return copy(e, rx[:, 4 * n:4 * n + 4, :].rearrange("f j t -> f (j t)"), bank(n % 4))

        def move_zt(base):
            return lambda e, n: copy(e, zt[:, :, 4 * n:4 * n + 4],
                                     PS[0:64, base + n % 4, :].rearrange("k (p t) -> k t p", p=4))

        def move_ta(ta, base):
            return lambda e, n: copy(e, ta[:, 4 * n:4 * n + 4, :].rearrange("k g n -> k (g n)"),
                                     bank(base + n % 4))

        def move_p2(e, n):
            k = P2_N[n]
            return copy(e, p2[:, :, 15 * n:15 * n + k],
                        PS[:, 4 + n % 4, 0:33 * k].rearrange("w (t f) -> w f t", f=33))

        def move_lnw(e, n):
            return copy(e, ln_w[:, n % 2, :, :].rearrange("w t h -> w (t h)"), bank(n % 2))

        def recur(e, sweep, starts=None, judge=None):
            sweep(1, 0, STEPS - BURN)
            if starts:
                starts(BURN + 1)
            sweep(BURN + 2, BURN, 0)
            done = BURN + 2 + STEPS
            if judge:
                judge(done)
            e.wait_ge(S("judged"), 1)
            again = e.value_load(FLAG[0:1, 0:1], min_val=0, max_val=1)
            with e.If(again > 0):
                with e.Fori(0, CHUNKS - 1) as i:
                    if starts:
                        starts(i * (STEPS + 1) + done)
                    sweep(i * (STEPS + 1) + (done + 1), i * STEPS + (BURN + STEPS), 0)
                e.wait_ge(S("state"), Q * (done + (STEPS + 1) * (CHUNKS - 1)))
            e.wait_ge(S("state"), Q * done)

        scalar_engine = nc.scalar
        small = ctx.enter_context(nc.allow_non_contiguous_dma("weights' columns"))
        block = ctx.enter_context(nc.Block())

        @block.sync
        def _(sp):
            sp.dma_start(CST[:, :], t["const"]).then_inc(S("const_in"), 16)
            for c in range(XC):
                rows = slice(XR * c, XR * c + XR)
                sp.dma_start(x_t[:, rows, :], x_tok[:, rows, :]).then_inc(S(f"x_in{c}"), 16)
            sp.wait_ge(S("y_filled"), 1)
            for g in range(G4):
                if g >= 3:
                    sp.wait_ge(S("xa"), g - 2)
                sp.dma_start(stage[:, g % 3, :, :],
                             x_row[:, 4 * g:4 * g + 4, :]).then_inc(S(f"stage_in{g % 3}"), 16)
            for g in range(G4):
                sp.wait_ge(S("result"), g + 1)
                sp.dma_start(out_row[:, 4 * g:4 * g + 4, :],
                             a0[:, 4 * g:4 * g + 4, :]).then_inc(S("stored"), 16)
            sp.wait_ge(S("stored"), 16 * G4)

        SMALL_IN = 10

        @block.gpsimd
        def _(pool):
            seq = [0]

            def link(ins):
                seq[0] += 1
                ins.then_inc(S("pool_seq"), 1)
                pool.wait_ge(S("pool_seq"), seq[0])

            pool.wait_ge(S("w_in"), 16 * SMALL_IN)
            wv, ps = wcp[:, 1952:1953], wcp[:, 1953:1954]
            lows = [slice(0, 8), slice(24, 32)]
            for k, (wt, part) in enumerate(((w_qry, 0), (w_qry, 1), (w_key, 0), (w_key, 1))):
                last = pool.tensor_copy(qk_c[:, k, :, :], wt[:, :, 1:9, part].rearrange("n h w -> n w h"))
            last.then_inc(S("qk_c"), 1)
            tmp = wtmp

            def b(part, lo=None, w=MW):
                v = w_proj[:, :, 1:1 + w, part] if lo is None else w_proj[:, lo, 1:1 + w, part]
                return v.rearrange("n h w -> n w h")

            def a(part, k):
                return w_val[:, 8 * k:8 * k + 8, 1:9, part].rearrange("n h w -> n w h")

            for part in range(2):
                link(pool.tensor_scalar(wy[:, :, part, :], b(part), wv, None, ALU.mult))
            for k, lo in enumerate(lows):
                tk = tmp[:, 0:LW, 8 * k:8 * k + 8]
                for part, (p, q, op) in ((0, (0, 0, ALU.add)), (0, (1, 1, ALU.subtract)),
                                      (1, (0, 1, ALU.add)), (1, (1, 0, ALU.add))):
                    o = wy[:, 0:LW, part, lo]
                    link(pool.tensor_tensor(tk, b(p, lo, LW), a(q, k), ALU.mult))
                    link(pool.tensor_tensor(o, o, tk, op))
                for part in range(2):
                    o = wy[:, 0:LW, part, lo]
                    link(pool.tensor_scalar(tk, a(part, k), ps, None, ALU.mult))
                    link(pool.tensor_tensor(o, o, tk, ALU.add))
            pool.wait_ge(S("const_in"), 16)
            pool.wait_ge(S("p1_filled"), len(P1_N))
            for k in range(4):
                pool.tensor_copy(sel_x[:, k, :].rearrange("t (n s) -> t n s", n=HG),
                                 ident[:, TB * k:TB * k + TB].unsqueeze(1).to_broadcast([128, HG, TB]))
                last = pool.tensor_copy(sel_w[:, k, :].rearrange("m (n s) -> m n s", n=HG),
                                        ident[0:NH, HG * k:HG * k + HG].unsqueeze(2).to_broadcast([NH, HG, TB]))
            last.then_inc(S("wy"), 1)

            pool.wait_ge(S("m_low"), 1)
            mb = mqk[:, 1, :].unsqueeze(2).to_broadcast([128, NH, NT])
            xb = [xlow_t[:, k, :].unsqueeze(1).to_broadcast([128, NH, NT]) for k in range(2)]
            pool.tensor_tensor(u_p, mb, xb[1], ALU.mult).then_inc(S("u_prod"), 1)
            pool.tensor_tensor(u_q, mb, xb[0], ALU.mult).then_inc(S("u_prod"), 1)

            for n in range(16):
                hg, bb = n // 4, n % 4
                if n == 0:
                    pool.wait_ge(S("rep"), 16)
                    pool.wait_ge(S("u_prod"), 2)
                    pool.wait_ge(S("cbd"), 1)
                if n >= 2:
                    pool.wait_ge(S("prod_used"), n - 1)
                pool.tensor_tensor(prod[:, n % 2, 1, :, 1, :], xrep[:, bb, :, 0, :], wr[:, hg, :, 1, :],
                                   ALU.mult).then_inc(S("prod_pool"), 1)

            pool.wait_ge(S("kap"), 1)
            for g in range(32):
                pool.wait_ge(S("a0"), g + 1)
                if g == 0:
                    pool.wait_ge(S("mix_filled"), 32)
                w = slice(4 * g, 4 * g + 4)
                pool.tensor_tensor(m1[:, :, w], a0[:, :, w], kap.unsqueeze(2).to_broadcast([128, NT, 4]),
                                   ALU.mult).then_inc(S("ka0"), 1)
            pool.wait_ge(S("ka0"), 32)
            for g in range(G4):
                pool.wait_ge(S(f"stage_in{g % 3}"), 16 * (g // 3 + 1))
                v = a0[:, 4 * g:4 * g + 4, :]
                pool.tensor_tensor(v, v, stage[:, g % 3, :, :], ALU.add).then_inc(S("xa"), 1)

        @block.tensor
        def _(pe):
            def mm(o, l, rhs, start=True, stop=True, **k):
                return pe.matmul(o, l, rhs, start=start, stop=stop, **k)

            def tr(o, i):
                n = i.partition_size() if callable(i.partition_size) else i.partition_size
                return pe.matmul(o, i, ident[0:n, 0:n], is_transpose=True, start=True, stop=True)

            pe.wait_ge(S("const_in"), 16)
            pe.wait_ge(S("row_in"), 16 * len(ROW_AT))
            for k in range(5):
                a, b = 512 * k, min(512 * k + 512, ROW_N)
                mm(PS[:, (4, 5, 6, 7, 0)[k], 0:b - a], ones[0:1, :], row1[:, a:b]).then_inc(S("prm_filled"), 1)
            pe.wait_ge(S("w_in"), 16 * SMALL_IN)
            pe.wait_ge(S("prm"), 5)
            pe.wait_ge(S("qk_c"), 1)
            for k in range(4):
                tr(PS[:, 4, 16 * k:16 * k + 16], qk_c[:, k, :, :])
            tr(PS[:, 5, 0:128], w_t)
            tr(PS[:, 5, 128:256], v_t).then_inc(S("wt_filled"), 1)

            def gram(n):
                emptied(pe, "col", n + 1)
                for h in range(4 * n, 4 * n + 4):
                    last = mm(PS[:, 7, 0:128], x_w[:, h, :], x_w[:, h, :], h == 0, h == H - 1)
                return last

            for c in range(XC):
                pe.wait_ge(S("ln_act"), c + 1)
                pe.wait_ge(S("ln_dve"), c + 1)
                for n in range(4 * c, 4 * c + 4):
                    if n >= 4:
                        emptied(pe, "col", n - 3)
                    for h in range(4 * n, 4 * n + 4):
                        last = tr(PS[:, n % 4, 128 * (h % 4):128 * (h % 4) + 128], x_t[:, h, :])
                    last.then_inc(S("col_filled"), 1)
                    if n >= 2:
                        gram(n - 2)
            gram(30)
            gram(31).then_inc(S("gf_filled"), 1)

            for g, k in enumerate(P1_N):
                if g >= 4:
                    emptied(pe, "p1", g - 3)
                for j in range(k):
                    last = mm(PS[:, g % 4, NF * j:NF * j + NF], x_w[:, :, 7 * g + j], basis)
                last.then_inc(S("p1_filled"), 1)
            emptied(pe, "p1", len(P1_N))
            pe.wait_ge(S("wt"), 1)
            for w in range(1, 17):
                o = PS[:, 4 + (w - 1) // 8, 64 * ((w - 1) % 8):64 * ((w - 1) % 8) + 64]
                mm(o, p1[:, COS[w], :], row_modes[:, 0:64], True, False)
                last = mm(o, p1[:, SIN[w], :], row_modes[:, 64:128], False, True)
            last.then_inc(S("modes_filled"), 1)
            for j in range(8):
                if j >= 4:
                    emptied(pe, "rx", j - 3)
                for half in range(2):
                    o = PS[64 * half:64 * half + 64, j % 4, :]
                    f = 32 * half + 4 * j
                    if f == 0:
                        mm(o[:, 0:256], gram_fn[:, 0:64], p1[:, 0:2, :])
                        last = mm(o[:, 256:512], gram_fn[:, 64:128], p1[:, 2:4, :])
                    else:
                        last = mm(o, gram_fn[:, 64:128], p1[:, f:f + 4, :])
                last.then_inc(S("rx_filled"), 1)
            for f in range(NF):
                last = mm(PS[:, 6, 2 * f:2 * f + 2], p1[:, f, :], edge_fn)
            last.then_inc(S("edge_filled"), 1)
            emptied(pe, "rx", 8)
            pe.wait_ge(S("edge_p"), 1)
            tr(PS[0:64, 6, 256:384], edge_p).then_inc(S("edge_t_filled"), 1)
            pe.wait_ge(S("xlow"), 1)
            tr(PS[:, 4, 0:128], xlow[:, 0, :, :])
            tr(PS[:, 4, 128:256], xlow[:, 1, :, :]).then_inc(S("xlow_filled"), 1)
            pe.wait_ge(S("gf"), 1)
            for j in range(32):
                mm(PS[:, 7, 0:128], rx[:, j, :], rx[:, j, :], j == 0, False)
            pe.wait_ge(S("edge_t"), 1)
            mm(PS[:, 7, 0:128], edge_t, edge_t, False, True).then_inc(S("g_filled"), 1)
            pe.wait_ge(S("wy"), 1)
            for n in range(16):
                if n >= 4:
                    pe.wait_ge(S("rep"), n - 3)
                half = n % 2
                if n < 8:
                    k = n // 2
                    sel = sel_w[:, k, :]
                    rhs = wy[:, 8 * half:8 * half + 8, :, :].rearrange("n w v h -> n (w v h)")
                else:
                    k = n // 2 - 4
                    sel = sel_x[:, k, :]
                    rhs = ts[:, 512 * half:512 * half + 512]
                    if n == 8:
                        pe.wait_ge(S("ts"), 1)
                mm(bank(n % 4), sel, rhs).then_inc(S("rep_filled"), 1)
                if n == 3:
                    pe.wait_ge(S("g_s"), 1)
                    tr(PS[:, 6, 384:512], g_s).then_inc(S("g_t_filled"), 1)
            pe.wait_ge(S("u"), 1)
            for k, u in enumerate((u_re, u_im)):
                for b in range(NB):
                    tb = slice(TB * b, TB * b + TB)
                    last = mm(PS[tb, 5, :], xlow_t[:, k, tb], u[:, :, tb], k == 0, k == 1,
                              skip_group_check=True)
            last.then_inc(S("s_filled"), 1)
            pe.wait_ge(S("prob"), 1)
            for k in range(4):
                last = tr(PS[:, 4, 128 * k:128 * k + 128], prob[:, 4 * k:4 * k + 4, :])
            last.then_inc(S("pt_filled"), 1)
            pe.wait_ge(S("cbd"), 1)
            tr(PS[:, 6, 0:128], cbd).then_inc(S("c_filled"), 1)
            pe.wait_ge(S("cft"), 1)
            tr(PS[:, 6, 128:256], cft)
            mm(PS[:, 6, 256:384], cft, gf).then_inc(S("k1_filled"), 1)
            pe.wait_ge(S("rep"), 16)
            for k in range(2):
                last = mm(bank(k), cft, t0[:, 512 * k:512 * k + 512])
            last.then_inc(S("cx_filled"), 1)
            pe.wait_ge(S("prob_t"), 1)
            for n in range(16):
                hg, b = n // 4, n % 4
                tb = slice(TB * b, TB * b + TB)
                pe.wait_ge(S("prod_dve"), n + 1)
                pe.wait_ge(S("prod_pool"), n + 1)
                for a in range(2):
                    for k in range(2):
                        rhs = prod[:, n % 2, a, 8 * k:8 * k + 8, :, :].rearrange("p w v h -> p (w v h)")
                        last = mm(PS[tb, 2 + k, :], prob_t[:, hg, tb], rhs, hg == 0 and a == 0,
                                  hg == 3 and a == 1, skip_group_check=True)
                last.then_inc(S("prod_used"), 1)
            mm(PS[0:1, 6, 0:1], ones[0:1, 0:1], ones[0:1, 0:1]).then_inc(S("y_filled"), 1)
            pe.wait_ge(S("dg"), 1)
            mm(PS[:, 6, 384:512], ones, dg).then_inc(S("bc_filled"), 1)
            pe.wait_ge(S("acft"), 1)
            for g in range(32):
                if g >= 4:
                    pe.wait_ge(S("a0"), g - 3)
                for w in range(4 * g, 4 * g + 4):
                    last = mm(PS[:, 4 + g % 4, 128 * (w % 4):128 * (w % 4) + 128], x_t[:, :, w], acft)
                last.then_inc(S("mix_filled"), 1)
                if g == 3:
                    pe.wait_ge(S("kap_dg"), 1)
                    mm(PS[:, 3, 0:128], ones, dg).then_inc(S("kap_filled"), 1)

            def inverse(i, z3, ta, zb, tb, b_free, consumed):
                for n in range(8):
                    if n >= 4:
                        emptied(pe, f"zt{i}", n - 3)
                    for p in range(4 * n, 4 * n + 4):
                        part, w = p // 16, p % 16
                        last = tr(PS[0:64, zb + n % 4, 128 * (p % 4):128 * (p % 4) + 128],
                                  z3[:, w, 1 - part:3 - part, :])
                    last.then_inc(S(f"zt{i}_filled"), 1)
                emptied(pe, f"zt{i}", 8)
                for n in range(8):
                    if n >= 4:
                        emptied(pe, f"ta{i}", n - 3)
                    for g in range(4 * n, 4 * n + 4):
                        last = mm(PS[:, tb + n % 4, 128 * (g % 4):128 * (g % 4) + 128],
                                  zt[:, 4 * g:4 * g + 4, :], fr[0:64, :])
                    last.then_inc(S(f"ta{i}_filled"), 1)

            pe.wait_ge(S("z3_1"), 1)
            pe.wait_ge(S("kap"), 1)
            pe.wait_ge(S("a0"), 32)
            inverse(1, z3_1, ta1, 0, 4, None, None)
            emptied(pe, "ta1", 8)
            for g in range(G4):
                if g >= 4:
                    pe.wait_ge(S("u_sum"), g - 3)
                mm(bank(g % 4), ta1[:, g, :], block_w).then_inc(S("b1_filled"), 1)
            for g, k in enumerate(P2_N):
                if g >= 4:
                    emptied(pe, "p2", g - 3)
                pe.wait_ge(S("m1"), min(G4, (15 * g + k + 3) // 4))
                for j in range(k):
                    last = mm(PS[:, 4 + g % 4, 33 * j:33 * j + 33], m1[:, 15 * g + j, :], basis17)
                last.then_inc(S("p2_filled"), 1)
            emptied(pe, "p2", len(P2_N))
            pe.wait_ge(S("u_sum"), G4)
            for i in range(MH):
                h = i if i < 16 else i - 32
                o = PS[:, i // 15, 34 * (i % 15):34 * (i % 15) + 34]
                last = mm(o, p2[:, abs(h), :], col_modes[:, 0:34], True, h == 0)
                if h:
                    a = 34 if h > 0 else 68
                    last = mm(o, p2[:, 16 + abs(h), :], col_modes[:, a:a + 34], False, True)
            last.then_inc(S("x1_filled"), 1)
            pe.wait_ge(S("rowsq"), 1)
            mm(PS[:, 3, 0:1], dg, ones[:, 0:1]).then_inc(S("sq_filled"), 1)
            pe.wait_ge(S("dg2"), 1)
            mm(PS[:, 3, 128:256], ones, dg)
            pe.wait_ge(S("z0"), 1)
            tr(PS[0:64, 3, 256:384], z0).then_inc(S("z0t_filled"), 1)
            pe.wait_ge(S("z0t"), 1)
            mm(PS[:, 3, 384:512], fr[0:64, :], z0t).then_inc(S("g0_filled"), 1)
            pe.wait_ge(S("z3_2"), 1)
            pe.wait_ge(S("g0"), 1)
            inverse(2, z3_2, ta2, 4, 0, None, None)
            emptied(pe, "ta2", 8)

            def hidden(k):
                pe.wait_ge(S("ln2_act"), k + 1)
                pe.wait_ge(S("ln2_dve"), k + 1)
                for n in range(4 * k, 4 * k + 5):
                    if n < 4 * k + 4:
                        if n >= 2:
                            emptied(pe, "lnw", n - 1)
                        for j in range(4):
                            last = tr(PS[:, n % 2, 128 * j:128 * j + 128], m1[:, 4 * n + j, :])
                        last.then_inc(S("lnw_filled"), 1)
                    if n > 4 * k:
                        emptied(pe, "lnw", n)
                        if n >= 3:
                            pe.wait_ge(S("wx"), n - 2)
                        mm(bank(2 + (n - 1) % 2), w_t, ln_w[:, (n - 1) % 2, :, :].rearrange("w t h -> w (t h)")
                           ).then_inc(S("wx_filled"), 1)

            for g in range(G4):
                if g >= 4:
                    pe.wait_ge(S("x1"), g - 3)
                mm(bank(4 + g % 4), ta2[:, g, :], block_w).then_inc(S("b2_filled"), 1)
                if g >= 8 and g % 4 == 3:
                    hidden(g // 4 - 2)
            hidden(6)
            hidden(7)

            def sweep(p0, k0, j0):
                for dj in range(2):
                    j = j0 + dj
                    for q in range(Q):
                        pe.wait_ge(S("state"), 4 * (p0 + dj) + q - 3)
                        mm(PS[:, q + 4 * dj, 0:128], v_t, y_s[:, q, (j - 1) % STEPS, :]).then_inc(S("vy"), 1)
                with pe.Fori(1, (STEPS - j0) // 2) as i:
                    for dj in range(2):
                        for q in range(Q):
                            pe.wait_ge(S("state"), i * (2 * Q) + (4 * (p0 + dj) + q - 3))
                            mm(PS[:, q + 4 * dj, 0:128], v_t,
                               BIG3[:, bass.ds(i * (2 * NT) + NT * (j0 + dj - 1 + STEPS * q), NT)]).then_inc(S("vy"), 1)

            def judge(p):
                pe.wait_ge(S("gap"), 1)
                tr(PS[0:1, 0, 0:128], s("gap")).then_inc(S("gap_filled"), 1)

            recur(pe, sweep, None, judge)
            for g in range(G4):
                if g >= 8:
                    pe.wait_ge(S("result"), g - 7)
                for j in range(4):
                    last = tr(PS[:, g % 8, 128 * j:128 * j + 128],
                              y_s[:, :, :, 4 * g + j].rearrange("d q j -> d (q j)"))
                last.then_inc(S("yt_filled"), 1)

        @block.scalar
        def _(act):
            for name, (a, n) in ROW_AT.items():
                act.dma_start(row1[:, a:a + n], flat(t[name])).then_inc(S("row_in"), 16)
            act.dma_start(wcp[:, 0:1088], t["proj_w"].rearrange("n o h w v -> n (o h w v)")).then_inc(S("w_in"), 16)
            for name, a in (("value_w", 1088), ("key_w", 1376), ("query_w", 1664)):
                act.dma_start(wcp[:, a:a + 288], t[name].rearrange("o n h w v -> n (o h w v)")).then_inc(S("w_in"), 16)
            act.dma_start(wcp[:, 1952:1953], t["value_skip_w"].rearrange("o n -> n o")).then_inc(S("w_in"), 16)
            act.dma_start(wcp[:, 1953:1954], t["proj_skip_w"]).then_inc(S("w_in"), 16)
            act.dma_start(w_t, t["W"]).then_inc(S("w_in"), 16)
            act.dma_start(v_t, t["V"]).then_inc(S("w_in"), 16)
            act.dma_start(s("gamma"), t["gamma"].unsqueeze(1)).then_inc(S("w_in"), 16)
            act.dma_start(s("beta"), t["beta"].unsqueeze(1)).then_inc(S("w_in"), 16)

            roots = [0]

            def root(o, i):
                roots[0] += 1
                act.wait_ge(S("root_of"), roots[0])
                act.activation(o, i, ACT.Sqrt).then_inc(S("root"), 1)

            for k in range(5):
                a, b = 512 * k, min(512 * k + 512, ROW_N)
                act.wait_ge(S("prm_filled"), k + 1)
                act.activation(PRM[:, a:b], PS[:, (4, 5, 6, 7, 0)[k], 0:b - a], ACT.Copy).then_inc(S("prm"), 1)
            act.wait_ge(S("wt_filled"), 1)
            act.activation(aqk.rearrange("m k n -> m (k n)"), PS[:, 4, 0:64], ACT.Copy)
            act.activation(w_t, PS[:, 5, 0:128], ACT.Copy)
            act.activation(v_t, PS[:, 5, 128:256], ACT.Copy).then_inc(S("wt"), 1)

            for c in range(XC):
                root(ln_r[:, XR * c:XR * c + XR], ln_tmp[:, c % 2, :])
                if c:
                    empty(act, "col", 4 * c - 4, 4 * c, move_col)
                act.wait_ge(S("ln_coef"), c + 1)
                for row in range(XR * c + LN_DVE, XR * c + XR):
                    last = act.activation(x_t[:, row, :], x_t[:, row, :], ACT.Identity,
                                          scale=ln_r[:, row:row + 1], bias=ln_b[:, row:row + 1])
                last.then_inc(S("ln_act"), 1)
            empty(act, "col", 4 * XC - 4, 4 * XC, move_col)
            root(s("s1"), s("rt"))
            act.wait_ge(S("s1"), 1)
            empty(act, "p1", 0, len(P1_N), move_p1)
            act.wait_ge(S("t0"), 1)
            act.activation(ts, modes_ps, ACT.Copy, scale=s("s1")).then_inc(S("ts"), 1)
            empty(act, "rx", 0, 8, move_rx)
            for n in range(16):
                act.wait_ge(S("rep_filled"), n + 1)
                act.activation(rep[:, 512 * n:512 * n + 512], bank(n % 4), ACT.Copy).then_inc(S("rep"), 1)
            act.wait_ge(S("s_shift"), 1)
            act.activation(prob, scr, ACT.Exp).then_inc(S("s_exp"), 1)
            act.wait_ge(S("pt_filled"), 1)
            act.activation(prob_t.rearrange("p g t -> p (g t)"), bank(4), ACT.Copy).then_inc(S("prob_t"), 1)
            act.wait_ge(S("cx_filled"), 1)
            act.activation(sq_dump, cx_ps, ACT.Square, accum_out=s("p_cx")).then_inc(S("p_cx"), 1)
            act.wait_ge(S("ma"), 1)
            act.activation(ztmp, ma, ACT.Square, accum_out=s("p_ma")).then_inc(S("p_ma"), 1)
            root(s("al"), s("rt"))
            root(s("rm"), s("rt"))
            for g in range(32):
                if g == 6:
                    act.wait_ge(S("zw"), 1)
                    act.activation(ztmp, zw, ACT.Square, accum_out=s("p_z1")).then_inc(S("p_z1"), 1)
                if g == 14:
                    root(s("r1"), s("rt"))
                act.wait_ge(S("mix_filled"), g + 1)
                act.activation(a0[:, :, 4 * g:4 * g + 4],
                               PS[:, 4 + g % 4, :].rearrange("h (w t) -> h t w", w=4), ACT.Copy).then_inc(S("a0"), 1)
            empty(act, "zt1", 0, 8, move_zt(0))
            empty(act, "ta1", 0, 8, move_ta(ta1, 4))
            for g in range(G4):
                act.wait_ge(S("u_sum"), g + 1)
                v = m1[:, 4 * g:4 * g + 4, :]
                act.activation(v, v, ACT.Gelu, bias=s("cu")).then_inc(S("m1"), 1)
            empty(act, "p2", 0, len(P2_N), move_p2)
            act.wait_ge(S("z2"), 1)
            act.activation(z2q.rearrange("t (k w) -> t k w", w=MW),
                           z2.rearrange("t h v w -> t (h v) w")[:, :, 1:17], ACT.Square,
                           accum_out=s("p_z2")).then_inc(S("p_z2"), 1)
            root(s("r2"), s("rt"))
            root(s("ro"), s("rt"))
            empty(act, "zt2", 0, 8, move_zt(4))
            act.wait_ge(S("xa"), G4)
            empty(act, "ta2", 0, 8, move_ta(ta2, 0))

            for k in range(XC + 2):
                if k < XC:
                    for g in range(4 * k, 4 * k + 4):
                        act.wait_ge(S("g0"), 1)
                        for i in range(4 * g, 4 * g + 4):
                            last = act.activation(m1[:, i, :], m1[:, i, :], ACT.Identity,
                                                  scale=bet[:, i:i + 1], bias=g0[:, i:i + 1])
                        last.then_inc(S("bm1"), 1)
                if 0 <= k - 1 < XC:
                    c = k - 1
                    root(ln_r[:, XR * c:XR * c + XR], ln_tmp[:, c % 2, :])
                    act.wait_ge(S("ln2_coef"), c + 1)
                    for row in range(XR * c + LN_DVE, XR * c + XR):
                        last = act.activation(m1[:, row, :], a0[:, row, :], ACT.Identity,
                                              scale=ln_r[:, row:row + 1], bias=ln_b[:, row:row + 1])
                    last.then_inc(S("ln2_act"), 1)
                if k >= 2:
                    c = k - 2
                    for n in range(4 * c, 4 * c + 5):
                        if n < 4 * c + 4:
                            if n >= 2 and n % 2 == 0:
                                act.wait_ge(S("wx_filled"), n - 1)
                            empty(act, "lnw", n, n + 1, move_lnw)
                        if n > 4 * c:
                            act.wait_ge(S("wx_filled"), n)
                            act.activation(wx[:, 4 * n - 4:4 * n, :].rearrange("d t h -> d (t h)"),
                                           bank(2 + (n - 1) % 2), ACT.Copy).then_inc(S("wx"), 1)
            root(s("bs"), s("rt"))
            act.wait_ge(S("bn_ab"), 1)
            act.wait_ge(S("bn"), G4)
            for q in range(2):
                act.activation(z_s[:, q, :, :], wx[:, :, STEPS * q:STEPS * q + STEPS].rearrange("d t j -> d j t"),
                               ACT.Identity, scale=s("bs"), bias=s("bb")).then_inc(S("z_act"), 1)

            def sweep(p0, k0, j0):
                if j0:
                    act.wait_ge(S("z_act"), 2)
                    act.wait_ge(S("z_dve"), 2)
                for dj in range(2):
                    for q in range(Q):
                        act.wait_ge(S("z_sum"), 4 * (k0 + dj) + (q + 1))
                        act.activation(y_s[:, q, j0 + dj, :], PS[:, q + 4 * dj, 0:NT], ACT.Sigmoid).then_inc(S("state"), 1)
                with act.Fori(1, (STEPS - j0) // 2) as i:
                    for dj in range(2):
                        for q in range(Q):
                            act.wait_ge(S("z_sum"), i * (2 * Q) + (4 * (k0 + dj) + (q + 1)))
                            act.activation(BIG3[:, bass.ds(i * (2 * NT) + NT * (j0 + dj + STEPS * q), NT)],
                                           PS[:, q + 4 * dj, 0:NT], ACT.Sigmoid).then_inc(S("state"), 1)

            recur(act, sweep)

        @block.vector
        def _(dve):
            seq = [0]

            def link(ins):
                seq[0] += 1
                ins.then_inc(S("dve_seq"), 1)
                dve.wait_ge(S("dve_seq"), seq[0])

            TT, TS, STT = dve.tensor_tensor, dve.tensor_scalar, dve.scalar_tensor_tensor
            roots = [0]

            def inv_root(o, i, eps, times=None):
                roots[0] += 1
                TS(s("rt"), i, eps, None, ALU.add).then_inc(S("root_of"), 1)
                dve.wait_ge(S("root"), roots[0])
                link(dve.reciprocal(o, o))
                if times is not None:
                    link(TT(o, o, times, ALU.mult))

            def ln_stats(c, src, eps, keep):
                st = ln_st[:, c % 2]
                for row in range(XR):
                    last = dve.bn_stats(st[:, row, :], src[:, XR * c + row, :])
                link(last)
                d, m, dd, v = ln_tmp[:, 4, :], ln_tmp[:, 2 + c % 2, :], ln_tmp[:, 5, :], ln_tmp[:, 6, :]
                TT(m, st[:, :, 1], st[:, :, 4], ALU.add)
                TT(v, st[:, :, 2], st[:, :, 5], ALU.add)
                link(TT(d, st[:, :, 1], st[:, :, 4], ALU.subtract))
                TS(v, v, 1.0 / W, None, ALU.mult)
                link(STT(dd, d, 0.25, d, ALU.mult, ALU.mult))
                keep = keep[:, XR * c:XR * c + XR] if keep is not None else d
                link(TT(keep, dd, v, ALU.add))
                TS(ln_tmp[:, c % 2, :], keep, eps, None, ALU.add).then_inc(S("root_of"), 1)

            def ln_coefs(c, done):
                roots[0] += 1
                dve.wait_ge(S("root"), roots[0])
                rs, b = ln_r[:, XR * c:XR * c + XR], ln_b[:, XR * c:XR * c + XR]
                link(dve.reciprocal(rs, rs))
                STT(b, ln_tmp[:, 2 + c % 2, :], -0.5, rs, ALU.mult, ALU.mult).then_inc(S(done), 1)
                dve.wait_ge(S(done), c + 1)

            dve.wait_ge(S("x_in0"), 16)
            ln_stats(0, x_t, LN_C_EPS, row_var)
            for c in range(XC):
                if c + 1 < XC:
                    dve.wait_ge(S(f"x_in{c + 1}"), 16)
                    ln_stats(c + 1, x_t, LN_C_EPS, row_var)
                ln_coefs(c, "ln_coef")
                for row in range(XR * c, XR * c + LN_DVE):
                    last = TS(x_t[:, row, :], x_t[:, row, :], ln_r[:, row:row + 1], ln_b[:, row:row + 1], ALU.mult, ALU.add)
                last.then_inc(S("ln_dve"), 1)
                if c:
                    empty(dve, "col", 4 * c - 4, 4 * c, move_col)
            empty(dve, "col", 4 * XC - 4, 4 * XC, move_col)
            link(TT(vr, row_var, ln_r, ALU.mult))
            link(TT(vr, vr, ln_r, ALU.mult))
            link(dve.tensor_reduce(s("v0"), vr, AX.X, ALU.add))
            link(TS(s("v0"), s("v0"), 1.0 / H, None, ALU.mult))
            dve.wait_ge(S("prm"), 5)
            inv_root(s("s1"), s("v0"), EPS, prm("norm1_g"))
            dve.tensor_copy(s("x0"), s("s1")).then_inc(S("s1"), 1)
            dve.wait_ge(S("gf_filled"), 1)
            dve.tensor_copy(gf, PS[:, 7, 0:NT]).then_inc(S("gf"), 1)
            dve.wait_ge(S("wt"), 1)
            wq, wk = prm("query_skip_w"), prm("key_skip_w")
            TT(wqk, wq, wk, ALU.mult)
            TT(aqk[:, 0, :], aqk[:, 0, :], wq, ALU.add)
            TT(pswv, prm("proj_skip_w"), prm("value_skip_w"), ALU.mult)
            link(TT(aqk[:, 2, :], aqk[:, 2, :], wk, ALU.add))
            for part, (p, q, op) in enumerate((((0, 2), (1, 3), ALU.add), ((0, 3), (1, 2), ALU.subtract))):
                link(TT(mqk[:, part, :], aqk[:, p[0], :], aqk[:, p[1], :], ALU.mult))
                link(TT(mqt, aqk[:, q[0], :], aqk[:, q[1], :], ALU.mult))
                link(TT(mqk[:, part, :], mqk[:, part, :], mqt, op))
            link(TT(mqk[:, 0, :], mqk[:, 0, :], wqk, ALU.subtract))
            link(TS(mqk[:, :, :], mqk[:, :, :], 128.0, None, ALU.mult))
            empty(dve, "p1", 0, len(P1_N), move_p1)
            dve.wait_ge(S("modes_filled"), 1)
            dve.tensor_copy(t0, modes_ps).then_inc(S("t0"), 1)
            dve.wait_ge(S("ts"), 1)
            tsm = modes(ts)
            for k, lo in enumerate((slice(0, 8), slice(24, 32))):
                last = dve.tensor_copy(xlow[:, :, :, 8 * k:8 * k + 8],
                                       tsm[:, 0:LW, :, lo].rearrange("t w v h -> t v w h"))
            last.then_inc(S("xlow"), 1)
            empty(dve, "rx", 0, 8, move_rx)
            dve.wait_ge(S("edge_filled"), 1)
            link(dve.tensor_copy(edge_s.rearrange("t f k -> t (f k)"), PS[:, 6, 0:2 * NF]))
            e, half = edge_s, 2 ** -0.5
            TS(edge_p[:, 0:1], e[:, 0, 0:1], half, None, ALU.mult)
            TT(edge_p[:, 1:2], e[:, 1, 0:1], e[:, 64, 1:2], ALU.add)
            TT(edge_p[:, 2:33], e[:, 2:33, 0], e[:, 33:64, 1], ALU.add)
            link(TT(edge_p[:, 33:64], e[:, 33:64, 0], e[:, 2:33, 1], ALU.subtract))
            TS(edge_p[:, 1:2], edge_p[:, 1:2], half, None, ALU.mult).then_inc(S("edge_p"), 1)
            dve.wait_ge(S("edge_t_filled"), 1)
            dve.tensor_copy(edge_t, PS[0:64, 6, 256:384]).then_inc(S("edge_t"), 1)
            dve.wait_ge(S("xlow_filled"), 1)
            dve.tensor_copy(xlow_t.rearrange("m v t -> m (v t)"), PS[:, 4, 0:256]).then_inc(S("m_low"), 1)
            dve.wait_ge(S("m_low"), 1)
            mb = mqk[:, 0, :].unsqueeze(2).to_broadcast([128, NH, NT])
            xb = [xlow_t[:, k, :].unsqueeze(1).to_broadcast([128, NH, NT]) for k in range(2)]
            TT(u_re, mb, xb[0], ALU.mult)
            link(TT(u_im, mb, xb[1], ALU.mult))
            dve.wait_ge(S("g_filled"), 1)
            TS(g_s, PS[:, 7, 0:NT], s("s1"), None, ALU.mult).then_inc(S("g_s"), 1)
            dve.wait_ge(S("u_prod"), 1)
            TT(u_re, u_re, u_p, ALU.subtract)
            dve.wait_ge(S("u_prod"), 2)
            TT(u_im, u_im, u_q, ALU.add).then_inc(S("u"), 1)
            dve.wait_ge(S("g_t_filled"), 1)
            dve.memset(cbd, 0.0)
            for b in range(NB):
                tb = slice(TB * b, TB * b + TB)
                last = TS(g_c[tb, :], PS[tb, 6, 384 + TB * b:384 + TB * b + TB], sc[tb, scn["s1"]:scn["s1"] + 1],
                          None, ALU.mult)
            link(last)
            link(TT(stmp, wqk.unsqueeze(2).to_broadcast([128, NH, TB]),
                    g_c.unsqueeze(1).to_broadcast([128, NH, TB]), ALU.mult))
            dve.wait_ge(S("s_filled"), 1)
            link(TT(scr, stmp, PS[:, 5, :].rearrange("t (n s) -> t n s", s=TB), ALU.add))
            link(dve.tensor_reduce(smax, scr, AX.X, ALU.max))
            TT(scr, scr, smax.unsqueeze(2).to_broadcast([128, NH, TB]), ALU.subtract).then_inc(S("s_shift"), 1)
            dve.wait_ge(S("s_exp"), 1)
            link(dve.tensor_reduce(ssum, prob, AX.X, ALU.add))
            link(dve.reciprocal(ssum, ssum))
            TT(prob, prob, ssum.unsqueeze(2).to_broadcast([128, NH, TB]), ALU.mult).then_inc(S("prob"), 1)
            dve.wait_ge(S("prob"), 1)
            link(TT(stmp, prob, pswv.unsqueeze(2).to_broadcast([128, NH, TB]), ALU.mult))
            link(dve.tensor_reduce(c32, stmp.rearrange("t n s -> t s n"), AX.X, ALU.add))
            for b in range(NB):
                tb = slice(TB * b, TB * b + TB)
                last = dve.tensor_copy(cbd[tb, tb], c32[tb, :])
            last.then_inc(S("cbd"), 1)
            dve.wait_ge(S("c_filled"), 1)
            STT(cft, PS[:, 6, 0:NT], s("s1"), ident, ALU.mult, ALU.add).then_inc(S("cft"), 1)
            dve.wait_ge(S("k1_filled"), 1)
            link(dve.tensor_copy(cf, PS[:, 6, 128:256]))
            link(TT(k1x, PS[:, 6, 256:384], cf, ALU.mult))
            link(dve.tensor_reduce(s("q"), k1x, AX.X, ALU.add))
            dve.wait_ge(S("rep"), 16)
            for n in range(16):
                hg, b = n // 4, n % 4
                if n >= 2:
                    dve.wait_ge(S("prod_used"), n - 1)
                TT(prod[:, n % 2, 0], xrep[:, b], wr[:, hg, :, 0:1, :].to_broadcast([128, MW, 2, MH]), ALU.mult)
                STT(prod[:, n % 2, 1, :, 0, :], xrep[:, b, :, 1, :], -1.0, wr[:, hg, :, 1, :],
                    ALU.mult, ALU.mult).then_inc(S("prod_dve"), 1)
            dve.wait_ge(S("y_filled"), 1)
            link(dve.tensor_copy(y_m, y_ps))
            dve.wait_ge(S("p_cx"), 1)
            TT(ma, cx_ps, y_m, ALU.add).then_inc(S("ma"), 1)
            dve.wait_ge(S("ma"), 1)
            dve.wait_ge(S("p_ma"), 1)
            TS(s("q"), s("q"), 1.0 / PIX, None, ALU.mult)
            link(TT(s("x0"), s("p_ma"), s("p_cx"), ALU.subtract))
            link(STT(s("va"), s("x0"), 2.0, s("q"), ALU.mult, ALU.add))
            inv_root(s("al"), s("va"), EPS, prm("attn_norm_g"))
            TS(dg, ident, s("al"), None, ALU.mult).then_inc(S("dg"), 1)
            link(TT(s("x0"), s("al"), s("al"), ALU.mult))
            link(TT(s("x0"), s("x0"), s("va"), ALU.mult))
            dve.wait_ge(S("bc_filled"), 1)
            TT(acft, cft, PS[:, 6, 384:512], ALU.mult).then_inc(S("acft"), 1)
            inv_root(s("rm"), s("x0"), EPS, prm("norm2_g"))
            link(TT(s("kappa"), s("rm"), prm("mixer_skip_w1"), ALU.mult))
            TS(dg, ident, s("kappa"), None, ALU.mult).then_inc(S("kap_dg"), 1)
            TT(s("sm"), s("rm"), s("al"), ALU.mult)
            w1 = prm("mixer_w1").rearrange("t (h w v) -> t v w h", v=2, w=17)[:, :, 1:17, :]
            mam, zwm, ztm, ym = modes(ma), modes(zw), modes(ztmp), modes(y_m)
            TT(zwm[:, :, 0, :], mam[:, :, 0, :], w1[:, 0], ALU.mult)
            TT(zwm[:, :, 1, :], mam[:, :, 0, :], w1[:, 1], ALU.mult)
            TT(ztm[:, :, 0, :], mam[:, :, 1, :], w1[:, 1], ALU.mult)
            link(TT(ztm[:, :, 1, :], mam[:, :, 1, :], w1[:, 0], ALU.mult))
            TT(zwm[:, :, 0, :], zwm[:, :, 0, :], ztm[:, :, 0, :], ALU.subtract)
            TT(zwm[:, :, 1, :], zwm[:, :, 1, :], ztm[:, :, 1, :], ALU.add).then_inc(S("zw"), 1)
            dve.wait_ge(S("zw"), 1)
            link(TS(y_m, y_m, s("al"), None, ALU.mult))
            dve.wait_ge(S("kap_filled"), 1)
            dve.tensor_copy(kap, PS[:, 3, 0:NT]).then_inc(S("kap"), 1)
            link(TT(s("x0"), s("sm"), s("sm"), ALU.mult))
            dve.wait_ge(S("p_z1"), 1)
            link(STT(s("x0"), s("p_z1"), 2.0, s("x0"), ALU.mult, ALU.mult))
            inv_root(s("r1"), s("x0"), EPS, prm("mixer_norm_g1"))
            link(TT(s("f1"), s("r1"), s("sm"), ALU.mult))
            link(TS(ztmp, y_m, s("kappa"), None, ALU.mult))
            o = z3_1.rearrange("t w k h -> t w (k h)")[:, :, MH:3 * MH]
            link(STT(o, zw.rearrange("t (w k) -> t w k", w=MW), s("f1"),
                     ztmp.rearrange("t (w k) -> t w k", w=MW), ALU.mult, ALU.add))
            TS(z3_1[:, :, 0, :], z3_1[:, :, 2, :], -1.0, None, ALU.mult).then_inc(S("z3_1"), 1)
            link(TT(s("cu"), prm("mixer_skip_w1"), prm("norm2_b"), ALU.mult))
            link(TT(s("cu"), s("cu"), prm("mixer_norm_b1"), ALU.add))
            link(TT(s("cu"), s("cu"), prm("mixer_skip_b1"), ALU.add))
            empty(dve, "zt1", 0, 8, move_zt(0))
            empty(dve, "ta1", 0, 8, move_ta(ta1, 4))
            dve.wait_ge(S("ka0"), 32)
            for g in range(G4 + 3):
                if g < G4:
                    dve.wait_ge(S("b1_filled"), g + 1)
                    v = m1[:, 4 * g:4 * g + 4, :].rearrange("h t w -> h (t w)")
                    TT(v, bank(g % 4), v, ALU.add).then_inc(S("u_sum"), 1)
                if g >= 3:
                    dve.wait_ge(S("m1"), g - 2)
                    for i in range(4 * (g - 3), 4 * (g - 3) + 4):
                        last = dve.bn_stats(st2[:, i, :], m1[:, i, :])
            link(last)
            TT(kap, st2[:, :, 1], st2[:, :, 1], ALU.mult)
            TT(bet, st2[:, :, 4], st2[:, :, 4], ALU.mult)
            link(TT(dg, st2[:, :, 2], st2[:, :, 5], ALU.add))
            link(TT(kap, kap, bet, ALU.add))
            STT(dg, kap, float(W // 2), dg, ALU.mult, ALU.add).then_inc(S("rowsq"), 1)
            empty(dve, "p2", 0, len(P2_N), move_p2)
            dve.wait_ge(S("x1_filled"), 1)
            for k, n in enumerate(X1_N):
                last = dve.tensor_copy(x1m[:, 15 * k:15 * k + n].rearrange("t h v w -> t (h v w)"), PS[:, k, 0:34 * n])
            link(last)
            w2 = prm("mixer_w2").rearrange("t (h w v) -> t v h w", v=2, w=17)
            TT(z2[:, :, 0, :], x1m[:, :, 0, :], w2[:, 0], ALU.mult)
            TT(z2[:, :, 1, :], x1m[:, :, 0, :], w2[:, 1], ALU.mult)
            TT(z2t[:, :, 0, :], x1m[:, :, 1, :], w2[:, 1], ALU.mult)
            link(TT(z2t[:, :, 1, :], x1m[:, :, 1, :], w2[:, 0], ALU.mult))
            TT(z2[:, :, 0, :], z2[:, :, 0, :], z2t[:, :, 0, :], ALU.subtract)
            TT(z2[:, :, 1, :], z2[:, :, 1, :], z2t[:, :, 1, :], ALU.add).then_inc(S("z2"), 1)
            dve.wait_ge(S("z2"), 1)
            gg = z2g
            TT(gg[:, 0:15], z2[:, 1:16, 0, 0], z2[:, 31:16:-1, 0, 0], ALU.add)
            TT(gg[:, 15:30], z2[:, 1:16, 1, 0], z2[:, 31:16:-1, 1, 0], ALU.subtract)
            link(dve.tensor_copy(gg[:, 30:32], z2[:, 16, :, 0]))
            link(TT(gg, gg, gg, ALU.mult))
            link(dve.tensor_reduce(s("g2"), gg, AX.X, ALU.add))
            link(TT(z2t.rearrange("t h v w -> t (h v w)"), z2.rearrange("t h v w -> t (h v w)"),
                    x1m.rearrange("t h v w -> t (h v w)"), ALU.mult))
            link(dve.tensor_reduce(s("cov"), z2t.rearrange("t h v w -> t (h v) w")[:, :, 1:17], AX.XY, ALU.add))
            link(dve.tensor_reduce(s("cov0"), z2t[:, 1:32, :, 0], AX.XY, ALU.add))
            link(STT(s("cov"), s("cov"), 2.0, s("cov0"), ALU.mult, ALU.add))
            link(TS(s("g2"), s("g2"), 0.5, None, ALU.mult))
            dve.wait_ge(S("p_z2"), 1)
            link(STT(s("v2"), s("p_z2"), 2.0, s("g2"), ALU.mult, ALU.add))
            inv_root(s("r2"), s("v2"), EPS, prm("mixer_norm_g2"))
            mean1 = s("mean1")
            link(dve.tensor_copy(mean1, x1m[:, 0, 0, 0:1]))
            link(TT(s("m1sq"), mean1, mean1, ALU.mult))
            dve.wait_ge(S("sq_filled"), 1)
            link(STT(s("vm1"), PS[:, 3, 0:1], 1.0 / PIX, s("m1sq"), ALU.mult, ALU.subtract))
            k2 = prm("mixer_skip_w2")
            link(TT(s("x0"), s("r2"), s("v2"), ALU.mult))
            link(TT(s("x1"), k2, s("cov"), ALU.mult))
            link(STT(s("x0"), s("x1"), 2.0, s("x0"), ALU.mult, ALU.add))
            link(TT(s("x0"), s("x0"), s("r2"), ALU.mult))
            link(TT(s("x1"), k2, s("vm1"), ALU.mult))
            link(TT(s("x1"), k2, s("x1"), ALU.mult))
            link(TT(s("x0"), s("x0"), s("x1"), ALU.add))
            inv_root(s("ro"), s("x0"), EPS, prm("mixer_out_g"))
            TT(s("alpha"), s("ro"), s("r2"), ALU.mult)
            link(TT(s("bt"), s("ro"), k2, ALU.mult))
            TS(dg, ident, s("bt"), None, ALU.mult).then_inc(S("dg2"), 1)
            link(TT(s("x1"), s("bt"), mean1, ALU.mult))
            link(TT(s("cb"), prm("mixer_out_b"), prm("attn_norm_b"), ALU.add))
            TS(z0.rearrange("t (v h) -> t v h", v=2)[:, 0, :], z2[:, :, 0, 0], s("alpha"), None, ALU.mult)
            link(TS(z0.rearrange("t (v h) -> t v h", v=2)[:, 1, :], z2[:, :, 1, 0], s("alpha"), None, ALU.mult))
            TT(z0[:, 0:1], s("cb"), s("x1"), ALU.subtract).then_inc(S("z0"), 1)
            for part in range(2):
                last = STT(z3_2[:, :, 1 + part, :], z2[:, :, part, 1:17].rearrange("t h w -> t w h"), s("alpha"),
                           ym[:, :, part, :], ALU.mult, ALU.add)
            link(last)
            TS(z3_2[:, :, 0, :], z3_2[:, :, 2, :], -1.0, None, ALU.mult).then_inc(S("z3_2"), 1)
            dve.wait_ge(S("z0t_filled"), 1)
            dve.tensor_copy(bet, PS[:, 3, 128:256])
            dve.tensor_copy(z0t, PS[0:64, 3, 256:384]).then_inc(S("z0t"), 1)
            dve.wait_ge(S("g0_filled"), 1)
            dve.tensor_copy(g0, PS[:, 3, 384:512]).then_inc(S("g0"), 1)
            empty(dve, "zt2", 0, 8, move_zt(4))
            dve.wait_ge(S("xa"), G4)
            empty(dve, "ta2", 0, 8, move_ta(ta2, 0))

            for k in range(XC + 2):
                if k < XC:
                    for g in range(4 * k, 4 * k + 4):
                        v = a0[:, 4 * g:4 * g + 4, :].rearrange("h t w -> h (t w)")
                        dve.wait_ge(S("bm1"), g + 1)
                        link(TT(v, v, m1[:, 4 * g:4 * g + 4, :].rearrange("h t w -> h (t w)"), ALU.add))
                        dve.wait_ge(S("b2_filled"), g + 1)
                        TT(v, v, bank(4 + g % 4), ALU.add).then_inc(S("x1"), 1)
                    dve.wait_ge(S("x1"), 4 * k + 4)
                    ln_stats(k, a0, EPS, None)
                if 0 <= k - 1 < XC:
                    c = k - 1
                    ln_coefs(c, "ln2_coef")
                    for row in range(XR * c, XR * c + LN_DVE):
                        last = TS(m1[:, row, :], a0[:, row, :], ln_r[:, row:row + 1], ln_b[:, row:row + 1], ALU.mult, ALU.add)
                    last.then_inc(S("ln2_dve"), 1)
                if k >= 2:
                    c = k - 2
                    for n in range(4 * c, 4 * c + 5):
                        if n < 4 * c + 4:
                            if n >= 2 and n % 2 == 1:
                                dve.wait_ge(S("wx_filled"), n - 1)
                            empty(dve, "lnw", n, n + 1, move_lnw)
                        if n > 4 * c:
                            dve.wait_ge(S("wx"), n)
                            dve.bn_stats(bn_st[:, n - 1, :],
                                         wx[:, 4 * n - 4:4 * n, :].rearrange("d t h -> d (t h)")).then_inc(S("bn"), 1)
            dve.wait_ge(S("bn"), G4)
            link(dve.bn_aggr(sc[:, 60:62], bn_st.rearrange("d g c -> d (g c)")))
            inv_root(s("bs"), sc[:, 61:62], EPS, s("gamma"))
            link(TT(s("x0"), sc[:, 60:61], s("bs"), ALU.mult))
            TT(s("bb"), s("beta"), s("x0"), ALU.subtract).then_inc(S("bn_ab"), 1)
            dve.wait_ge(S("bn_ab"), 1)
            dve.wait_ge(S("wx"), G4)
            for q in range(2, 4):
                TS(z_s[:, q, :, :], wx[:, :, STEPS * q:STEPS * q + STEPS].rearrange("d t j -> d j t"),
                   s("bs"), s("bb"), ALU.mult, ALU.add).then_inc(S("z_dve"), 1)

            def shifted(o, last):
                dve.tensor_copy(o[:, 1:Q, :], last[:, 0:Q - 1, :])
                link(dve.tensor_copy(o[:, 0, 1:NT], last[:, Q - 1, 0:NT - 1]))
                link(dve.memset(o[:, 0, 0:NT:TB], 0.0))

            def sweep(p0, k0, j0):
                if j0:
                    dve.wait_ge(S("z_act"), 2)
                    dve.wait_ge(S("z_dve"), 2)
                    dve.memset(y_s[:, :, j0 - 1, :], 0.0).then_inc(S("state"), Q)
                for dj in range(2):
                    for q in range(Q):
                        b = PS[:, q + 4 * dj, 0:NT]
                        dve.wait_ge(S("vy"), 4 * (k0 + dj) + (q + 1))
                        TT(b, b, z_s[:, q, j0 + dj, :], ALU.add).then_inc(S("z_sum"), 1)
                with dve.Fori(1, (STEPS - j0) // 2) as i:
                    for dj in range(2):
                        for q in range(Q):
                            b = PS[:, q + 4 * dj, 0:NT]
                            dve.wait_ge(S("vy"), i * (2 * Q) + (4 * (k0 + dj) + (q + 1)))
                            TT(b, b, BIG1[:, bass.ds(i * (2 * NT) + NT * (j0 + dj + STEPS * q), NT)],
                               ALU.add).then_inc(S("z_sum"), 1)

            def starts(p):
                dve.wait_ge(S("state"), Q * p)
                shifted(start_a, y_s[:, :, STEPS - 1, :])
                dve.tensor_copy(y_s[:, :, STEPS - 1, :], start_a).then_inc(S("state"), Q)

            def judge(p):
                dve.wait_ge(S("state"), Q * p)
                shifted(start_b, y_s[:, :, STEPS - 1, :])
                link(TT(start_b, start_b, start_a, ALU.subtract))
                link(TT(start_b, start_b, start_b, ALU.mult))
                dve.tensor_reduce(s("gap"), start_b, AX.XY, ALU.max).then_inc(S("gap"), 1)
                dve.wait_ge(S("gap_filled"), 1)
                link(dve.tensor_reduce(sc[0:1, 63:64], PS[0:1, 0, 0:NT], AX.X, ALU.max))
                link(TS(sc[0:1, 63:64], sc[0:1, 63:64], TOL * TOL, None, ALU.is_le))
                TS(FLAG[0:1, 0:1], sc[0:1, 63:64], -1.0, 1.0, ALU.mult, ALU.add).then_inc(S("judged"), 1)

            recur(dve, sweep, starts, judge)
            for g in range(G4):
                dve.wait_ge(S("yt_filled"), g + 1)
                v = a0[:, 4 * g:4 * g + 4, :].rearrange("h t w -> h (t w)")
                TT(v, v, bank(g % 8), ALU.add).then_inc(S("result"), 1)


_NAMES = ["x", "L0_conv_key_w", "L0_conv_key_skip_w", "L0_conv_query_w", "L0_conv_query_skip_w",
          "L0_conv_value_w", "L0_conv_value_skip_w", "L0_conv_proj_w", "L0_conv_proj_skip_w",
          "L0_conv_norm1_g", "L0_conv_attn_norm_g", "L0_conv_attn_norm_b", "L0_conv_norm2_g",
          "L0_conv_norm2_b", "L0_conv_mixer_w1", "L0_conv_mixer_skip_w1", "L0_conv_mixer_skip_b1",
          "L0_conv_mixer_norm_g1", "L0_conv_mixer_norm_b1", "L0_conv_mixer_w2",
          "L0_conv_mixer_skip_w2", "L0_conv_mixer_norm_g2", "L0_conv_mixer_out_g",
          "L0_conv_mixer_out_b", "L0_ffn_W", "L0_ffn_V", "L0_ffn_gamma", "L0_ffn_beta"]


def kernel(**inputs):
    import concourse.bacc as bacc
    from concourse.bass_utils import run_bass_kernel_spmd as run

    nc = bacc.Bacc("TRN2", target_bir_lowering=False, num_devices=1)
    arrays, tensors = {}, {}
    for name in _NAMES + ["const"]:
        a = np.ascontiguousarray(CONST if name == "const" else inputs[name])
        arrays[f"in_{name}"] = a
        tensors[name.replace("L0_conv_", "").replace("L0_ffn_", "")] = nc.dram_tensor(
            f"in_{name}", a.shape, mybir.dt.from_np(a.dtype), kind="ExternalInput").ap()
    out = nc.dram_tensor("out_x", inputs["x"].shape, F32, kind="ExternalOutput").ap()
    metaformer(nc, tensors, out)
    r = run(nc, [arrays], core_ids=[0])
    return r.results[0]["out_x"]
```

```python
from contextlib import ExitStack

import numpy as np
import concourse.bass as bass
from concourse import mybir

F32 = mybir.dt.float32
I32 = mybir.dt.int32
ALU = mybir.AluOpType
ACT = mybir.ActivationFunctionType
AX = mybir.AxisListType

NT, H, W = 128, 128, 128
NB, TB = 4, 32
NH, HG = 16, 4
MH, MW = 32, 16
MODES = MW * 2 * MH
LH, LW = 16, 8
NF = 65
PIX = H * W
LN_C_EPS, EPS = 1e-6, 1e-5
XC = 8
XR = H // XC
LN_DVE, LN_POOL = 2, 4
KA_POOL = 20
G4 = NT // 4
P2_T = 12
LAG_P2, LAG_M2 = 6, 9
LAG_LN, LAG_TR, LAG_MV, LAG_W, LAG_WX, LAG_BN = 6, 7, 8, 9, 10, 11
STEPS, BURN = 32, 10
Q = H // STEPS
CHUNKS = TB * Q
TOL = 1e-6

FUNCS = [("c", 0), ("c", 32)] + [("c", k) for k in range(1, 32)] + [("s", k) for k in range(1, 33)]
COS = {k: i for i, (f, k) in enumerate(FUNCS) if f == "c"}
SIN = {k: i for i, (f, k) in enumerate(FUNCS) if f == "s"}

SCALARS = ["norm1_g", "attn_norm_g", "attn_norm_b", "norm2_g", "norm2_b", "mixer_norm_g1",
           "mixer_norm_b1", "mixer_norm_g2", "mixer_out_g", "mixer_out_b", "mixer_skip_w1",
           "mixer_skip_b1", "mixer_skip_w2"]
ROW_AT = {n: (i, 1) for i, n in enumerate(SCALARS)}
for _i, _n in enumerate(["query_skip_w", "key_skip_w", "value_skip_w", "proj_skip_w"]):
    ROW_AT[_n] = (len(SCALARS) + NH * _i, NH)
ROW_W = len(SCALARS) + 4 * NH
ROW_AT["mixer_w1"] = (ROW_W, MH * 17 * 2)
ROW_AT["mixer_w2"] = (ROW_W + MH * 17 * 2, MH * 17 * 2)
ROW_N = ROW_W + 2 * MH * 17 * 2


def constants():
    n = np.arange(128)

    def func(f, k):
        a = 2 * np.pi * n * k / 128
        return np.cos(a) if f == "c" else np.sin(a)

    half = np.array([2 ** -0.5 if f == "c" and k in (0, 32) else 1 for f, k in FUNCS])
    basis = np.stack([func(f, k) for f, k in FUNCS], 1) / 128 * half
    g = np.zeros((128, 64))
    for k in range(32):
        g[:, k] = func("c", k) * (1 if k == 0 else 2 ** 0.5)
    for k in range(1, 32):
        g[:, 31 + k] = func("s", k) * 2 ** 0.5
    g = g * 8 / 128
    gram = g * 2 ** 0.5
    edge = np.zeros((128, 2, 64))
    for i, (f, k) in enumerate(FUNCS[:64]):
        edge[:, 0, i] = func(f, k) * half[i]
        edge[:, 1, i] = {"c": 1, "s": -1}[f] * func("s" if f == "c" else "c", k) * half[i]
    edge = edge.reshape(128, 128) / 128 * (8 / 128 * 2 ** 0.5)
    h = np.concatenate([np.arange(16), np.arange(-16, 0)])
    ah = 2 * np.pi * np.outer(n, h) / 128
    ch, sh = np.cos(ah), np.sin(ah)
    row_modes = np.concatenate([ch, -sh, -sh, -ch], 1) / 128
    aw = 2 * np.pi * np.outer(n, np.arange(17)) / 128
    cw, sw = np.cos(aw), np.sin(aw)
    col_modes = np.concatenate([cw, -sw, -sw, -cw, sw, cw], 1) / 128
    basis17 = np.concatenate([cw, sw[:, 1:]], 1) / 128
    fr = np.zeros((128, 128))
    fr[:64] = np.concatenate([ch.T, -sh.T], 0)
    block = np.zeros((128, 512))
    for j in range(4):
        block[32 * j:32 * j + 16, 128 * j:128 * j + 128] = 2 * cw.T[1:17]
        block[32 * j + 16:32 * j + 32, 128 * j:128 * j + 128] = 2 * sw.T[1:17]
    at, out, x = {}, [], 0
    for name, p in (("ident", np.eye(128)), ("basis", basis), ("gram", gram), ("edge", edge),
                    ("row_modes", row_modes), ("col_modes", col_modes), ("basis17", basis17),
                    ("fr", fr), ("block", block), ("ones", np.ones((128, 128)))):
        at[name] = (x, p.shape[1])
        out.append(p)
        x += p.shape[1]
    return np.concatenate(out, 1).astype(np.float32), at


CONST, CONST_AT = constants()


def metaformer(nc, t, out):
    x_tok = t["x"].rearrange("b s h w -> (b s) h w")
    x_row = t["x"].rearrange("b s h w -> h (b s) w")
    out_row = out.rearrange("b s h w -> h (b s) w")
    ctx = ExitStack()
    with ctx:
        def sb(name, shape, dt=F32):
            return ctx.enter_context(nc.sbuf_tensor(name, shape, dt))

        def sem(name):
            return ctx.enter_context(nc.semaphore(name))

        PS = ctx.enter_context(nc.psum_tensor("PS", [128, 8, 512], F32))
        CST = sb("CST", [128, CONST.shape[1]])

        def const(name):
            a, n = CONST_AT[name]
            return CST[:, a:a + n]

        ident, basis, gram_fn, edge_fn = const("ident"), const("basis"), const("gram"), const("edge")
        row_modes, col_modes, basis17 = const("row_modes"), const("col_modes"), const("basis17")
        fr, block_w, ones = const("fr"), const("block"), const("ones")

        BIG1 = sb("BIG1", [128, PIX])
        BIG2 = sb("BIG2", [128, PIX])
        BIG3 = sb("BIG3", [128, PIX])
        SML = sb("SML", [128, 2624])
        FLAG = sb("FLAG", [1, 1], I32)

        def flat(a):
            n = 1
            for k in a.shape:
                n *= k
            names = "abcde"[:len(a.shape)]
            v = a.rearrange(" ".join(names) + " -> (" + " ".join(names) + ")") if len(names) > 1 else a
            return v.unsqueeze(0)

        x_t = BIG1[:, :].rearrange("t (h w) -> t h w", w=W)
        m1 = BIG1[:, :].rearrange("h (t w) -> h t w", w=W)
        z_s = BIG1[:, :].rearrange("d (q j t) -> d q j t", q=Q, t=NT)
        x_w = BIG2[:, :].rearrange("w (h t) -> w h t", t=NT)
        a0 = BIG2[:, :].rearrange("h (t w) -> h t w", w=W)
        rx = BIG2[:, 0:4096].rearrange("f (j t) -> f j t", t=NT)
        u_re = BIG2[:, 4096:6144].rearrange("m (n t) -> m n t", t=NT)
        u_im = BIG2[:, 6144:8192].rearrange("m (n t) -> m n t", t=NT)
        u_p = BIG2[:, 8192:10240].rearrange("m (n t) -> m n t", t=NT)
        u_q = BIG2[:, 10240:12288].rearrange("m (n t) -> m n t", t=NT)
        scr = BIG2[:, 12288:12800].rearrange("t (n s) -> t n s", s=TB)
        prob = BIG2[:, 12800:13312].rearrange("t (n s) -> t n s", s=TB)
        stmp = BIG2[:, 13312:13824].rearrange("t (n s) -> t n s", s=TB)
        edge_t = BIG2[0:64, 14020:14148]
        g_s = BIG2[:, 14148:14276]
        xlow = BIG2[:, 14276:14532].rearrange("t (v w h) -> t v w h", v=2, w=LW)
        xlow_t = BIG2[:, 14532:14788].rearrange("m (v t) -> m v t", v=2)
        cbd = BIG2[:, 14788:14916]
        cf = BIG2[:, 14916:15044]
        k1x = BIG2[:, 15044:15172]
        c32 = BIG2[:, 15172:15204]
        g_c = BIG2[:, 15204:15236]
        sel_x = BIG2[:, 15272:15784].rearrange("t (b p) -> t b p", b=NB)
        sel_w = BIG2[0:NH, 15784:16296].rearrange("n (g p) -> n g p", g=4)
        sq_dump = BIG2[:, 12288:13312]
        smax = BIG2[:, 15236:15252]
        ssum = BIG2[:, 15252:15268]

        row1 = BIG3[0:1, 0:ROW_N]
        row_var = BIG3[:, 2816:2944]
        vr = BIG3[:, 2944:3072]
        p1 = BIG3[:, 0:NF * NT].rearrange("h (f t) -> h f t", t=NT)
        wcp = BIG3[0:NH, 8320:8320 + 1088 + 3 * 288 + 2]
        w_proj = wcp[:, 0:1088].rearrange("n (h w v) -> n h w v", h=MH, v=2)
        w_val = wcp[:, 1088:1376].rearrange("n (h w v) -> n h w v", h=LH, v=2)
        w_key = wcp[:, 1376:1664].rearrange("n (h w v) -> n h w v", h=LH, v=2)
        w_qry = wcp[:, 1664:1952].rearrange("n (h w v) -> n h w v", h=LH, v=2)
        wy = BIG3[0:NH, 10276:11300].rearrange("n (w v h) -> n w v h", v=2, h=MH)
        wtmp = BIG3[0:NH, 11300:11812].rearrange("n (w h) -> n w h", h=MH)
        aqk = BIG3[:, 12352:12416].rearrange("m (k n) -> m k n", n=NH)
        mqk = BIG3[:, 12320:12352].rearrange("m (k n) -> m k n", n=NH)
        wqk = BIG3[:, 12288:12304]
        qk_c = BIG3[0:NH, 7600:8112].rearrange("n (k w h) -> n k w h", k=4, h=LH)
        mqt = BIG3[:, 11940:11956]
        pswv = BIG3[:, 12304:12320]
        PRM = BIG3[:, 12544:12544 + ROW_N]
        gf = BIG3[:, 12416:12544]
        row_sum = BIG3[:, 14800:15312].rearrange("w (k t) -> w k t", t=NT)
        edge_x = BIG3[:, 11956:12212].rearrange("w (k t) -> w k t", t=NT)
        t0 = BIG3[:, 14800:15824]
        prob_t = BIG3[:, 15824:16336].rearrange("p (g t) -> p g t", g=4)
        rep = BIG3[:, 0:8192]
        wr = BIG3[:, 0:4096].rearrange("p (g w v h) -> p g w v h", g=4, v=2, h=MH)
        xrep = BIG3[:, 4096:8192].rearrange("p (b w v h) -> p b w v h", b=4, v=2, h=MH)

        def prod(n):
            hg, b = n // 4, n % 4
            v = BIG2[:, 4096 + 2048 * b:6144 + 2048 * b] if hg % 2 else (
                BIG2[:, 2048 * b:2048 * b + 2048] if b < 2 else BIG3[:, 4096 + 2048 * b:6144 + 2048 * b])
            return v.rearrange("p (a w v h) -> p a w v h", a=2, v=2, h=MH)
        zt = BIG3[0:64, 0:4096].rearrange("k (t p) -> k t p", p=32)
        ta1 = BIG3[:, 4096:8192].rearrange("k (g n) -> k g n", n=H)
        y_m = BIG3[:, 8192:9216]
        ma = BIG3[:, 9216:10240]
        zw = BIG3[:, 10240:11264]
        ztmp = BIG3[:, 11264:12288]
        stage = BIG3[:, 14800:16336].rearrange("h (k t w) -> h k t w", k=3, w=W)
        p2 = BIG3[:, 0:33 * NT].rearrange("w (f t) -> w f t", t=NT)
        x1m = BIG3[:, 4352:5440].rearrange("t (h v w) -> t h v w", v=2, w=17)
        z2 = BIG3[:, 5440:6528].rearrange("t (h v w) -> t h v w", v=2, w=17)
        z2q = BIG3[:, 0:1024]
        z2g = BIG3[:, 1024:1056]
        z2t = BIG3[:, 6528:7616].rearrange("t (h v w) -> t h v w", v=2, w=17)
        ta2 = BIG3[:, 12288:16384].rearrange("k (g n) -> k g n", n=H)
        st2 = BIG3[:, 10240:10240 + NT * 6].rearrange("h (t k) -> h t k", k=6)
        wx = BIG3[:, :].rearrange("d (t h) -> d t h", h=H)
        y_s = BIG3[:, :].rearrange("d (q j t) -> d q j t", q=Q, t=NT)

        ts = SML[:, 0:1024]
        ln_w = SML[:, 0:1024].rearrange("w (k t h) -> w k t h", k=2, h=H)
        start_a = SML[:, 0:512].rearrange("d (q t) -> d q t", q=Q)
        start_b = SML[:, 512:1024].rearrange("d (q t) -> d q t", q=Q)
        cft = SML[:, 1024:1152]
        acft = SML[:, 1152:1280]
        ln_r = SML[:, 1024:1152]
        ln_b = SML[:, 1152:1280]
        w_t = SML[:, 1280:1408]
        v_t = SML[:, 1408:1536]
        sc = SML[:, 1536:1600]
        kap = SML[:, 1600:1728]
        bet = SML[:, 1728:1856]
        g0 = SML[:, 1856:1984]
        dg = SML[:, 1984:2112]
        z0 = SML[:, 2112:2176]
        z0t = SML[0:64, 2176:2304]
        ln_st = SML[:, 2304:2496].rearrange("p (k v c) -> p k v c", k=2, c=6)
        ln_tmp = SML[:, 2496:2624].rearrange("p (k v) -> p k v", v=16)
        bn_st = SML[:, 1984:2176].rearrange("p (g c) -> p g c", c=6)
        scn = {}

        def s(name):
            if name not in scn:
                scn[name] = len(scn)
                assert len(scn) <= 64
            return sc[:, scn[name]:scn[name] + 1]

        def prm(name):
            a, n = ROW_AT[name]
            return PRM[:, a:a + n]

        def modes(a):
            return a.rearrange("t (w v h) -> t w v h", v=2, h=MH)
        z3_1 = BIG3[:, 4096:5632].rearrange("t (w k h) -> t w k h", k=3, h=MH)
        z3_2 = BIG3[:, 9216:10752].rearrange("t (w k h) -> t w k h", k=3, h=MH)

        sems = {}

        def S(name):
            if name not in sems:
                sems[name] = sem(name)
            return sems[name]

        def bank(k):
            return PS[:, k, :]

        cx_ps = PS[:, 0:2, :].rearrange("t a n -> t (a n)")
        y_ps = PS[:, 2:4, :].rearrange("t a n -> t (a n)")
        modes_ps = PS[:, 4:6, :].rearrange("t a n -> t (a n)")

        P1_N = [min(7, NT - 7 * g) for g in range((NT + 6) // 7)]
        P2_N = [min(P2_T, NT - P2_T * g) for g in range((NT + P2_T - 1) // P2_T)]
        X1_N = [15, 15, 2]

        def emptied(e, name, n):
            if (n + 1) // 2:
                e.wait_ge(S(name + "_act"), (n + 1) // 2)
            if n // 2:
                e.wait_ge(S(name + "_dve"), n // 2)

        def empty(e, name, n0, n1, move):
            act = e is scalar_engine
            for n in range(n0, n1):
                if (n % 2 == 0) == act:
                    e.wait_ge(S(name + "_filled"), n + 1)
                    move(e, n).then_inc(S(name + ("_act" if act else "_dve")), 1)

        def copy(e, o, i):
            return e.activation(o, i, ACT.Copy) if e is scalar_engine else e.tensor_copy(o, i)

        def move_col(e, n):
            return copy(e, x_w[:, 4 * n:4 * n + 4, :].rearrange("w h t -> w (h t)"), bank(n % 4))

        def move_p1(e, n):
            k = P1_N[n]
            return copy(e, p1[:, :, 7 * n:7 * n + k],
                        PS[:, n % 4, 0:NF * k].rearrange("h (t f) -> h f t", f=NF))

        def move_rx(e, n):
            return copy(e, rx[:, 4 * n:4 * n + 4, :].rearrange("f j t -> f (j t)"), bank(n % 4))

        def move_zt(base):
            return lambda e, n: copy(e, zt[:, :, 4 * n:4 * n + 4],
                                     PS[0:64, base + n % 4, :].rearrange("k (p t) -> k t p", p=4))

        def move_ta(ta, base):
            return lambda e, n: copy(e, ta[:, 4 * n:4 * n + 4, :].rearrange("k g n -> k (g n)"),
                                     bank(base + n % 4))

        def move_p2(e, n):
            k = P2_N[n]
            return copy(e, p2[:, :, P2_T * n:P2_T * n + k],
                        PS[:, 4 + n % 4, 0:33 * k].rearrange("w (t f) -> w f t", f=33))

        def empty_p2(e, i):
            g = i - LAG_M2
            if g >= 0 and (g % (P2_T // 4) == P2_T // 4 - 1 or g == G4 - 1):
                n = 4 * g // P2_T
                empty(e, "p2", n, n + 1, move_p2)

        def move_lnw(e, n):
            return copy(e, ln_w[:, n % 2, :, :].rearrange("w t h -> w (t h)"), bank(n % 2))

        def recur(e, sweep, starts=None, judge=None):
            sweep(1, 0, STEPS - BURN)
            if starts:
                starts(BURN + 1)
            sweep(BURN + 2, BURN, 0)
            done = BURN + 2 + STEPS
            if judge:
                judge(done)
            e.wait_ge(S("judged"), 1)
            again = e.value_load(FLAG[0:1, 0:1], min_val=0, max_val=1)
            with e.If(again > 0):
                with e.Fori(0, CHUNKS - 1) as i:
                    if starts:
                        starts(i * (STEPS + 1) + done)
                    sweep(i * (STEPS + 1) + (done + 1), i * STEPS + (BURN + STEPS), 0)
                e.wait_ge(S("state"), Q * (done + (STEPS + 1) * (CHUNKS - 1)))
            e.wait_ge(S("state"), Q * done)

        scalar_engine = nc.scalar
        small = ctx.enter_context(nc.allow_non_contiguous_dma("weights' columns"))
        block = ctx.enter_context(nc.Block())

        @block.sync
        def _(sp):
            sp.dma_start(ident, t["const"][:, 0:128]).then_inc(S("ident_in"), 16)
            for c in range(XC):
                rows = slice(XR * c, XR * c + XR)
                sp.dma_start(x_t[:, rows, :], x_tok[:, rows, :]).then_inc(S(f"x_in{c}"), 16)
            sp.dma_start(CST[:, 128:], t["const"][:, 128:]).then_inc(S("const_in"), 16)
            for name, (a, n) in ROW_AT.items():
                sp.dma_start(row1[:, a:a + n], flat(t[name])).then_inc(S("row_in"), 16)
            sp.dma_start(wcp[:, 0:1088], t["proj_w"].rearrange("n o h w v -> n (o h w v)")).then_inc(S("w_in"), 16)
            for name, a in (("value_w", 1088), ("key_w", 1376), ("query_w", 1664)):
                sp.dma_start(wcp[:, a:a + 288], t[name].rearrange("o n h w v -> n (o h w v)")).then_inc(S("w_in"), 16)
            sp.dma_start(wcp[:, 1952:1953], t["value_skip_w"].rearrange("o n -> n o")).then_inc(S("w_in"), 16)
            sp.dma_start(wcp[:, 1953:1954], t["proj_skip_w"]).then_inc(S("w_in"), 16)
            sp.dma_start(w_t, t["W"]).then_inc(S("w_in"), 16)
            sp.dma_start(v_t, t["V"]).then_inc(S("w_in"), 16)
            sp.dma_start(s("gamma"), t["gamma"].unsqueeze(1)).then_inc(S("w_in"), 16)
            sp.dma_start(s("beta"), t["beta"].unsqueeze(1)).then_inc(S("w_in"), 16)
            sp.wait_ge(S("y_filled"), 1)
            for g in range(G4):
                if g >= 3:
                    sp.wait_ge(S("xa"), g - 2)
                sp.dma_start(stage[:, g % 3, :, :],
                             x_row[:, 4 * g:4 * g + 4, :]).then_inc(S(f"stage_in{g % 3}"), 16)
            for g in range(G4):
                sp.wait_ge(S("result"), g + 1)
                sp.dma_start(out_row[:, 4 * g:4 * g + 4, :],
                             a0[:, 4 * g:4 * g + 4, :]).then_inc(S("stored"), 16)
            sp.wait_ge(S("stored"), 16 * G4)

        SMALL_IN = 10

        @block.gpsimd
        def _(pool):
            seq = [0]

            def link(ins):
                seq[0] += 1
                ins.then_inc(S("pool_seq"), 1)
                pool.wait_ge(S("pool_seq"), seq[0])

            for c in range(XC):
                pool.wait_ge(S("ln_coef"), c + 1)
                for row in range(XR * c + LN_DVE, XR * c + LN_DVE + LN_POOL):
                    last = pool.tensor_scalar(x_t[:, row, :], x_t[:, row, :], ln_r[:, row:row + 1],
                                              ln_b[:, row:row + 1], ALU.mult, ALU.add)
                last.then_inc(S("ln_pool"), 1)
            pool.wait_ge(S("w_in"), 16 * SMALL_IN)
            wv, ps = wcp[:, 1952:1953], wcp[:, 1953:1954]
            lows = [slice(0, 8), slice(24, 32)]
            for k, (wt, part) in enumerate(((w_qry, 0), (w_qry, 1), (w_key, 0), (w_key, 1))):
                last = pool.tensor_copy(qk_c[:, k, :, :], wt[:, :, 1:9, part].rearrange("n h w -> n w h"))
            last.then_inc(S("qk_c"), 1)
            tmp = wtmp

            def b(part, lo=None, w=MW):
                v = w_proj[:, :, 1:1 + w, part] if lo is None else w_proj[:, lo, 1:1 + w, part]
                return v.rearrange("n h w -> n w h")

            def a(part, k):
                return w_val[:, 8 * k:8 * k + 8, 1:9, part].rearrange("n h w -> n w h")

            for part in range(2):
                link(pool.tensor_scalar(wy[:, :, part, :], b(part), wv, None, ALU.mult))
            for k, lo in enumerate(lows):
                tk = tmp[:, 0:LW, 8 * k:8 * k + 8]
                for part, (p, q, op) in ((0, (0, 0, ALU.add)), (0, (1, 1, ALU.subtract)),
                                      (1, (0, 1, ALU.add)), (1, (1, 0, ALU.add))):
                    o = wy[:, 0:LW, part, lo]
                    link(pool.tensor_tensor(tk, b(p, lo, LW), a(q, k), ALU.mult))
                    link(pool.tensor_tensor(o, o, tk, op))
                for part in range(2):
                    o = wy[:, 0:LW, part, lo]
                    link(pool.tensor_scalar(tk, a(part, k), ps, None, ALU.mult))
                    link(pool.tensor_tensor(o, o, tk, ALU.add))
            pool.wait_ge(S("const_in"), 16)
            pool.wait_ge(S("p1_filled"), len(P1_N))
            pool.wait_ge(S("edge_x"), 1)
            for k in range(4):
                pool.tensor_copy(sel_x[:, k, :].rearrange("t (n s) -> t n s", n=HG),
                                 ident[:, TB * k:TB * k + TB].unsqueeze(1).to_broadcast([128, HG, TB]))
                last = pool.tensor_copy(sel_w[:, k, :].rearrange("m (n s) -> m n s", n=HG),
                                        ident[0:NH, HG * k:HG * k + HG].unsqueeze(2).to_broadcast([NH, HG, TB]))
            last.then_inc(S("wy"), 1)

            pool.wait_ge(S("m_low"), 1)
            mb = mqk[:, 1, :].unsqueeze(2).to_broadcast([128, NH, NT])
            xb = [xlow_t[:, k, :].unsqueeze(1).to_broadcast([128, NH, NT]) for k in range(2)]
            pool.tensor_tensor(u_p, mb, xb[1], ALU.mult).then_inc(S("u_prod"), 1)
            pool.tensor_tensor(u_q, mb, xb[0], ALU.mult).then_inc(S("u_prod"), 1)

            for n in range(16):
                hg, b = n // 4, n % 4
                if n == 0:
                    pool.wait_ge(S("rep"), 16)
                    pool.wait_ge(S("g_filled"), 1)
                if n == 4:
                    pool.wait_ge(S("s_filled"), 1)
                if n >= 8:
                    pool.wait_ge(S("prod_used"), hg - 1)
                pool.tensor_tensor(prod(n)[:, 1, :, 1, :], xrep[:, b, :, 0, :], wr[:, hg, :, 1, :],
                                   ALU.mult).then_inc(S("prod_pool"), 1)

            pool.wait_ge(S("kap"), 1)
            for g in range(KA_POOL):
                pool.wait_ge(S("a0"), g + 1)
                if g == 0:
                    pool.wait_ge(S("mix_filled"), 32)
                w = slice(4 * g, 4 * g + 4)
                pool.tensor_tensor(m1[:, :, w], a0[:, :, w], kap.unsqueeze(2).to_broadcast([128, NT, 4]),
                                   ALU.mult).then_inc(S("ka0"), 1)
            pool.wait_ge(S("ka0"), 32)
            for g in range(G4):
                pool.wait_ge(S(f"stage_in{g % 3}"), 16 * (g // 3 + 1))
                v = a0[:, 4 * g:4 * g + 4, :]
                pool.tensor_tensor(v, v, stage[:, g % 3, :, :], ALU.add).then_inc(S("xa"), 1)
            pool.wait_ge(S("xa"), G4)
            for i in range(G4 + LAG_LN):
                if i < G4:
                    pool.wait_ge(S("bm1"), i + 1)
                    v = a0[:, 4 * i:4 * i + 4, :]
                    pool.tensor_tensor(v, v, m1[:, 4 * i:4 * i + 4, :], ALU.add).then_inc(S("xm"), 1)
                g = i - LAG_LN
                if g >= 0:
                    pool.wait_ge(S("ln2_coef"), g // 4 + 1)
                    n = 4 * g + 3
                    pool.tensor_scalar(m1[:, n, :], a0[:, n, :], ln_r[:, n:n + 1], ln_b[:, n:n + 1],
                                       ALU.mult, ALU.add).then_inc(S("ln2_pool"), 1)

        @block.tensor
        def _(pe):
            def mm(o, l, rhs, start=True, stop=True, **k):
                return pe.matmul(o, l, rhs, start=start, stop=stop, **k)

            def tr(o, i):
                n = i.partition_size() if callable(i.partition_size) else i.partition_size
                return pe.matmul(o, i, ident[0:n, 0:n], is_transpose=True, start=True, stop=True)

            def gram(n):
                emptied(pe, "col", n + 1)
                for h in range(4 * n, 4 * n + 4):
                    last = mm(PS[:, 7, 0:128], x_w[:, h, :], x_w[:, h, :], h == 0, h == H - 1)
                return last

            pe.wait_ge(S("ident_in"), 16)
            for c in range(XC):
                pe.wait_ge(S("ln_act"), c + 1)
                pe.wait_ge(S("ln_dve"), c + 1)
                pe.wait_ge(S("ln_pool"), c + 1)
                for n in range(4 * c, 4 * c + 4):
                    if n >= 4:
                        emptied(pe, "col", n - 3)
                    for h in range(4 * n, 4 * n + 4):
                        last = tr(PS[:, n % 4, 128 * (h % 4):128 * (h % 4) + 128], x_t[:, h, :])
                    last.then_inc(S("col_filled"), 1)
                    if n >= 4:
                        gram(n - 4)
                if c >= 5:
                    if c == 5:
                        pe.wait_ge(S("const_in"), 16)
                        pe.wait_ge(S("row_in"), 16 * len(ROW_AT))
                    for k in ((0, 1), (2, 3), (4,))[c - 5]:
                        if k >= 3:
                            pe.wait_ge(S("prm"), k - 2)
                        a, b = 512 * k, min(512 * k + 512, ROW_N)
                        mm(PS[:, 4 + k % 3, 0:b - a], ones[0:1, :], row1[:, a:b]).then_inc(S("prm_filled"), 1)
            pe.wait_ge(S("w_in"), 16 * SMALL_IN)
            pe.wait_ge(S("prm"), 5)
            pe.wait_ge(S("qk_c"), 1)
            for k in range(4):
                tr(PS[:, 4, 16 * k:16 * k + 16], qk_c[:, k, :, :])
            tr(PS[:, 5, 0:128], w_t)
            tr(PS[:, 5, 128:256], v_t).then_inc(S("wt_filled"), 1)
            for n in range(28, 31):
                gram(n)
            gram(31).then_inc(S("gf_filled"), 1)

            for g, k in enumerate(P1_N):
                if g >= 4:
                    emptied(pe, "p1", g - 3)
                for j in range(k):
                    last = mm(PS[:, g % 4, NF * j:NF * j + NF], x_w[:, :, 7 * g + j], basis)
                last.then_inc(S("p1_filled"), 1)
            emptied(pe, "p1", len(P1_N))
            pe.wait_ge(S("edge_x"), 1)
            for k in range(2):
                last = mm(PS[0:64, 6, 256:384], edge_fn[:, 64 * k:64 * k + 64], edge_x[:, k, :], k == 0, k == 1)
            last.then_inc(S("edge_t_filled"), 1)
            pe.wait_ge(S("wt"), 1)
            for w in range(1, 17):
                o = PS[:, 4 + (w - 1) // 8, 64 * ((w - 1) % 8):64 * ((w - 1) % 8) + 64]
                mm(o, p1[:, COS[w], :], row_modes[:, 0:64], True, False)
                last = mm(o, p1[:, SIN[w], :], row_modes[:, 64:128], False, True)
            last.then_inc(S("modes_filled"), 1)
            for j in range(8):
                if j >= 4:
                    emptied(pe, "rx", j - 3)
                for half in range(2):
                    o = PS[64 * half:64 * half + 64, j % 4, :]
                    f = 32 * half + 4 * j
                    last = mm(o, gram_fn, p1[:, f:f + 4, :])
                last.then_inc(S("rx_filled"), 1)
            pe.wait_ge(S("xlow"), 1)
            tr(PS[:, 4, 0:128], xlow[:, 0, :, :])
            tr(PS[:, 4, 128:256], xlow[:, 1, :, :]).then_inc(S("xlow_filled"), 1)
            emptied(pe, "rx", 8)
            pe.wait_ge(S("gf"), 1)
            for j in range(32):
                mm(PS[:, 7, 0:128], rx[:, j, :], rx[:, j, :], j == 0, False)
            pe.wait_ge(S("edge_t"), 1)
            mm(PS[:, 7, 0:128], edge_t, edge_t, False, True).then_inc(S("g_filled"), 1)
            pe.wait_ge(S("wy"), 1)
            for n in range(16):
                if n >= 4:
                    pe.wait_ge(S("rep"), n - 3)
                half = n % 2
                if n < 8:
                    k = n // 2
                    sel = sel_w[:, k, :]
                    rhs = wy[:, 8 * half:8 * half + 8, :, :].rearrange("n w v h -> n (w v h)")
                else:
                    k = n // 2 - 4
                    sel = sel_x[:, k, :]
                    rhs = ts[:, 512 * half:512 * half + 512]
                    if n == 8:
                        pe.wait_ge(S("ts"), 1)
                if n == 8:
                    pe.wait_ge(S("u"), 1)
                    for part, u in enumerate((u_re, u_im)):
                        for b in range(NB):
                            tb = slice(TB * b, TB * b + TB)
                            last = mm(PS[tb, 5, :], xlow_t[:, part, tb], u[:, :, tb], part == 0, part == 1,
                                      skip_group_check=True)
                    last.then_inc(S("s_filled"), 1)
                mm(bank(n % 4), sel, rhs).then_inc(S("rep_filled"), 1)
                if n == 3:
                    pe.wait_ge(S("g_s"), 1)
                    tr(PS[:, 6, 384:512], g_s).then_inc(S("g_t_filled"), 1)

            def attend(hg):
                for n in range(4 * hg, 4 * hg + 4):
                    pe.wait_ge(S("prod_dve"), n + 1)
                    pe.wait_ge(S("prod_pool"), n + 1)
                for a in range(2):
                    for k in range(2):
                        for b in range(NB):
                            tb = slice(TB * b, TB * b + TB)
                            rhs = prod(4 * hg + b)[:, a, 8 * k:8 * k + 8, :, :].rearrange("p w v h -> p (w v h)")
                            last = mm(PS[tb, 2 + k, :], prob_t[:, hg, tb], rhs, hg == 0 and a == 0,
                                      hg == 3 and a == 1, skip_group_check=True)
                return last

            pe.wait_ge(S("prob"), 1)
            for k in range(4):
                last = tr(PS[:, 4, 128 * k:128 * k + 128], prob[:, 4 * k:4 * k + 4, :])
            last.then_inc(S("pt_filled"), 1)
            pe.wait_ge(S("rep"), 16)
            pe.wait_ge(S("prob_t"), 1)
            attend(0).then_inc(S("prod_used"), 1)
            pe.wait_ge(S("cbd"), 1)
            tr(PS[:, 6, 0:128], cbd).then_inc(S("c_filled"), 1)
            attend(1).then_inc(S("prod_used"), 1)
            pe.wait_ge(S("cft"), 1)
            tr(PS[:, 6, 128:256], cft)
            mm(PS[:, 6, 256:384], cft, gf).then_inc(S("k1_filled"), 1)
            for k in range(2):
                last = mm(bank(k), cft, t0[:, 512 * k:512 * k + 512])
            last.then_inc(S("cx_filled"), 1)
            attend(2).then_inc(S("prod_used"), 1)
            attend(3)
            mm(PS[0:1, 6, 0:1], ones[0:1, 0:1], ones[0:1, 0:1]).then_inc(S("y_filled"), 1)
            pe.wait_ge(S("dg"), 1)
            mm(PS[:, 6, 384:512], ones, dg).then_inc(S("bc_filled"), 1)
            pe.wait_ge(S("acft"), 1)
            for g in range(32):
                if g >= 4:
                    pe.wait_ge(S("a0"), g - 3)
                for w in range(4 * g, 4 * g + 4):
                    last = mm(PS[:, 4 + g % 4, 128 * (w % 4):128 * (w % 4) + 128], x_t[:, :, w], acft)
                last.then_inc(S("mix_filled"), 1)
                if g == 3:
                    pe.wait_ge(S("kap_dg"), 1)
                    mm(PS[:, 3, 0:128], ones, dg).then_inc(S("kap_filled"), 1)

            def inverse(i, z3, ta, zb, tb, b_free, consumed):
                for n in range(8):
                    if n >= 4:
                        emptied(pe, f"zt{i}", n - 3)
                    for p in range(4 * n, 4 * n + 4):
                        part, w = p // 16, p % 16
                        last = tr(PS[0:64, zb + n % 4, 128 * (p % 4):128 * (p % 4) + 128],
                                  z3[:, w, 1 - part:3 - part, :])
                    last.then_inc(S(f"zt{i}_filled"), 1)
                emptied(pe, f"zt{i}", 8)
                for n in range(8):
                    if n >= 4:
                        emptied(pe, f"ta{i}", n - 3)
                    for g in range(4 * n, 4 * n + 4):
                        last = mm(PS[:, tb + n % 4, 128 * (g % 4):128 * (g % 4) + 128],
                                  zt[:, 4 * g:4 * g + 4, :], fr[0:64, :])
                    last.then_inc(S(f"ta{i}_filled"), 1)

            pe.wait_ge(S("z3_1"), 1)
            pe.wait_ge(S("kap"), 1)
            pe.wait_ge(S("a0"), 32)
            inverse(1, z3_1, ta1, 0, 4, None, None)
            emptied(pe, "ta1", 8)
            for i in range(G4 + LAG_P2):
                if i < G4:
                    if i >= 4:
                        pe.wait_ge(S("u_sum"), i - 3)
                    mm(bank(i % 4), ta1[:, i, :], block_w).then_inc(S("b1_filled"), 1)
                g = i - LAG_P2
                if g >= 0:
                    n, j = 4 * g // P2_T, 4 * g % P2_T
                    if j == 0 and n >= 4:
                        emptied(pe, "p2", n - 3)
                    pe.wait_ge(S("m1"), g + 1)
                    for k in range(4):
                        last = mm(PS[:, 4 + n % 4, 33 * (j + k):33 * (j + k) + 33], m1[:, 4 * g + k, :], basis17)
                    if j + 4 == P2_N[n]:
                        last.then_inc(S("p2_filled"), 1)
            emptied(pe, "p2", len(P2_N))
            pe.wait_ge(S("u_sum"), G4)
            for i in range(MH):
                h = i if i < 16 else i - 32
                o = PS[:, i // 15, 34 * (i % 15):34 * (i % 15) + 34]
                last = mm(o, p2[:, abs(h), :], col_modes[:, 0:34], True, h == 0)
                if h:
                    a = 34 if h > 0 else 68
                    last = mm(o, p2[:, 16 + abs(h), :], col_modes[:, a:a + 34], False, True)
            last.then_inc(S("x1_filled"), 1)
            pe.wait_ge(S("rowsq"), 1)
            mm(PS[:, 3, 0:1], dg, ones[:, 0:1]).then_inc(S("sq_filled"), 1)
            pe.wait_ge(S("dg2"), 1)
            mm(PS[:, 3, 128:256], ones, dg)
            pe.wait_ge(S("z0"), 1)
            tr(PS[0:64, 3, 256:384], z0).then_inc(S("z0t_filled"), 1)
            pe.wait_ge(S("z0t"), 1)
            mm(PS[:, 3, 384:512], fr[0:64, :], z0t).then_inc(S("g0_filled"), 1)
            pe.wait_ge(S("z3_2"), 1)
            pe.wait_ge(S("g0"), 1)
            inverse(2, z3_2, ta2, 4, 0, None, None)
            emptied(pe, "ta2", 8)

            for i in range(G4 + LAG_W):
                if i < G4:
                    if i >= 4:
                        pe.wait_ge(S("x1"), i - 3)
                    mm(bank(4 + i % 4), ta2[:, i, :], block_w).then_inc(S("b2_filled"), 1)
                g = i - LAG_TR
                if 0 <= g < G4:
                    pe.wait_ge(S("ln2_act"), g + 1)
                    pe.wait_ge(S("ln2_dve"), g + 1)
                    pe.wait_ge(S("ln2_pool"), g + 1)
                    if g >= 2:
                        emptied(pe, "lnw", g - 1)
                    for j in range(4):
                        last = tr(PS[:, g % 2, 128 * j:128 * j + 128], m1[:, 4 * g + j, :])
                    last.then_inc(S("lnw_filled"), 1)
                g = i - LAG_W
                if g >= 0:
                    emptied(pe, "lnw", g + 1)
                    if g >= 2:
                        pe.wait_ge(S("wx"), g - 1)
                    mm(bank(2 + g % 2), w_t,
                       ln_w[:, g % 2, :, :].rearrange("w t h -> w (t h)")).then_inc(S("wx_filled"), 1)

            def sweep(p0, k0, j0):
                for dj in range(2):
                    j = j0 + dj
                    for q in range(Q):
                        pe.wait_ge(S("state"), 4 * (p0 + dj) + q - 3)
                        mm(PS[:, q + 4 * dj, 0:128], v_t, y_s[:, q, (j - 1) % STEPS, :]).then_inc(S("vy"), 1)
                with pe.Fori(1, (STEPS - j0) // 2) as i:
                    for dj in range(2):
                        for q in range(Q):
                            pe.wait_ge(S("state"), i * (2 * Q) + (4 * (p0 + dj) + q - 3))
                            mm(PS[:, q + 4 * dj, 0:128], v_t,
                               BIG3[:, bass.ds(i * (2 * NT) + NT * (j0 + dj - 1 + STEPS * q), NT)]).then_inc(S("vy"), 1)

            def judge(p):
                pe.wait_ge(S("gap"), 1)
                tr(PS[0:1, 0, 0:128], s("gap")).then_inc(S("gap_filled"), 1)

            recur(pe, sweep, None, judge)
            for g in range(G4):
                if g >= 8:
                    pe.wait_ge(S("result"), g - 7)
                for j in range(4):
                    last = tr(PS[:, g % 8, 128 * j:128 * j + 128],
                              y_s[:, :, :, 4 * g + j].rearrange("d q j -> d (q j)"))
                last.then_inc(S("yt_filled"), 1)

        @block.scalar
        def _(act):
            roots = [0]

            def root(o, i):
                roots[0] += 1
                act.wait_ge(S("root_of"), roots[0])
                act.activation(o, i, ACT.Sqrt).then_inc(S("root"), 1)

            def move_prm(k):
                a, b = 512 * k, min(512 * k + 512, ROW_N)
                act.wait_ge(S("prm_filled"), k + 1)
                act.activation(PRM[:, a:b], PS[:, 4 + k % 3, 0:b - a], ACT.Copy).then_inc(S("prm"), 1)

            for c in range(XC):
                root(ln_r[:, XR * c:XR * c + XR], ln_tmp[:, c % 2, :])
                if c:
                    empty(act, "col", 4 * c - 4, 4 * c, move_col)
                act.wait_ge(S("ln_coef"), c + 1)
                for row in range(XR * c + LN_DVE + LN_POOL, XR * c + XR):
                    last = act.activation(x_t[:, row, :], x_t[:, row, :], ACT.Identity,
                                          scale=ln_r[:, row:row + 1], bias=ln_b[:, row:row + 1])
                last.then_inc(S("ln_act"), 1)
                if c >= 6:
                    for k in ((0, 1), (2, 3))[c - 6]:
                        move_prm(k)
            empty(act, "col", 4 * XC - 4, 4 * XC, move_col)
            move_prm(4)
            act.wait_ge(S("wt_filled"), 1)
            act.activation(aqk.rearrange("m k n -> m (k n)"), PS[:, 4, 0:64], ACT.Copy)
            act.activation(w_t, PS[:, 5, 0:128], ACT.Copy)
            act.activation(v_t, PS[:, 5, 128:256], ACT.Copy).then_inc(S("wt"), 1)
            root(s("s1"), s("rt"))
            act.wait_ge(S("s1"), 1)
            empty(act, "p1", 0, len(P1_N), move_p1)
            act.wait_ge(S("t0"), 1)
            act.activation(ts, modes_ps, ACT.Copy, scale=s("s1")).then_inc(S("ts"), 1)
            empty(act, "rx", 0, 8, move_rx)
            for n in range(16):
                act.wait_ge(S("rep_filled"), n + 1)
                act.activation(rep[:, 512 * n:512 * n + 512], bank(n % 4), ACT.Copy).then_inc(S("rep"), 1)
            act.wait_ge(S("s_shift"), 1)
            act.activation(prob, scr, ACT.Exp).then_inc(S("s_exp"), 1)
            act.wait_ge(S("pt_filled"), 1)
            act.activation(prob_t.rearrange("p g t -> p (g t)"), bank(4), ACT.Copy).then_inc(S("prob_t"), 1)
            act.wait_ge(S("cx_filled"), 1)
            act.activation(sq_dump, cx_ps, ACT.Square, accum_out=s("p_cx")).then_inc(S("p_cx"), 1)
            act.wait_ge(S("ma"), 1)
            act.activation(ztmp, ma, ACT.Square, accum_out=s("p_ma")).then_inc(S("p_ma"), 1)
            root(s("al"), s("rt"))
            root(s("rm"), s("rt"))
            for g in range(32):
                if g == 6:
                    act.wait_ge(S("zw"), 1)
                    act.activation(ztmp, zw, ACT.Square, accum_out=s("p_z1")).then_inc(S("p_z1"), 1)
                if g == 14:
                    root(s("r1"), s("rt"))
                act.wait_ge(S("mix_filled"), g + 1)
                act.activation(a0[:, :, 4 * g:4 * g + 4],
                               PS[:, 4 + g % 4, :].rearrange("h (w t) -> h t w", w=4), ACT.Copy).then_inc(S("a0"), 1)
            empty(act, "zt1", 0, 8, move_zt(0))
            empty(act, "ta1", 0, 8, move_ta(ta1, 4))
            for i in range(G4 + LAG_M2):
                if i < G4:
                    act.wait_ge(S("u_sum"), i + 1)
                    v = m1[:, 4 * i:4 * i + 4, :]
                    act.activation(v, v, ACT.Gelu, bias=s("cu")).then_inc(S("m1"), 1)
                empty_p2(act, i)
            act.wait_ge(S("z2"), 1)
            act.activation(z2q.rearrange("t (k w) -> t k w", w=MW),
                           z2.rearrange("t h v w -> t (h v) w")[:, :, 1:17], ACT.Square,
                           accum_out=s("p_z2")).then_inc(S("p_z2"), 1)
            root(s("r2"), s("rt"))
            root(s("ro"), s("rt"))
            def skip_path(g):
                for n in range(4 * g, 4 * g + 4):
                    last = act.activation(m1[:, n, :], m1[:, n, :], ACT.Identity,
                                          scale=bet[:, n:n + 1], bias=g0[:, n:n + 1])
                last.then_inc(S("bm1"), 1)

            empty(act, "zt2", 0, 8, move_zt(4))
            act.wait_ge(S("g0"), 1)
            for g in range(4):
                skip_path(g)
            act.wait_ge(S("xa"), G4)
            empty(act, "ta2", 0, 8, move_ta(ta2, 0))

            for i in range(G4 + LAG_WX):
                if i % 4 == 1 and 0 <= i // 4 - 1 < XC:
                    c = i // 4 - 1
                    root(ln_r[:, XR * c:XR * c + XR], ln_tmp[:, c % 2, :])
                if 4 <= i < G4:
                    skip_path(i)
                g = i - LAG_LN
                if 0 <= g < G4:
                    act.wait_ge(S("ln2_coef"), g // 4 + 1)
                    for n in range(4 * g + 1, 4 * g + 3):
                        last = act.activation(m1[:, n, :], a0[:, n, :], ACT.Identity,
                                              scale=ln_r[:, n:n + 1], bias=ln_b[:, n:n + 1])
                    last.then_inc(S("ln2_act"), 1)
                g = i - LAG_MV
                if 0 <= g < G4 and g % 2 == 0:
                    if g >= 2:
                        act.wait_ge(S("wx_filled"), g - 1)
                    empty(act, "lnw", g, g + 1, move_lnw)
                g = i - LAG_WX
                if g >= 0:
                    act.wait_ge(S("wx_filled"), g + 1)
                    act.activation(wx[:, 4 * g:4 * g + 4, :].rearrange("d t h -> d (t h)"),
                                   bank(2 + g % 2), ACT.Copy).then_inc(S("wx"), 1)
            root(s("bs"), s("rt"))
            act.wait_ge(S("bn_ab"), 1)
            act.wait_ge(S("bn"), G4)
            for q in range(2):
                act.activation(z_s[:, q, :, :], wx[:, :, STEPS * q:STEPS * q + STEPS].rearrange("d t j -> d j t"),
                               ACT.Identity, scale=s("bs"), bias=s("bb")).then_inc(S("z_act"), 1)

            def sweep(p0, k0, j0):
                if j0:
                    act.wait_ge(S("z_act"), 2)
                    act.wait_ge(S("z_dve"), 2)
                for dj in range(2):
                    for q in range(Q):
                        act.wait_ge(S("z_sum"), 4 * (k0 + dj) + (q + 1))
                        act.activation(y_s[:, q, j0 + dj, :], PS[:, q + 4 * dj, 0:NT], ACT.Sigmoid).then_inc(S("state"), 1)
                with act.Fori(1, (STEPS - j0) // 2) as i:
                    for dj in range(2):
                        for q in range(Q):
                            act.wait_ge(S("z_sum"), i * (2 * Q) + (4 * (k0 + dj) + (q + 1)))
                            act.activation(BIG3[:, bass.ds(i * (2 * NT) + NT * (j0 + dj + STEPS * q), NT)],
                                           PS[:, q + 4 * dj, 0:NT], ACT.Sigmoid).then_inc(S("state"), 1)

            recur(act, sweep)

        @block.vector
        def _(dve):
            seq = [0]

            def link(ins):
                seq[0] += 1
                ins.then_inc(S("dve_seq"), 1)
                dve.wait_ge(S("dve_seq"), seq[0])

            TT, TS, STT = dve.tensor_tensor, dve.tensor_scalar, dve.scalar_tensor_tensor
            roots = [0]

            def inv_root(o, i, eps, times=None):
                roots[0] += 1
                TS(s("rt"), i, eps, None, ALU.add).then_inc(S("root_of"), 1)
                dve.wait_ge(S("root"), roots[0])
                link(dve.reciprocal(o, o))
                if times is not None:
                    link(TT(o, o, times, ALU.mult))

            def ln_rows(c, src, n0, n1):
                for row in range(n0, n1):
                    last = dve.bn_stats(ln_st[:, c % 2, row, :], src[:, XR * c + row, :])
                return last

            def ln_moments(c, src, n0, eps, keep):
                st = ln_st[:, c % 2]
                link(ln_rows(c, src, n0, XR))
                d, m, dd, v = ln_tmp[:, 4, :], ln_tmp[:, 2 + c % 2, :], ln_tmp[:, 5, :], ln_tmp[:, 6, :]
                TT(m, st[:, :, 1], st[:, :, 4], ALU.add)
                TT(v, st[:, :, 2], st[:, :, 5], ALU.add)
                link(TT(d, st[:, :, 1], st[:, :, 4], ALU.subtract))
                TS(v, v, 1.0 / W, None, ALU.mult)
                link(STT(dd, d, 0.25, d, ALU.mult, ALU.mult))
                keep = keep[:, XR * c:XR * c + XR] if keep is not None else d
                link(TT(keep, dd, v, ALU.add))
                TS(ln_tmp[:, c % 2, :], keep, eps, None, ALU.add).then_inc(S("root_of"), 1)

            def ln_coefs(c, done):
                roots[0] += 1
                dve.wait_ge(S("root"), roots[0])
                rs, b = ln_r[:, XR * c:XR * c + XR], ln_b[:, XR * c:XR * c + XR]
                link(dve.reciprocal(rs, rs))
                STT(b, ln_tmp[:, 2 + c % 2, :], -0.5, rs, ALU.mult, ALU.mult).then_inc(S(done), 1)
                dve.wait_ge(S(done), c + 1)

            dve.wait_ge(S("x_in0"), 16)
            ln_moments(0, x_t, 0, LN_C_EPS, row_var)
            for c in range(XC):
                if c + 1 < XC:
                    dve.wait_ge(S(f"x_in{c + 1}"), 16)
                    ln_moments(c + 1, x_t, 0, LN_C_EPS, row_var)
                ln_coefs(c, "ln_coef")
                for row in range(XR * c, XR * c + LN_DVE):
                    last = TS(x_t[:, row, :], x_t[:, row, :], ln_r[:, row:row + 1], ln_b[:, row:row + 1], ALU.mult, ALU.add)
                last.then_inc(S("ln_dve"), 1)
                if c:
                    empty(dve, "col", 4 * c - 4, 4 * c, move_col)
            empty(dve, "col", 4 * XC - 4, 4 * XC, move_col)
            link(TT(vr, row_var, ln_r, ALU.mult))
            link(TT(vr, vr, ln_r, ALU.mult))
            link(dve.tensor_reduce(s("v0"), vr, AX.X, ALU.add))
            link(TS(s("v0"), s("v0"), 1.0 / H, None, ALU.mult))
            dve.wait_ge(S("prm"), 5)
            inv_root(s("s1"), s("v0"), EPS, prm("norm1_g"))
            dve.tensor_copy(s("x0"), s("s1")).then_inc(S("s1"), 1)
            dve.wait_ge(S("gf_filled"), 1)
            dve.tensor_copy(gf, PS[:, 7, 0:NT]).then_inc(S("gf"), 1)
            dve.wait_ge(S("wt"), 1)
            wq, wk = prm("query_skip_w"), prm("key_skip_w")
            TT(wqk, wq, wk, ALU.mult)
            TT(aqk[:, 0, :], aqk[:, 0, :], wq, ALU.add)
            TT(pswv, prm("proj_skip_w"), prm("value_skip_w"), ALU.mult)
            link(TT(aqk[:, 2, :], aqk[:, 2, :], wk, ALU.add))
            for part, (p, q, op) in enumerate((((0, 2), (1, 3), ALU.add), ((0, 3), (1, 2), ALU.subtract))):
                link(TT(mqk[:, part, :], aqk[:, p[0], :], aqk[:, p[1], :], ALU.mult))
                link(TT(mqt, aqk[:, q[0], :], aqk[:, q[1], :], ALU.mult))
                link(TT(mqk[:, part, :], mqk[:, part, :], mqt, op))
            link(TT(mqk[:, 0, :], mqk[:, 0, :], wqk, ALU.subtract))
            link(TS(mqk[:, :, :], mqk[:, :, :], 128.0, None, ALU.mult))
            emptied(dve, "col", 32)
            for k in range(8):
                empty(dve, "p1", 2 * k, 2 * k + 2, move_p1)
                half = slice(64 * (k % 2), 64 * (k % 2) + 64)
                last = dve.tensor_reduce(row_sum[:, k // 2, half], x_w[:, k // 2::4, half].rearrange("w h t -> w t h"),
                                         AX.X, ALU.add)
            link(last)
            TT(edge_x[:, 0, :], row_sum[:, 0, :], row_sum[:, 2, :], ALU.subtract)
            TT(edge_x[:, 1, :], row_sum[:, 1, :], row_sum[:, 3, :], ALU.subtract).then_inc(S("edge_x"), 1)
            empty(dve, "p1", 16, len(P1_N), move_p1)
            dve.wait_ge(S("modes_filled"), 1)
            dve.tensor_copy(t0, modes_ps).then_inc(S("t0"), 1)
            dve.wait_ge(S("ts"), 1)
            tsm = modes(ts)
            for k, lo in enumerate((slice(0, 8), slice(24, 32))):
                last = dve.tensor_copy(xlow[:, :, :, 8 * k:8 * k + 8],
                                       tsm[:, 0:LW, :, lo].rearrange("t w v h -> t v w h"))
            last.then_inc(S("xlow"), 1)
            empty(dve, "rx", 0, 8, move_rx)
            dve.wait_ge(S("edge_t_filled"), 1)
            dve.tensor_copy(edge_t, PS[0:64, 6, 256:384]).then_inc(S("edge_t"), 1)
            dve.wait_ge(S("xlow_filled"), 1)
            dve.tensor_copy(xlow_t.rearrange("m v t -> m (v t)"), PS[:, 4, 0:256]).then_inc(S("m_low"), 1)
            dve.wait_ge(S("m_low"), 1)
            mb = mqk[:, 0, :].unsqueeze(2).to_broadcast([128, NH, NT])
            xb = [xlow_t[:, k, :].unsqueeze(1).to_broadcast([128, NH, NT]) for k in range(2)]
            TT(u_re, mb, xb[0], ALU.mult)
            link(TT(u_im, mb, xb[1], ALU.mult))
            dve.wait_ge(S("g_filled"), 1)
            TS(g_s, PS[:, 7, 0:NT], s("s1"), None, ALU.mult).then_inc(S("g_s"), 1)
            dve.wait_ge(S("u_prod"), 1)
            TT(u_re, u_re, u_p, ALU.subtract)
            dve.wait_ge(S("u_prod"), 2)
            TT(u_im, u_im, u_q, ALU.add).then_inc(S("u"), 1)
            dve.wait_ge(S("g_t_filled"), 1)
            dve.memset(cbd, 0.0)
            for b in range(NB):
                tb = slice(TB * b, TB * b + TB)
                last = TS(g_c[tb, :], PS[tb, 6, 384 + TB * b:384 + TB * b + TB], sc[tb, scn["s1"]:scn["s1"] + 1],
                          None, ALU.mult)
            link(last)
            link(TT(stmp, wqk.unsqueeze(2).to_broadcast([128, NH, TB]),
                    g_c.unsqueeze(1).to_broadcast([128, NH, TB]), ALU.mult))
            dve.wait_ge(S("s_filled"), 1)
            link(TT(scr, stmp, PS[:, 5, :].rearrange("t (n s) -> t n s", s=TB), ALU.add))
            link(dve.tensor_reduce(smax, scr, AX.X, ALU.max))
            TT(scr, scr, smax.unsqueeze(2).to_broadcast([128, NH, TB]), ALU.subtract).then_inc(S("s_shift"), 1)
            dve.wait_ge(S("s_exp"), 1)
            link(dve.tensor_reduce(ssum, prob, AX.X, ALU.add))
            link(dve.reciprocal(ssum, ssum))
            TT(prob, prob, ssum.unsqueeze(2).to_broadcast([128, NH, TB]), ALU.mult).then_inc(S("prob"), 1)
            dve.wait_ge(S("prob"), 1)

            def products(hg):
                if hg >= 2:
                    dve.wait_ge(S("prod_used"), hg - 1)
                for b in range(NB):
                    o = prod(4 * hg + b)
                    TT(o[:, 0], xrep[:, b], wr[:, hg, :, 0:1, :].to_broadcast([128, MW, 2, MH]), ALU.mult)
                    STT(o[:, 1, :, 0, :], xrep[:, b, :, 1, :], -1.0, wr[:, hg, :, 1, :],
                        ALU.mult, ALU.mult).then_inc(S("prod_dve"), 1)

            dve.wait_ge(S("rep"), 16)
            products(0)
            link(TT(stmp, prob, pswv.unsqueeze(2).to_broadcast([128, NH, TB]), ALU.mult))
            link(dve.tensor_reduce(c32, stmp.rearrange("t n s -> t s n"), AX.X, ALU.add))
            for b in range(NB):
                tb = slice(TB * b, TB * b + TB)
                last = dve.tensor_copy(cbd[tb, tb], c32[tb, :])
            last.then_inc(S("cbd"), 1)
            products(1)
            dve.wait_ge(S("c_filled"), 1)
            STT(cft, PS[:, 6, 0:NT], s("s1"), ident, ALU.mult, ALU.add).then_inc(S("cft"), 1)
            dve.wait_ge(S("k1_filled"), 1)
            link(dve.tensor_copy(cf, PS[:, 6, 128:256]))
            link(TT(k1x, PS[:, 6, 256:384], cf, ALU.mult))
            link(dve.tensor_reduce(s("q"), k1x, AX.X, ALU.add))
            products(2)
            products(3)
            dve.wait_ge(S("y_filled"), 1)
            link(dve.tensor_copy(y_m, y_ps))
            dve.wait_ge(S("p_cx"), 1)
            TT(ma, cx_ps, y_m, ALU.add).then_inc(S("ma"), 1)
            dve.wait_ge(S("ma"), 1)
            dve.wait_ge(S("p_ma"), 1)
            TS(s("q"), s("q"), 1.0 / PIX, None, ALU.mult)
            link(TT(s("x0"), s("p_ma"), s("p_cx"), ALU.subtract))
            link(STT(s("va"), s("x0"), 2.0, s("q"), ALU.mult, ALU.add))
            inv_root(s("al"), s("va"), EPS, prm("attn_norm_g"))
            TS(dg, ident, s("al"), None, ALU.mult).then_inc(S("dg"), 1)
            link(TT(s("x0"), s("al"), s("al"), ALU.mult))
            link(TT(s("x0"), s("x0"), s("va"), ALU.mult))
            dve.wait_ge(S("bc_filled"), 1)
            TT(acft, cft, PS[:, 6, 384:512], ALU.mult).then_inc(S("acft"), 1)
            inv_root(s("rm"), s("x0"), EPS, prm("norm2_g"))
            link(TT(s("kappa"), s("rm"), prm("mixer_skip_w1"), ALU.mult))
            TS(dg, ident, s("kappa"), None, ALU.mult).then_inc(S("kap_dg"), 1)
            TT(s("sm"), s("rm"), s("al"), ALU.mult)
            w1 = prm("mixer_w1").rearrange("t (h w v) -> t v w h", v=2, w=17)[:, :, 1:17, :]
            mam, zwm, ztm, ym = modes(ma), modes(zw), modes(ztmp), modes(y_m)
            TT(zwm[:, :, 0, :], mam[:, :, 0, :], w1[:, 0], ALU.mult)
            TT(zwm[:, :, 1, :], mam[:, :, 0, :], w1[:, 1], ALU.mult)
            TT(ztm[:, :, 0, :], mam[:, :, 1, :], w1[:, 1], ALU.mult)
            link(TT(ztm[:, :, 1, :], mam[:, :, 1, :], w1[:, 0], ALU.mult))
            TT(zwm[:, :, 0, :], zwm[:, :, 0, :], ztm[:, :, 0, :], ALU.subtract)
            TT(zwm[:, :, 1, :], zwm[:, :, 1, :], ztm[:, :, 1, :], ALU.add).then_inc(S("zw"), 1)
            dve.wait_ge(S("zw"), 1)
            link(TS(y_m, y_m, s("al"), None, ALU.mult))
            dve.wait_ge(S("kap_filled"), 1)
            dve.tensor_copy(kap, PS[:, 3, 0:NT]).then_inc(S("kap"), 1)
            link(TT(s("x0"), s("sm"), s("sm"), ALU.mult))
            dve.wait_ge(S("p_z1"), 1)
            link(STT(s("x0"), s("p_z1"), 2.0, s("x0"), ALU.mult, ALU.mult))
            inv_root(s("r1"), s("x0"), EPS, prm("mixer_norm_g1"))
            link(TT(s("f1"), s("r1"), s("sm"), ALU.mult))
            link(TS(ztmp, y_m, s("kappa"), None, ALU.mult))
            o = z3_1.rearrange("t w k h -> t w (k h)")[:, :, MH:3 * MH]
            link(STT(o, zw.rearrange("t (w k) -> t w k", w=MW), s("f1"),
                     ztmp.rearrange("t (w k) -> t w k", w=MW), ALU.mult, ALU.add))
            TS(z3_1[:, :, 0, :], z3_1[:, :, 2, :], -1.0, None, ALU.mult).then_inc(S("z3_1"), 1)
            link(TT(s("cu"), prm("mixer_skip_w1"), prm("norm2_b"), ALU.mult))
            link(TT(s("cu"), s("cu"), prm("mixer_norm_b1"), ALU.add))
            link(TT(s("cu"), s("cu"), prm("mixer_skip_b1"), ALU.add))
            dve.wait_ge(S("mix_filled"), 32)
            for g in range(KA_POOL, 32):
                dve.wait_ge(S("a0"), g + 1)
                w = slice(4 * g, 4 * g + 4)
                TT(m1[:, :, w], a0[:, :, w], kap.unsqueeze(2).to_broadcast([128, NT, 4]),
                   ALU.mult).then_inc(S("ka0"), 1)
            empty(dve, "zt1", 0, 8, move_zt(0))
            empty(dve, "ta1", 0, 8, move_ta(ta1, 4))
            dve.wait_ge(S("ka0"), 32)
            for i in range(G4 + LAG_M2):
                if i < G4:
                    dve.wait_ge(S("b1_filled"), i + 1)
                    v = m1[:, 4 * i:4 * i + 4, :].rearrange("h t w -> h (t w)")
                    TT(v, bank(i % 4), v, ALU.add).then_inc(S("u_sum"), 1)
                if 0 <= i - 3 < G4:
                    dve.wait_ge(S("m1"), i - 2)
                    for n in range(4 * (i - 3), 4 * (i - 3) + 4):
                        last = dve.bn_stats(st2[:, n, :], m1[:, n, :])
                empty_p2(dve, i)
            link(last)
            TT(kap, st2[:, :, 1], st2[:, :, 1], ALU.mult)
            TT(bet, st2[:, :, 4], st2[:, :, 4], ALU.mult)
            link(TT(dg, st2[:, :, 2], st2[:, :, 5], ALU.add))
            link(TT(kap, kap, bet, ALU.add))
            STT(dg, kap, float(W // 2), dg, ALU.mult, ALU.add).then_inc(S("rowsq"), 1)
            dve.wait_ge(S("x1_filled"), 1)
            for k, n in enumerate(X1_N):
                last = dve.tensor_copy(x1m[:, 15 * k:15 * k + n].rearrange("t h v w -> t (h v w)"), PS[:, k, 0:34 * n])
            link(last)
            w2 = prm("mixer_w2").rearrange("t (h w v) -> t v h w", v=2, w=17)
            TT(z2[:, :, 0, :], x1m[:, :, 0, :], w2[:, 0], ALU.mult)
            TT(z2[:, :, 1, :], x1m[:, :, 0, :], w2[:, 1], ALU.mult)
            TT(z2t[:, :, 0, :], x1m[:, :, 1, :], w2[:, 1], ALU.mult)
            link(TT(z2t[:, :, 1, :], x1m[:, :, 1, :], w2[:, 0], ALU.mult))
            TT(z2[:, :, 0, :], z2[:, :, 0, :], z2t[:, :, 0, :], ALU.subtract)
            TT(z2[:, :, 1, :], z2[:, :, 1, :], z2t[:, :, 1, :], ALU.add).then_inc(S("z2"), 1)
            dve.wait_ge(S("z2"), 1)
            gg = z2g
            TT(gg[:, 0:15], z2[:, 1:16, 0, 0], z2[:, 31:16:-1, 0, 0], ALU.add)
            TT(gg[:, 15:30], z2[:, 1:16, 1, 0], z2[:, 31:16:-1, 1, 0], ALU.subtract)
            link(dve.tensor_copy(gg[:, 30:32], z2[:, 16, :, 0]))
            link(TT(gg, gg, gg, ALU.mult))
            link(dve.tensor_reduce(s("g2"), gg, AX.X, ALU.add))
            link(TT(z2t.rearrange("t h v w -> t (h v w)"), z2.rearrange("t h v w -> t (h v w)"),
                    x1m.rearrange("t h v w -> t (h v w)"), ALU.mult))
            link(dve.tensor_reduce(s("cov"), z2t.rearrange("t h v w -> t (h v) w")[:, :, 1:17], AX.XY, ALU.add))
            link(dve.tensor_reduce(s("cov0"), z2t[:, 1:32, :, 0], AX.XY, ALU.add))
            link(STT(s("cov"), s("cov"), 2.0, s("cov0"), ALU.mult, ALU.add))
            link(TS(s("g2"), s("g2"), 0.5, None, ALU.mult))
            dve.wait_ge(S("p_z2"), 1)
            link(STT(s("v2"), s("p_z2"), 2.0, s("g2"), ALU.mult, ALU.add))
            inv_root(s("r2"), s("v2"), EPS, prm("mixer_norm_g2"))
            mean1 = s("mean1")
            link(dve.tensor_copy(mean1, x1m[:, 0, 0, 0:1]))
            link(TT(s("m1sq"), mean1, mean1, ALU.mult))
            dve.wait_ge(S("sq_filled"), 1)
            link(STT(s("vm1"), PS[:, 3, 0:1], 1.0 / PIX, s("m1sq"), ALU.mult, ALU.subtract))
            k2 = prm("mixer_skip_w2")
            link(TT(s("x0"), s("r2"), s("v2"), ALU.mult))
            link(TT(s("x1"), k2, s("cov"), ALU.mult))
            link(STT(s("x0"), s("x1"), 2.0, s("x0"), ALU.mult, ALU.add))
            link(TT(s("x0"), s("x0"), s("r2"), ALU.mult))
            link(TT(s("x1"), k2, s("vm1"), ALU.mult))
            link(TT(s("x1"), k2, s("x1"), ALU.mult))
            link(TT(s("x0"), s("x0"), s("x1"), ALU.add))
            inv_root(s("ro"), s("x0"), EPS, prm("mixer_out_g"))
            TT(s("alpha"), s("ro"), s("r2"), ALU.mult)
            link(TT(s("bt"), s("ro"), k2, ALU.mult))
            TS(dg, ident, s("bt"), None, ALU.mult).then_inc(S("dg2"), 1)
            link(TT(s("x1"), s("bt"), mean1, ALU.mult))
            link(TT(s("cb"), prm("mixer_out_b"), prm("attn_norm_b"), ALU.add))
            TS(z0.rearrange("t (v h) -> t v h", v=2)[:, 0, :], z2[:, :, 0, 0], s("alpha"), None, ALU.mult)
            link(TS(z0.rearrange("t (v h) -> t v h", v=2)[:, 1, :], z2[:, :, 1, 0], s("alpha"), None, ALU.mult))
            TT(z0[:, 0:1], s("cb"), s("x1"), ALU.subtract).then_inc(S("z0"), 1)
            for part in range(2):
                last = STT(z3_2[:, :, 1 + part, :], z2[:, :, part, 1:17].rearrange("t h w -> t w h"), s("alpha"),
                           ym[:, :, part, :], ALU.mult, ALU.add)
            link(last)
            TS(z3_2[:, :, 0, :], z3_2[:, :, 2, :], -1.0, None, ALU.mult).then_inc(S("z3_2"), 1)
            dve.wait_ge(S("z0t_filled"), 1)
            dve.tensor_copy(bet, PS[:, 3, 128:256])
            dve.tensor_copy(z0t, PS[0:64, 3, 256:384]).then_inc(S("z0t"), 1)
            dve.wait_ge(S("g0_filled"), 1)
            dve.tensor_copy(g0, PS[:, 3, 384:512]).then_inc(S("g0"), 1)
            empty(dve, "zt2", 0, 8, move_zt(4))
            dve.wait_ge(S("xa"), G4)
            empty(dve, "ta2", 0, 8, move_ta(ta2, 0))

            for i in range(G4 + LAG_BN):
                g = i - 1
                if 0 <= g < G4:
                    v = a0[:, 4 * g:4 * g + 4, :].rearrange("h t w -> h (t w)")
                    dve.wait_ge(S("xm"), g + 1)
                    dve.wait_ge(S("b2_filled"), g + 1)
                    TT(v, v, bank(4 + g % 4), ALU.add).then_inc(S("x1"), 1)
                    dve.wait_ge(S("x1"), g + 1)
                    if g % 4 == 3:
                        ln_moments(g // 4, a0, 12, EPS, None)
                    else:
                        ln_rows(g // 4, a0, 4 * (g % 4), 4 * (g % 4) + 4)
                g = i - LAG_LN
                if 0 <= g < G4:
                    TS(m1[:, 4 * g, :], a0[:, 4 * g, :], ln_r[:, 4 * g:4 * g + 1], ln_b[:, 4 * g:4 * g + 1],
                       ALU.mult, ALU.add).then_inc(S("ln2_dve"), 1)
                g = i - LAG_MV
                if 0 <= g < G4 and g % 2 == 1:
                    if g >= 2:
                        dve.wait_ge(S("wx_filled"), g - 1)
                    empty(dve, "lnw", g, g + 1, move_lnw)
                g = i - LAG_BN
                if g >= 0:
                    dve.wait_ge(S("wx"), g + 1)
                    dve.bn_stats(bn_st[:, g, :],
                                 wx[:, 4 * g:4 * g + 4, :].rearrange("d t h -> d (t h)")).then_inc(S("bn"), 1)
                if i % 4 == 1 and 0 <= i // 4 - 1 < XC:
                    ln_coefs(i // 4 - 1, "ln2_coef")
            dve.wait_ge(S("bn"), G4)
            link(dve.bn_aggr(sc[:, 60:62], bn_st.rearrange("d g c -> d (g c)")))
            inv_root(s("bs"), sc[:, 61:62], EPS, s("gamma"))
            link(TT(s("x0"), sc[:, 60:61], s("bs"), ALU.mult))
            TT(s("bb"), s("beta"), s("x0"), ALU.subtract).then_inc(S("bn_ab"), 1)
            dve.wait_ge(S("bn_ab"), 1)
            dve.wait_ge(S("wx"), G4)
            for q in range(2, 4):
                TS(z_s[:, q, :, :], wx[:, :, STEPS * q:STEPS * q + STEPS].rearrange("d t j -> d j t"),
                   s("bs"), s("bb"), ALU.mult, ALU.add).then_inc(S("z_dve"), 1)

            def shifted(o, last):
                dve.tensor_copy(o[:, 1:Q, :], last[:, 0:Q - 1, :])
                link(dve.tensor_copy(o[:, 0, 1:NT], last[:, Q - 1, 0:NT - 1]))
                link(dve.memset(o[:, 0, 0:NT:TB], 0.0))

            def sweep(p0, k0, j0):
                if j0:
                    dve.wait_ge(S("z_act"), 2)
                    dve.wait_ge(S("z_dve"), 2)
                    dve.memset(y_s[:, :, j0 - 1, :], 0.0).then_inc(S("state"), Q)
                for dj in range(2):
                    for q in range(Q):
                        b = PS[:, q + 4 * dj, 0:NT]
                        dve.wait_ge(S("vy"), 4 * (k0 + dj) + (q + 1))
                        TT(b, b, z_s[:, q, j0 + dj, :], ALU.add).then_inc(S("z_sum"), 1)
                with dve.Fori(1, (STEPS - j0) // 2) as i:
                    for dj in range(2):
                        for q in range(Q):
                            b = PS[:, q + 4 * dj, 0:NT]
                            dve.wait_ge(S("vy"), i * (2 * Q) + (4 * (k0 + dj) + (q + 1)))
                            TT(b, b, BIG1[:, bass.ds(i * (2 * NT) + NT * (j0 + dj + STEPS * q), NT)],
                               ALU.add).then_inc(S("z_sum"), 1)

            def starts(p):
                dve.wait_ge(S("state"), Q * p)
                shifted(start_a, y_s[:, :, STEPS - 1, :])
                dve.tensor_copy(y_s[:, :, STEPS - 1, :], start_a).then_inc(S("state"), Q)

            def judge(p):
                dve.wait_ge(S("state"), Q * p)
                shifted(start_b, y_s[:, :, STEPS - 1, :])
                link(TT(start_b, start_b, start_a, ALU.subtract))
                link(TT(start_b, start_b, start_b, ALU.mult))
                dve.tensor_reduce(s("gap"), start_b, AX.XY, ALU.max).then_inc(S("gap"), 1)
                dve.wait_ge(S("gap_filled"), 1)
                link(dve.tensor_reduce(sc[0:1, 63:64], PS[0:1, 0, 0:NT], AX.X, ALU.max))
                link(TS(sc[0:1, 63:64], sc[0:1, 63:64], TOL * TOL, None, ALU.is_le))
                TS(FLAG[0:1, 0:1], sc[0:1, 63:64], -1.0, 1.0, ALU.mult, ALU.add).then_inc(S("judged"), 1)

            recur(dve, sweep, starts, judge)
            for g in range(G4):
                dve.wait_ge(S("yt_filled"), g + 1)
                v = a0[:, 4 * g:4 * g + 4, :].rearrange("h t w -> h (t w)")
                TT(v, v, bank(g % 8), ALU.add).then_inc(S("result"), 1)


_NAMES = ["x", "L0_conv_key_w", "L0_conv_key_skip_w", "L0_conv_query_w", "L0_conv_query_skip_w",
          "L0_conv_value_w", "L0_conv_value_skip_w", "L0_conv_proj_w", "L0_conv_proj_skip_w",
          "L0_conv_norm1_g", "L0_conv_attn_norm_g", "L0_conv_attn_norm_b", "L0_conv_norm2_g",
          "L0_conv_norm2_b", "L0_conv_mixer_w1", "L0_conv_mixer_skip_w1", "L0_conv_mixer_skip_b1",
          "L0_conv_mixer_norm_g1", "L0_conv_mixer_norm_b1", "L0_conv_mixer_w2",
          "L0_conv_mixer_skip_w2", "L0_conv_mixer_norm_g2", "L0_conv_mixer_out_g",
          "L0_conv_mixer_out_b", "L0_ffn_W", "L0_ffn_V", "L0_ffn_gamma", "L0_ffn_beta"]


def kernel(**inputs):
    import concourse.bacc as bacc
    from concourse.bass_utils import run_bass_kernel_spmd as run

    nc = bacc.Bacc("TRN2", target_bir_lowering=False, num_devices=1)
    arrays, tensors = {}, {}
    for name in _NAMES + ["const"]:
        a = np.ascontiguousarray(CONST if name == "const" else inputs[name])
        arrays[f"in_{name}"] = a
        tensors[name.replace("L0_conv_", "").replace("L0_ffn_", "")] = nc.dram_tensor(
            f"in_{name}", a.shape, mybir.dt.from_np(a.dtype), kind="ExternalInput").ap()
    out = nc.dram_tensor("out_x", inputs["x"].shape, F32, kind="ExternalOutput").ap()
    metaformer(nc, tensors, out)
    r = run(nc, [arrays], core_ids=[0])
    return r.results[0]["out_x"]
```

```python
from contextlib import ExitStack

import numpy as np
import concourse.bass as bass
from concourse import mybir

F32 = mybir.dt.float32
I32 = mybir.dt.int32
ALU = mybir.AluOpType
ACT = mybir.ActivationFunctionType
AX = mybir.AxisListType

NT, H, W = 128, 128, 128
NB, TB = 4, 32
NH, HG = 16, 4
MH, MW = 32, 16
MODES = MW * 2 * MH
LH, LW = 16, 8
NF = 65
PIX = H * W
LN_C_EPS, EPS = 1e-6, 1e-5
XC = 8
XR = H // XC
LN_DVE, LN_POOL = 4, 6
G4 = NT // 4
P2_T = 12
LN2_ACT = (4, 3)
LAG_P2, LAG_M2 = 5, 7
LAG_LN, LAG_TR, LAG_MV, LAG_W, LAG_WX, LAG_BN = 6, 7, 8, 9, 10, 12
STEPS, BURN = 16, 10
Q = H // STEPS
CHUNKS = TB * Q
GR = NB
TOL = 1e-5

FUNCS = [("c", 0), ("c", 32)] + [("c", k) for k in range(1, 32)] + [("s", k) for k in range(1, 33)]
COS = {k: i for i, (f, k) in enumerate(FUNCS) if f == "c"}
SIN = {k: i for i, (f, k) in enumerate(FUNCS) if f == "s"}

SCALARS = ["norm1_g", "attn_norm_g", "attn_norm_b", "norm2_g", "norm2_b", "mixer_norm_g1",
           "mixer_norm_b1", "mixer_norm_g2", "mixer_out_g", "mixer_out_b", "mixer_skip_w1",
           "mixer_skip_b1", "mixer_skip_w2"]
ROW_AT = {n: (i, 1) for i, n in enumerate(SCALARS)}
for _i, _n in enumerate(["query_skip_w", "key_skip_w", "value_skip_w", "proj_skip_w"]):
    ROW_AT[_n] = (len(SCALARS) + NH * _i, NH)
ROW_W = len(SCALARS) + 4 * NH
ROW_AT["mixer_w1"] = (ROW_W, MH * 17 * 2)
ROW_AT["mixer_w2"] = (ROW_W + MH * 17 * 2, MH * 17 * 2)
ROW_N = ROW_W + 2 * MH * 17 * 2


def constants():
    n = np.arange(128)

    def func(f, k):
        a = 2 * np.pi * n * k / 128
        return np.cos(a) if f == "c" else np.sin(a)

    half = np.array([2 ** -0.5 if f == "c" and k in (0, 32) else 1 for f, k in FUNCS])
    basis = np.stack([func(f, k) for f, k in FUNCS], 1) / 128 * half
    g = np.zeros((128, 64))
    for k in range(32):
        g[:, k] = func("c", k) * (1 if k == 0 else 2 ** 0.5)
    for k in range(1, 32):
        g[:, 31 + k] = func("s", k) * 2 ** 0.5
    g = g * 8 / 128
    gram = g * 2 ** 0.5
    edge = np.zeros((128, 2, 64))
    for i, (f, k) in enumerate(FUNCS[:64]):
        edge[:, 0, i] = func(f, k) * half[i]
        edge[:, 1, i] = {"c": 1, "s": -1}[f] * func("s" if f == "c" else "c", k) * half[i]
    edge = edge.reshape(128, 128) / 128 * (8 / 128 * 2 ** 0.5)
    h = np.concatenate([np.arange(16), np.arange(-16, 0)])
    ah = 2 * np.pi * np.outer(n, h) / 128
    ch, sh = np.cos(ah), np.sin(ah)
    row_modes = np.concatenate([ch, -sh, -sh, -ch], 1) / 128
    aw = 2 * np.pi * np.outer(n, np.arange(17)) / 128
    cw, sw = np.cos(aw), np.sin(aw)
    col_modes = np.concatenate([cw, -sw, -sw, -cw, sw, cw], 1) / 128
    basis17 = np.concatenate([cw, sw[:, 1:]], 1) / 128
    fr = np.zeros((128, 128))
    fr[:64] = np.concatenate([ch.T, -sh.T], 0)
    block = np.zeros((128, 512))
    for j in range(4):
        block[32 * j:32 * j + 16, 128 * j:128 * j + 128] = 2 * cw.T[1:17]
        block[32 * j + 16:32 * j + 32, 128 * j:128 * j + 128] = 2 * sw.T[1:17]
    at, out, x = {}, [], 0
    for name, p in (("ident", np.eye(128)), ("basis", basis), ("gram", gram), ("edge", edge),
                    ("row_modes", row_modes), ("col_modes", col_modes), ("basis17", basis17),
                    ("fr", fr), ("block", block), ("ones", np.ones((128, 128)))):
        at[name] = (x, p.shape[1])
        out.append(p)
        x += p.shape[1]
    return np.concatenate(out, 1).astype(np.float32), at


CONST, CONST_AT = constants()


def metaformer(nc, t, out):
    x_tok = t["x"].rearrange("b s h w -> (b s) h w")
    x_row = t["x"].rearrange("b s h w -> h (b s) w")
    out_row = out.rearrange("b s h w -> h (b s) w")
    ctx = ExitStack()
    with ctx:
        def sb(name, shape, dt=F32):
            return ctx.enter_context(nc.sbuf_tensor(name, shape, dt))

        def sem(name):
            return ctx.enter_context(nc.semaphore(name))

        PS = ctx.enter_context(nc.psum_tensor("PS", [128, 8, 512], F32))
        CST = sb("CST", [128, CONST.shape[1]])

        def const(name):
            a, n = CONST_AT[name]
            return CST[:, a:a + n]

        ident, basis, gram_fn, edge_fn = const("ident"), const("basis"), const("gram"), const("edge")
        row_modes, col_modes, basis17 = const("row_modes"), const("col_modes"), const("basis17")
        fr, block_w, ones = const("fr"), const("block"), const("ones")

        BIG1 = sb("BIG1", [128, PIX])
        BIG2 = sb("BIG2", [128, PIX])
        BIG3 = sb("BIG3", [128, PIX])
        SML = sb("SML", [128, 2624])
        FLAG = sb("FLAG", [1, 1], I32)

        def flat(a):
            n = 1
            for k in a.shape:
                n *= k
            names = "abcde"[:len(a.shape)]
            v = a.rearrange(" ".join(names) + " -> (" + " ".join(names) + ")") if len(names) > 1 else a
            return v.unsqueeze(0)

        x_t = BIG1[:, :].rearrange("t (h w) -> t h w", w=W)
        m1 = BIG1[:, :].rearrange("h (t w) -> h t w", w=W)
        y_s = BIG1[:, :].rearrange("d (q j t) -> d q j t", q=Q, t=NT)
        x_w = BIG2[:, :].rearrange("w (h t) -> w h t", t=NT)
        a0 = BIG2[:, :].rearrange("h (t w) -> h t w", w=W)
        rx = BIG2[:, 0:4096].rearrange("f (j t) -> f j t", t=NT)
        u_re = BIG2[:, 4096:6144].rearrange("m (n t) -> m n t", t=NT)
        u_im = BIG2[:, 6144:8192].rearrange("m (n t) -> m n t", t=NT)
        u_p = BIG2[:, 8192:10240].rearrange("m (n t) -> m n t", t=NT)
        u_q = BIG2[:, 10240:12288].rearrange("m (n t) -> m n t", t=NT)
        wr = BIG2[:, 12288:16384].rearrange("p (g w v h) -> p g w v h", g=4, v=2, h=MH)

        row_var = BIG3[:, 2816:2944]
        vr = BIG3[:, 2944:3072]
        p1 = BIG3[:, 0:NF * NT].rearrange("h (f t) -> h f t", t=NT)
        wcp = BIG3[0:NH, 8320:8320 + 1088 + 3 * 288 + 2]
        w_proj = wcp[:, 0:1088].rearrange("n (h w v) -> n h w v", h=MH, v=2)
        w_val = wcp[:, 1088:1376].rearrange("n (h w v) -> n h w v", h=LH, v=2)
        w_key = wcp[:, 1376:1664].rearrange("n (h w v) -> n h w v", h=LH, v=2)
        w_qry = wcp[:, 1664:1952].rearrange("n (h w v) -> n h w v", h=LH, v=2)
        wy = BIG3[0:NH, 10276:11300].rearrange("n (w v h) -> n w v h", v=2, h=MH)
        wtmp = BIG3[0:NH, 11300:11812].rearrange("n (w h) -> n w h", h=MH)
        aqk = BIG3[:, 12352:12416].rearrange("m (k n) -> m k n", n=NH)
        mqk = BIG3[:, 12320:12352].rearrange("m (k n) -> m k n", n=NH)
        wqk = BIG3[:, 12288:12304]
        qk_c = BIG3[0:NH, 7600:8112].rearrange("n (k w h) -> n k w h", k=4, h=LH)
        mqt = BIG3[:, 11940:11956]
        xlow = BIG3[:, 11300:11556].rearrange("t (v w h) -> t v w h", v=2, w=LW)
        xlow_t = BIG3[:, 11556:11812].rearrange("m (v t) -> m v t", v=2)
        edge_t = BIG3[0:64, 11812:11940]
        pswv = BIG3[:, 12304:12320]
        PRM = BIG3[:, 12544:12544 + ROW_N]
        gf = BIG3[:, 12416:12544]
        row_sum = BIG3[:, 14800:15312].rearrange("w (k t) -> w k t", t=NT)
        edge_x = BIG3[:, 11956:12212].rearrange("w (k t) -> w k t", t=NT)
        t0 = BIG3[:, 14800:15824]
        prob_t = BIG3[:, 15824:16336].rearrange("p (g t) -> p g t", g=4)
        scr = BIG3[:, 0:512].rearrange("t (n s) -> t n s", s=TB)
        prob = BIG3[:, 512:1024].rearrange("t (n s) -> t n s", s=TB)
        stmp = BIG3[:, 1024:1536].rearrange("t (n s) -> t n s", s=TB)
        g_s = BIG3[:, 1536:1664]
        cbd = BIG3[:, 1664:1792]
        cf = BIG3[:, 1792:1920]
        k1x = BIG3[:, 1920:2048]
        c32 = BIG3[:, 2048:2080]
        g_c = BIG3[:, 2080:2112]
        smax = BIG3[:, 2112:2128]
        ssum = BIG3[:, 2128:2144]
        cx = BIG3[:, 2144:3168]
        sq_dump = BIG3[:, 0:1024]
        xrep = BIG3[:, 4096:8192].rearrange("p (b w v h) -> p b w v h", b=4, v=2, h=MH)

        def prod(n):
            hg, b = n // 4, n % 4
            v = BIG2[:, 4096 + 2048 * b:6144 + 2048 * b] if hg % 2 else (
                BIG2[:, 2048 * b:2048 * b + 2048] if b < 2 else BIG3[:, 4096 + 2048 * b:6144 + 2048 * b])
            return v.rearrange("p (a w v h) -> p a w v h", a=2, v=2, h=MH)

        zt = BIG3[0:64, 0:4096].rearrange("k (t p) -> k t p", p=32)
        ta1 = BIG3[:, 4096:8192].rearrange("k (g n) -> k g n", n=H)
        y_m = BIG3[:, 8192:9216]
        ma = BIG3[:, 9216:10240]
        zw = BIG3[:, 10240:11264]
        ztmp = BIG3[:, 11264:12288]
        stage = BIG3[:, 14800:16336].rearrange("h (k t w) -> h k t w", k=3, w=W)
        p2 = BIG3[:, 0:33 * NT].rearrange("w (f t) -> w f t", t=NT)
        x1m = BIG3[:, 4352:5440].rearrange("t (h v w) -> t h v w", v=2, w=17)
        z2 = BIG3[:, 5440:6528].rearrange("t (h v w) -> t h v w", v=2, w=17)
        z2q = BIG3[:, 0:1024]
        z2g = BIG3[:, 1024:1056]
        z2t = BIG3[:, 6528:7616].rearrange("t (h v w) -> t h v w", v=2, w=17)
        ta2 = BIG3[:, 12288:16384].rearrange("k (g n) -> k g n", n=H)
        st2 = BIG3[:, 10240:10240 + NT * 6].rearrange("h (t k) -> h t k", k=6)
        wx_step = BIG3[:, :].rearrange("d (b q j t) -> d b q j t", b=NB, q=Q, t=TB)

        def wx(g):
            v = BIG3[:, :].rearrange("d (b h t) -> d b h t", b=NB, t=TB)
            return v[:, 4 * g // TB, :, 4 * g % TB:4 * g % TB + 4]

        ts = SML[:, 0:1024]
        ln_w = SML[:, 0:1024].rearrange("w (k n) -> w k n", k=2)
        start_a = SML[:, 0:1024].rearrange("d (q t) -> d q t", q=Q)
        start_b = SML[:, 1600:2624].rearrange("d (q t) -> d q t", q=Q)
        cft = SML[:, 1024:1152]
        acft = SML[:, 1152:1280]
        ln_r = SML[:, 1024:1152]
        ln_b = SML[:, 1152:1280]
        w_t = SML[:, 1280:1408]
        v_t = SML[:, 1408:1536]
        sc = SML[:, 1536:1600]
        kap = SML[:, 1600:1728]
        bet = SML[:, 1728:1856]
        g0 = SML[:, 1856:1984]
        dg = SML[:, 1984:2112]
        z0 = SML[:, 2112:2176]
        z0t = SML[0:64, 2176:2304]
        ln_st = SML[:, 2304:2496].rearrange("p (k v c) -> p k v c", k=2, c=6)
        ln_tmp = SML[:, 2496:2624].rearrange("p (k v) -> p k v", v=16)
        bn_st = SML[:, 1984:2176].rearrange("p (g c) -> p g c", c=6)
        scn = {}

        def s(name):
            if name not in scn:
                scn[name] = len(scn)
                assert len(scn) <= 54
            return sc[:, scn[name]:scn[name] + 1]

        def prm(name):
            a, n = ROW_AT[name]
            return PRM[:, a:a + n]

        def modes(a):
            return a.rearrange("t (w v h) -> t w v h", v=2, h=MH)

        z3_1 = BIG3[:, 4096:5632].rearrange("t (w k h) -> t w k h", k=3, h=MH)
        z3_2 = BIG3[:, 9216:10752].rearrange("t (w k h) -> t w k h", k=3, h=MH)

        wy_rows = nc.dram_tensor("wy_rows", [NH, MODES], F32).ap()
        sems = {}

        def S(name):
            if name not in sems:
                sems[name] = sem(name)
            return sems[name]

        def bank(k):
            return PS[:, k, :]

        cx_ps = PS[:, 0:2, :].rearrange("t a n -> t (a n)")
        y_ps = PS[:, 2:4, :].rearrange("t a n -> t (a n)")
        modes_ps = PS[:, 4:6, :].rearrange("t a n -> t (a n)")

        LN2_DVE = np.cumsum([LN2_ACT[g % 2] < 4 for g in range(G4)]).tolist()
        P1_N = [min(7, NT - 7 * g) for g in range((NT + 6) // 7)]
        P2_N = [min(P2_T, NT - P2_T * g) for g in range((NT + P2_T - 1) // P2_T)]
        X1_AT = {k: ((k - 1) // 7, 68 * ((k - 1) % 7)) for k in range(1, 16)} | {0: (2, 68), 16: (2, 102)}

        def emptied(e, name, n):
            if (n + 1) // 2:
                e.wait_ge(S(name + "_act"), (n + 1) // 2)
            if n // 2:
                e.wait_ge(S(name + "_dve"), n // 2)

        def empty(e, name, n0, n1, move):
            act = e is scalar_engine
            for n in range(n0, n1):
                if (n % 2 == 0) == act:
                    e.wait_ge(S(name + "_filled"), n + 1)
                    move(e, n).then_inc(S(name + ("_act" if act else "_dve")), 1)

        def copy(e, o, i):
            return e.activation(o, i, ACT.Copy) if e is scalar_engine else e.tensor_copy(o, i)

        def move_col(e, n):
            return copy(e, x_w[:, 4 * n:4 * n + 4, :].rearrange("w h t -> w (h t)"), bank(n % 4))

        def move_p1(e, n):
            k = P1_N[n]
            return copy(e, p1[:, :, 7 * n:7 * n + k],
                        PS[:, n % 4, 0:NF * k].rearrange("h (t f) -> h f t", f=NF))

        def move_rx(e, n):
            return copy(e, rx[:, 4 * n:4 * n + 4, :].rearrange("f j t -> f (j t)"), bank(n % 4))

        def move_zt(base):
            return lambda e, n: copy(e, zt[:, :, 4 * n:4 * n + 4],
                                     PS[0:64, base + n % 4, :].rearrange("k (p t) -> k t p", p=4))

        def move_ta(ta, base):
            return lambda e, n: copy(e, ta[:, 4 * n:4 * n + 4, :].rearrange("k g n -> k (g n)"),
                                     bank(base + n % 4))

        def move_p2(e, n):
            k = P2_N[n]
            return copy(e, p2[:, :, P2_T * n:P2_T * n + k],
                        PS[:, 6 + n % 2, 0:33 * k].rearrange("w (t f) -> w f t", f=33))

        def move_lnw(e, n):
            return copy(e, ln_w[:, n % 2].rearrange("w (h t) -> w t h", t=4),
                        bank(n % 2).rearrange("w (t h) -> w t h", t=4))

        def at(states, g, j):
            return states[:, :, bass.ds(j, 1), TB * g:TB * g + TB]

        def start(g):
            return start_a[:, :, TB * g:TB * g + TB].unsqueeze(2)

        def sums(g, dj):
            return PS[:, g + GR * dj, 0:Q * TB].rearrange("d (q j t) -> d q j t", q=Q, t=TB)

        def recur(e, sweep, starts=None, judge=None):
            sweep(0, 0, STEPS - BURN)
            if starts:
                starts(BURN)
            sweep(1, BURN, 0)
            rounds = BURN + STEPS
            if judge:
                judge(rounds)
            e.wait_ge(S("judged"), 1)
            again = e.value_load(FLAG[0:1, 0:1], min_val=0, max_val=1)
            with e.If(again > 0):
                with e.Fori(0, CHUNKS - 1) as i:
                    if starts:
                        starts(i * STEPS + rounds)
                    sweep(i + 2, i * STEPS + rounds, 0)
                e.wait_ge(S("state"), GR * (rounds + STEPS * (CHUNKS - 1)))
            e.wait_ge(S("state"), GR * rounds)

        scalar_engine = nc.scalar
        small = ctx.enter_context(nc.allow_non_contiguous_dma("weights' columns"))
        block = ctx.enter_context(nc.Block())

        @block.sync
        def _(sp):
            sp.dma_start(ident, t["const"][:, 0:128]).then_inc(S("ident_in"), 16)
            for c in range(XC):
                rows = slice(XR * c, XR * c + XR)
                sp.dma_start(x_t[:, rows, :], x_tok[:, rows, :]).then_inc(S(f"x_in{c}"), 16)
            sp.dma_start(CST[:, 128:], t["const"][:, 128:]).then_inc(S("const_in"), 16)
            for name, (a, n) in ROW_AT.items():
                sp.dma_start(PRM[:, a:a + n], flat(t[name]).to_broadcast([128, n])).then_inc(S("prm"), 16)
            sp.dma_start(wcp[:, 0:1088], t["proj_w"].rearrange("n o h w v -> n (o h w v)")).then_inc(S("w_in"), 16)
            for name, a in (("value_w", 1088), ("key_w", 1376), ("query_w", 1664)):
                sp.dma_start(wcp[:, a:a + 288], t[name].rearrange("o n h w v -> n (o h w v)")).then_inc(S("w_in"), 16)
            sp.dma_start(wcp[:, 1952:1953], t["value_skip_w"].rearrange("o n -> n o")).then_inc(S("w_in"), 16)
            sp.dma_start(wcp[:, 1953:1954], t["proj_skip_w"]).then_inc(S("w_in"), 16)
            sp.dma_start(w_t, t["W"]).then_inc(S("w_in"), 16)
            sp.dma_start(v_t, t["V"]).then_inc(S("w_in"), 16)
            sp.dma_start(s("gamma"), t["gamma"].unsqueeze(1)).then_inc(S("w_in"), 16)
            sp.dma_start(s("beta"), t["beta"].unsqueeze(1)).then_inc(S("w_in"), 16)
            sp.wait_ge(S("wy"), 4)
            sp.dma_start(wy_rows, wy.rearrange("n w v h -> n (w v h)")).then_inc(S("wy_out"), 16)
            sp.wait_ge(S("wy_out"), 16)
            sp.wait_ge(S("p1_filled"), len(P1_N))
            sp.wait_ge(S("edge_x"), 1)
            for hg in range(NH // HG):
                for n in range(HG):
                    sp.dma_start(wr[TB * n:TB * n + TB, hg].rearrange("s w v h -> s (w v h)"),
                                 wy_rows[HG * hg + n:HG * hg + n + 1, :].to_broadcast([TB, MODES])).then_inc(S("rep"), 16)
            sp.wait_ge(S("ts"), 1)
            sp.wait_ge(S("rx_filled"), 8)
            for b in range(NB):
                for n in range(HG):
                    sp.dma_start(xrep[TB * n:TB * n + TB, b].rearrange("s w v h -> s (w v h)"),
                                 ts[TB * b:TB * b + TB, :]).then_inc(S("rep"), 16)
            sp.wait_ge(S("y_filled"), 1)
            for g in range(G4):
                if g >= 3:
                    sp.wait_ge(S("xa"), g - 2)
                sp.dma_start(stage[:, g % 3, :, :],
                             x_row[:, 4 * g:4 * g + 4, :]).then_inc(S(f"stage_in{g % 3}"), 16)
            for g in range(G4):
                sp.wait_ge(S("result"), g + 1)
                sp.dma_start(out_row[:, 4 * g:4 * g + 4, :],
                             a0[:, 4 * g:4 * g + 4, :]).then_inc(S("stored"), 16)
            sp.wait_ge(S("stored"), 16 * G4)

        SMALL_IN = 10

        @block.gpsimd
        def _(pool):
            seq = [0]

            def link(ins):
                seq[0] += 1
                ins.then_inc(S("pool_seq"), 1)
                pool.wait_ge(S("pool_seq"), seq[0])

            for c in range(XC):
                pool.wait_ge(S("ln_coef"), c + 1)
                for row in range(XR * c + LN_DVE, XR * c + LN_DVE + LN_POOL):
                    last = pool.tensor_scalar(x_t[:, row, :], x_t[:, row, :], ln_r[:, row:row + 1],
                                              ln_b[:, row:row + 1], ALU.mult, ALU.add)
                last.then_inc(S("ln_pool"), 1)
            pool.wait_ge(S("w_in"), 16 * SMALL_IN)
            wv, ps = wcp[:, 1952:1953], wcp[:, 1953:1954]
            lows = [slice(0, 8), slice(24, 32)]
            for k, (wt, part) in enumerate(((w_qry, 0), (w_qry, 1), (w_key, 0), (w_key, 1))):
                last = pool.tensor_copy(qk_c[:, k, :, :], wt[:, :, 1:9, part].rearrange("n h w -> n w h"))
            last.then_inc(S("qk_c"), 1)

            def b(part, lo=None, w=MW):
                v = w_proj[:, :, 1:1 + w, part] if lo is None else w_proj[:, lo, 1:1 + w, part]
                return v.rearrange("n h w -> n w h")

            def a(part, k):
                return w_val[:, 8 * k:8 * k + 8, 1:9, part].rearrange("n h w -> n w h")

            for part in range(2):
                link(pool.tensor_scalar(wy[:, :, part, :], b(part), wv, None, ALU.mult))
            for k, lo in enumerate(lows):
                tk = wtmp[:, 0:LW, 8 * k:8 * k + 8]
                for part, (p, q, op) in ((0, (0, 0, ALU.add)), (0, (1, 1, ALU.subtract)),
                                      (1, (0, 1, ALU.add)), (1, (1, 0, ALU.add))):
                    o = wy[:, 0:LW, part, lo]
                    link(pool.tensor_tensor(tk, b(p, lo, LW), a(q, k), ALU.mult))
                    link(pool.tensor_tensor(o, o, tk, op))
                for part in range(2):
                    o = wy[:, 0:LW, part, lo]
                    link(pool.tensor_scalar(tk, a(part, k), ps, None, ALU.mult))
                    pool.tensor_tensor(o, o, tk, ALU.add).then_inc(S("wy"), 1)
                    pool.wait_ge(S("wy"), 2 * k + part + 1)
            pool.wait_ge(S("m_low"), 1)
            mb = mqk[:, 1, :].unsqueeze(2).to_broadcast([128, NH, NT])
            xb = [xlow_t[:, k, :].unsqueeze(1).to_broadcast([128, NH, NT]) for k in range(2)]
            pool.tensor_tensor(u_p, mb, xb[1], ALU.mult).then_inc(S("u_prod"), 1)
            pool.tensor_tensor(u_q, mb, xb[0], ALU.mult).then_inc(S("u_prod"), 1)

            for hg in range(NH // HG):
                if hg == 0:
                    pool.wait_ge(S("rep"), 16 * 32)
                    pool.wait_ge(S("g_filled"), 1)
                    pool.wait_ge(S("s_filled"), 1)
                if hg >= 2:
                    pool.wait_ge(S("prod_used"), hg - 1)
                pool.tensor_tensor(prod(4 * hg + 3)[:, 0, :, 1, :], xrep[:, 3, :, 1, :], wr[:, hg, :, 0, :],
                                   ALU.mult).then_inc(S("prod_pool"), 1)
                for b in range(NB):
                    pool.tensor_tensor(prod(4 * hg + b)[:, 1, :, 1, :], xrep[:, b, :, 0, :], wr[:, hg, :, 1, :],
                                       ALU.mult).then_inc(S("prod_pool"), 1)

            pool.wait_ge(S("kap"), 1)
            pool.wait_ge(S("a0"), 32)
            pool.wait_ge(S("mix_filled"), 32)
            for g in range(G4):
                v = slice(4 * g, 4 * g + 4)
                pool.tensor_tensor(m1[:, v, :], a0[:, v, :], kap[:, v].unsqueeze(2).to_broadcast([128, 4, W]),
                                   ALU.mult).then_inc(S("ka0"), 1)
            pool.wait_ge(S("ka0"), 32)
            for g in range(G4):
                pool.wait_ge(S(f"stage_in{g % 3}"), 16 * (g // 3 + 1))
                v = a0[:, 4 * g:4 * g + 4, :]
                pool.tensor_tensor(v, v, stage[:, g % 3, :, :], ALU.add).then_inc(S("xa"), 1)
            pool.wait_ge(S("xa"), G4)
            pool.wait_ge(S("bet"), 1)
            for i in range(G4 + 1):
                if i < G4:
                    v = slice(4 * i, 4 * i + 4)
                    pool.tensor_tensor(m1[:, v, :], m1[:, v, :], bet[:, v].unsqueeze(2).to_broadcast([128, 4, W]),
                                       ALU.mult).then_inc(S("bm1"), 1)
                if i:
                    v = slice(4 * i - 4, 4 * i)
                    pool.wait_ge(S("bm1"), i)
                    pool.tensor_tensor(a0[:, v, :], a0[:, v, :], m1[:, v, :], ALU.add).then_inc(S("xm"), 1)
            pool.wait_ge(S("g0"), 1)
            pool.wait_ge(S("ln2_act"), G4)
            pool.wait_ge(S("ln2_dve"), LN2_DVE[-1])
            for g in range(G4):
                v = slice(4 * g, 4 * g + 4)
                pool.tensor_tensor(a0[:, v, :], a0[:, v, :], g0[:, v].unsqueeze(2).to_broadcast([128, 4, W]),
                                   ALU.add).then_inc(S("x1_g0"), 1)

        @block.tensor
        def _(pe):
            def mm(o, l, rhs, start=True, stop=True, **k):
                return pe.matmul(o, l, rhs, start=start, stop=stop, **k)

            def tr(o, i):
                n = i.partition_size() if callable(i.partition_size) else i.partition_size
                return pe.matmul(o, i, ident[0:n, 0:n], is_transpose=True, start=True, stop=True)

            def gram(n):
                emptied(pe, "col", n + 1)
                for h in range(4 * n, 4 * n + 4):
                    last = mm(PS[:, 7, 0:128], x_w[:, h, :], x_w[:, h, :], h == 0, h == H - 1)
                return last

            pe.wait_ge(S("ident_in"), 16)
            for c in range(XC):
                pe.wait_ge(S("ln_act"), c + 1)
                pe.wait_ge(S("ln_dve"), c + 1)
                pe.wait_ge(S("ln_pool"), c + 1)
                for n in range(4 * c, 4 * c + 4):
                    if n >= 4:
                        emptied(pe, "col", n - 3)
                    for h in range(4 * n, 4 * n + 4):
                        last = tr(PS[:, n % 4, 128 * (h % 4):128 * (h % 4) + 128], x_t[:, h, :])
                    last.then_inc(S("col_filled"), 1)
                    if n >= 4:
                        gram(n - 4)
            pe.wait_ge(S("w_in"), 16 * SMALL_IN)
            pe.wait_ge(S("prm"), 16 * len(ROW_AT))
            pe.wait_ge(S("qk_c"), 1)
            for k in range(4):
                tr(PS[:, 4, 16 * k:16 * k + 16], qk_c[:, k, :, :])
            tr(PS[:, 5, 0:128], w_t)
            tr(PS[:, 5, 128:256], v_t).then_inc(S("wt_filled"), 1)
            for n in range(28, 31):
                gram(n)
            gram(31).then_inc(S("gf_filled"), 1)

            pe.wait_ge(S("const_in"), 16)
            for g, k in enumerate(P1_N):
                if g >= 4:
                    emptied(pe, "p1", g - 3)
                for j in range(k):
                    last = mm(PS[:, g % 4, NF * j:NF * j + NF], x_w[:, :, 7 * g + j], basis)
                last.then_inc(S("p1_filled"), 1)
            emptied(pe, "p1", len(P1_N))
            pe.wait_ge(S("edge_x"), 1)
            for k in range(2):
                last = mm(PS[0:64, 6, 256:384], edge_fn[:, 64 * k:64 * k + 64], edge_x[:, k, :], k == 0, k == 1)
            last.then_inc(S("edge_t_filled"), 1)
            pe.wait_ge(S("wt"), 1)
            for w in range(1, 17):
                o = PS[:, 4 + (w - 1) // 8, 64 * ((w - 1) % 8):64 * ((w - 1) % 8) + 64]
                mm(o, p1[:, COS[w], :], row_modes[:, 0:64], True, False)
                last = mm(o, p1[:, SIN[w], :], row_modes[:, 64:128], False, True)
            last.then_inc(S("modes_filled"), 1)
            for j in range(8):
                if j >= 4:
                    emptied(pe, "rx", j - 3)
                for half in range(2):
                    o = PS[64 * half:64 * half + 64, j % 4, :]
                    f = 32 * half + 4 * j
                    last = mm(o, gram_fn, p1[:, f:f + 4, :])
                last.then_inc(S("rx_filled"), 1)
                if j == 4:
                    pe.wait_ge(S("xlow"), 1)
                    tr(PS[:, 4, 0:128], xlow[:, 0, :, :])
                    tr(PS[:, 4, 128:256], xlow[:, 1, :, :]).then_inc(S("xlow_filled"), 1)
            emptied(pe, "rx", 8)
            pe.wait_ge(S("gf"), 1)
            for j in range(32):
                mm(PS[:, 7, 0:128], rx[:, j, :], rx[:, j, :], j == 0, False)
            pe.wait_ge(S("edge_t"), 1)
            mm(PS[:, 7, 0:128], edge_t, edge_t, False, True).then_inc(S("g_filled"), 1)
            pe.wait_ge(S("g_s"), 1)
            tr(PS[:, 6, 384:512], g_s).then_inc(S("g_t_filled"), 1)
            pe.wait_ge(S("u"), 1)
            for part, u in enumerate((u_re, u_im)):
                for b in range(NB):
                    tb = slice(TB * b, TB * b + TB)
                    last = mm(PS[tb, 5, :], xlow_t[:, part, tb], u[:, :, tb], part == 0, part == 1,
                              skip_group_check=True)
            last.then_inc(S("s_filled"), 1)

            def attend(hg):
                for a in range(2):
                    pe.wait_ge(S("prod_dve"), 8 * hg + 4 * a + 4)
                    pe.wait_ge(S("prod_pool"), 5 * hg + 4 * a + 1)
                    for k in range(2):
                        for b in range(NB):
                            tb = slice(TB * b, TB * b + TB)
                            rhs = prod(4 * hg + b)[:, a, 8 * k:8 * k + 8, :, :].rearrange("p w v h -> p (w v h)")
                            last = mm(PS[tb, 2 + k, :], prob_t[:, hg, tb], rhs, hg == 0 and a == 0,
                                      hg == 3 and a == 1, skip_group_check=True)
                return last

            pe.wait_ge(S("prob"), 1)
            for k in range(4):
                last = tr(PS[:, 4, 128 * k:128 * k + 128], prob[:, 4 * k:4 * k + 4, :])
            last.then_inc(S("pt_filled"), 1)
            pe.wait_ge(S("prob_t"), 1)
            attend(0).then_inc(S("prod_used"), 1)
            pe.wait_ge(S("cbd"), 1)
            tr(PS[:, 6, 0:128], cbd).then_inc(S("c_filled"), 1)
            attend(1).then_inc(S("prod_used"), 1)
            pe.wait_ge(S("cft"), 1)
            tr(PS[:, 6, 128:256], cft)
            mm(PS[:, 6, 256:384], cft, gf).then_inc(S("k1_filled"), 1)
            for k in range(2):
                last = mm(bank(k), cft, t0[:, 512 * k:512 * k + 512])
            last.then_inc(S("cx_filled"), 1)
            attend(2).then_inc(S("prod_used"), 1)
            attend(3)
            mm(PS[0:1, 6, 0:1], ones[0:1, 0:1], ones[0:1, 0:1]).then_inc(S("y_filled"), 1)
            pe.wait_ge(S("dg"), 1)
            mm(PS[:, 6, 384:512], ones, dg).then_inc(S("bc_filled"), 1)
            def transposes(i, z3, n, zb):
                if n % 4 == 0:
                    pe.wait_ge(S(f"z3_{i}"), n // 4 + 1)
                for p in range(4 * n, 4 * n + 4):
                    part, w = p // 16, p % 16
                    last = tr(PS[0:64, zb + n % 4, 128 * (p % 4):128 * (p % 4) + 128], z3[:, w, 1 - part:3 - part, :])
                last.then_inc(S(f"zt{i}_filled"), 1)

            def rows(i, ta, tb):
                for n in range(8):
                    if n >= 4:
                        emptied(pe, f"ta{i}", n - 3)
                    for g in range(4 * n, 4 * n + 4):
                        last = mm(PS[:, tb + n % 4, 128 * (g % 4):128 * (g % 4) + 128],
                                  zt[:, 4 * g:4 * g + 4, :], fr[0:64, :])
                    last.then_inc(S(f"ta{i}_filled"), 1)

            pe.wait_ge(S("acft"), 1)
            for g in range(32):
                if g >= 4:
                    pe.wait_ge(S("a0"), g - 3)
                for w in range(4 * g, 4 * g + 4):
                    last = mm(PS[:, 4 + g % 4, 128 * (w % 4):128 * (w % 4) + 128], x_t[:, :, w], acft)
                last.then_inc(S("mix_filled"), 1)
                if g == 3:
                    pe.wait_ge(S("kap_dg"), 1)
                    mm(PS[:, 3, 0:128], ones, dg).then_inc(S("kap_filled"), 1)
                if g >= 24:
                    n = g - 24
                    if n == 0:
                        pe.wait_ge(S("kap"), 1)
                    if n >= 4:
                        pe.wait_ge(S("zt1"), n - 3)
                    transposes(1, z3_1, n, 0)
            pe.wait_ge(S("zt1"), 8)
            rows(1, ta1, 0)
            emptied(pe, "ta1", 8)
            pe.wait_ge(S("a0"), 32)
            for turn in range(0, G4 + LAG_P2, 4):
                for i in range(turn, min(turn + 4, G4)):
                    if i >= 6:
                        pe.wait_ge(S("u_sum"), i - 5)
                    mm(bank(i % 6), ta1[:, i, :], block_w).then_inc(S("b1_filled"), 1)
                for g in range(max(turn - LAG_P2, 0), min(turn - LAG_P2 + 4, G4)):
                    n, j = 4 * g // P2_T, 4 * g % P2_T
                    if j == 0 and n >= 2:
                        pe.wait_ge(S("p2"), n - 1)
                    pe.wait_ge(S("m1"), g + 1)
                    for k in range(4):
                        last = mm(PS[:, 6 + n % 2, 33 * (j + k):33 * (j + k) + 33], m1[:, 4 * g + k, :], basis17)
                    if j + 4 == P2_N[n]:
                        last.then_inc(S("p2_filled"), 1)
            pe.wait_ge(S("p2"), len(P2_N))
            pe.wait_ge(S("u_sum"), G4)
            for k, (bk, a) in X1_AT.items():
                n = 68 if 0 < k < 16 else 34
                o, fn = PS[:, bk, a:a + n], p2[:, k, :]
                cos = col_modes[:, 0:34].unsqueeze(1).to_broadcast([128, n // 34, 34])
                last = mm(o, fn, cos, True, k == 0)
                if k:
                    sin = col_modes[:, 34:102] if k < 16 else col_modes[:, 68:102]
                    last = mm(o, p2[:, 16 + k, :], sin, False, True)
                if k in (7, 14, 16):
                    last.then_inc(S("x1_filled"), 1)
                if k == 7:
                    pe.wait_ge(S("rowsq"), 1)
                    mm(PS[:, 3, 0:1], dg, ones[:, 0:1]).then_inc(S("sq_filled"), 1)
            def skip_factors(n):
                if n == 4:
                    pe.wait_ge(S("dg2"), 1)
                    mm(PS[:, 3, 128:256], ones, dg)
                    pe.wait_ge(S("z0"), 1)
                    tr(PS[0:64, 3, 256:384], z0).then_inc(S("z0t_filled"), 1)
                if n == 7:
                    pe.wait_ge(S("z0t"), 1)
                    mm(PS[:, 3, 384:512], fr[0:64, :], z0t).then_inc(S("g0_filled"), 1)

            for n in range(8):
                if n >= 4:
                    emptied(pe, "zt2", n - 3)
                transposes(2, z3_2, n, 4)
                skip_factors(n)
            emptied(pe, "zt2", 8)
            pe.wait_ge(S("g0"), 1)
            rows(2, ta2, 0)
            emptied(pe, "ta2", 8)

            for i in range(G4 + LAG_W):
                if i < G4:
                    if i >= 4:
                        pe.wait_ge(S("x1"), i - 3)
                    mm(bank(4 + i % 4), ta2[:, i, :], block_w).then_inc(S("b2_filled"), 1)
                g = i - LAG_TR
                if 0 <= g < G4:
                    pe.wait_ge(S("ln2_act"), g + 1)
                    if LN2_ACT[g % 2] < 4:
                        pe.wait_ge(S("ln2_dve"), LN2_DVE[g])
                    if g >= 2:
                        pe.wait_ge(S("lnw"), g - 1)
                    for j in range(4):
                        last = tr(PS[:, g % 2, 128 * j:128 * j + 128], m1[:, 4 * g + j, :])
                    last.then_inc(S("lnw_filled"), 1)
                g = i - LAG_W
                if g >= 0:
                    pe.wait_ge(S("lnw"), g + 1)
                    if g >= 2:
                        pe.wait_ge(S("wx"), g - 1)
                    mm(bank(2 + g % 2), w_t, ln_w[:, g % 2]).then_inc(S("wx_filled"), 1)

            def sweep(n, k0, j0):
                for dj in range(2):
                    for g in range(GR):
                        if dj:
                            pe.wait_ge(S("state"), GR * k0 + g + 1)
                        else:
                            pe.wait_ge(S("start"), n * GR + (g + 1))
                        mm(sums(g, dj), v_t, at(y_s, g, j0) if dj else start(g)).then_inc(S("vy"), 1)
                with pe.Fori(1, (STEPS - j0) // 2) as i:
                    for dj in range(2):
                        for g in range(GR):
                            pe.wait_ge(S("state"), i * (2 * GR) + (GR * (k0 + dj) + g + 1 - GR))
                            mm(sums(g, dj), v_t, at(y_s, g, i * 2 + (j0 + dj - 1))).then_inc(S("vy"), 1)

            def judge(p):
                pe.wait_ge(S("gap"), 1)
                tr(PS[0:1, 0, 0:128], s("gap")).then_inc(S("gap_filled"), 1)

            recur(pe, sweep, None, judge)
            for g in range(G4):
                if g >= 8:
                    pe.wait_ge(S("result"), g - 7)
                for j in range(4):
                    last = tr(PS[:, g % 8, 128 * j:128 * j + 128],
                              y_s[:, :, :, 4 * g + j].rearrange("d q j -> d (q j)"))
                last.then_inc(S("yt_filled"), 1)

        @block.scalar
        def _(act):
            def load_table(function):
                act.activation(sc[0:1, 59:60], ident[0:1, 0:1], function)

            roots = [0]

            def root(o, i):
                roots[0] += 1
                act.wait_ge(S("root_of"), roots[0])
                act.activation(o, i, ACT.Sqrt).then_inc(S("root"), 1)

            for c in range(XC):
                root(ln_r[:, XR * c:XR * c + XR], ln_tmp[:, c % 2, :])
                if c:
                    empty(act, "col", 4 * c - 4, 4 * c, move_col)
                act.wait_ge(S("ln_coef"), c + 1)
                for row in range(XR * c + LN_DVE + LN_POOL, XR * c + XR):
                    last = act.activation(x_t[:, row, :], x_t[:, row, :], ACT.Identity,
                                          scale=ln_r[:, row:row + 1], bias=ln_b[:, row:row + 1])
                last.then_inc(S("ln_act"), 1)
            empty(act, "col", 4 * XC - 4, 4 * XC, move_col)
            act.wait_ge(S("wt_filled"), 1)
            act.activation(aqk.rearrange("m k n -> m (k n)"), PS[:, 4, 0:64], ACT.Copy)
            act.activation(w_t, PS[:, 5, 0:128], ACT.Copy)
            act.activation(v_t, PS[:, 5, 128:256], ACT.Copy).then_inc(S("wt"), 1)
            root(s("s1"), s("rt"))
            act.wait_ge(S("s1"), 1)
            empty(act, "p1", 0, len(P1_N), move_p1)
            act.wait_ge(S("t0"), 1)
            act.activation(ts, modes_ps, ACT.Copy, scale=s("s1")).then_inc(S("ts"), 1)
            empty(act, "rx", 0, 8, move_rx)
            load_table(ACT.Exp)
            act.wait_ge(S("s_shift"), 1)
            act.activation(prob, scr, ACT.Exp).then_inc(S("s_exp"), 1)
            act.wait_ge(S("pt_filled"), 1)
            act.activation(prob_t.rearrange("p g t -> p (g t)"), bank(4), ACT.Copy).then_inc(S("prob_t"), 1)
            load_table(ACT.Sqrt)
            act.wait_ge(S("cx_filled"), 1)
            act.activation(cx, cx_ps, ACT.Copy).then_inc(S("cx"), 1)
            act.wait_ge(S("cx"), 1)
            act.activation(sq_dump, cx, ACT.Square, accum_out=s("p_cx")).then_inc(S("p_cx"), 1)
            act.wait_ge(S("ma"), 1)
            act.activation(ztmp, ma, ACT.Square, accum_out=s("p_ma")).then_inc(S("p_ma"), 1)
            root(s("al"), s("rt"))
            root(s("rm"), s("rt"))
            for g in range(32):
                if g == 6:
                    act.wait_ge(S("zw"), 1)
                    act.activation(ztmp, zw, ACT.Square, accum_out=s("p_z1")).then_inc(S("p_z1"), 1)
                if g == 14:
                    root(s("r1"), s("rt"))
                act.wait_ge(S("mix_filled"), g + 1)
                act.activation(a0[:, :, 4 * g:4 * g + 4],
                               PS[:, 4 + g % 4, :].rearrange("h (w t) -> h t w", w=4), ACT.Copy).then_inc(S("a0"), 1)
            load_table(ACT.Gelu)
            empty(act, "ta1", 0, 8, move_ta(ta1, 0))
            for i in range(G4 + LAG_M2):
                if i < G4:
                    act.wait_ge(S("u_sum"), i + 1)
                    v = m1[:, 4 * i:4 * i + 4, :]
                    act.activation(v, v, ACT.Gelu, bias=s("cu")).then_inc(S("m1"), 1)
                g = i - LAG_M2
                if g >= 0 and (4 * g + 4) % P2_T == 0 or g == G4 - 1:
                    n = 4 * g // P2_T
                    act.wait_ge(S("p2_filled"), n + 1)
                    move_p2(act, n).then_inc(S("p2"), 1)
            load_table(ACT.Sqrt)
            act.wait_ge(S("z2"), 1)
            act.activation(z2q.rearrange("t (k w) -> t k w", w=MW),
                           z2.rearrange("t h v w -> t (h v) w")[:, :, 1:17], ACT.Square,
                           accum_out=s("p_z2")).then_inc(S("p_z2"), 1)
            root(s("r2"), s("rt"))
            root(s("ro"), s("rt"))
            empty(act, "zt2", 0, 8, move_zt(4))
            act.wait_ge(S("xa"), G4)
            empty(act, "ta2", 0, 8, move_ta(ta2, 0))

            for i in range(G4 + LAG_WX):
                if i % 4 == 1 and 0 <= i // 4 - 1 < XC:
                    c = i // 4 - 1
                    root(ln_r[:, XR * c:XR * c + XR], ln_tmp[:, c % 2, :])
                g = i - LAG_LN
                if 0 <= g < G4:
                    act.wait_ge(S("ln2_coef"), g // 4 + 1)
                    for n in range(4 * g, 4 * g + LN2_ACT[g % 2]):
                        last = act.activation(m1[:, n, :], a0[:, n, :], ACT.Identity,
                                              scale=ln_r[:, n:n + 1], bias=ln_b[:, n:n + 1])
                    last.then_inc(S("ln2_act"), 1)
                g = i - LAG_MV
                if 0 <= g < G4:
                    if g >= 2:
                        act.wait_ge(S("wx_filled"), g - 1)
                    act.wait_ge(S("lnw_filled"), g + 1)
                    move_lnw(act, g).then_inc(S("lnw"), 1)
                g = i - LAG_WX
                if g >= 0:
                    act.wait_ge(S("wx_filled"), g + 1)
                    act.activation(wx(g), bank(2 + g % 2).rearrange("d (h t) -> d h t", t=4),
                                   ACT.Copy).then_inc(S("wx"), 1)
            root(s("bs"), s("rt"))
            act.wait_ge(S("bn_ab"), 1)
            act.wait_ge(S("bn"), G4)
            def sweep(n, k0, j0):
                for dj in range(2):
                    for g in range(GR):
                        act.wait_ge(S("vy_wx"), GR * (k0 + dj) + g + 1)
                        act.activation(at(y_s, g, j0 + dj), sums(g, dj), ACT.Sigmoid, bias=s("bb")).then_inc(S("state"), 1)
                with act.Fori(1, (STEPS - j0) // 2) as i:
                    for dj in range(2):
                        for g in range(GR):
                            act.wait_ge(S("vy_wx"), i * (2 * GR) + (GR * (k0 + dj) + g + 1))
                            act.activation(at(y_s, g, i * 2 + (j0 + dj)), sums(g, dj),
                                           ACT.Sigmoid, bias=s("bb")).then_inc(S("state"), 1)

            recur(act, sweep)

        @block.vector
        def _(dve):
            seq = [0]

            def link(ins):
                seq[0] += 1
                ins.then_inc(S("dve_seq"), 1)
                dve.wait_ge(S("dve_seq"), seq[0])

            TT, TS, STT = dve.tensor_tensor, dve.tensor_scalar, dve.scalar_tensor_tensor
            roots = [0]

            def ask_root(i, eps):
                TS(s("rt"), i, eps, None, ALU.add).then_inc(S("root_of"), 1)

            def inv_root(o, i, eps, times=None):
                ask_root(i, eps)
                take_root(o, times)

            def take_root(o, times=None):
                roots[0] += 1
                dve.wait_ge(S("root"), roots[0])
                link(dve.reciprocal(o, o))
                if times is not None:
                    link(TT(o, o, times, ALU.mult))

            def ln_rows(c, src, n0, n1):
                for row in range(n0, n1):
                    last = dve.bn_stats(ln_st[:, c % 2, row, :], src[:, XR * c + row, :])
                return last

            def ln_moments(c, src, n0, eps, keep):
                st = ln_st[:, c % 2]
                link(ln_rows(c, src, n0, XR))
                d, m, dd, v = ln_tmp[:, 4, :], ln_tmp[:, 2 + c % 2, :], ln_tmp[:, 5, :], ln_tmp[:, 6, :]
                TT(m, st[:, :, 1], st[:, :, 4], ALU.add)
                TT(v, st[:, :, 2], st[:, :, 5], ALU.add)
                link(TT(d, st[:, :, 1], st[:, :, 4], ALU.subtract))
                TS(v, v, 1.0 / W, None, ALU.mult)
                link(STT(dd, d, 0.25, d, ALU.mult, ALU.mult))
                keep = keep[:, XR * c:XR * c + XR] if keep is not None else d
                link(TT(keep, dd, v, ALU.add))
                TS(ln_tmp[:, c % 2, :], keep, eps, None, ALU.add).then_inc(S("root_of"), 1)

            def ln_coefs(c, done):
                roots[0] += 1
                dve.wait_ge(S("root"), roots[0])
                rs, b = ln_r[:, XR * c:XR * c + XR], ln_b[:, XR * c:XR * c + XR]
                link(dve.reciprocal(rs, rs))
                STT(b, ln_tmp[:, 2 + c % 2, :], -0.5, rs, ALU.mult, ALU.mult).then_inc(S(done), 1)
                dve.wait_ge(S(done), c + 1)

            dve.wait_ge(S("x_in0"), 16)
            ln_moments(0, x_t, 0, LN_C_EPS, row_var)
            for c in range(XC):
                if c + 1 < XC:
                    dve.wait_ge(S(f"x_in{c + 1}"), 16)
                    ln_moments(c + 1, x_t, 0, LN_C_EPS, row_var)
                ln_coefs(c, "ln_coef")
                for row in range(XR * c, XR * c + LN_DVE):
                    last = TS(x_t[:, row, :], x_t[:, row, :], ln_r[:, row:row + 1], ln_b[:, row:row + 1], ALU.mult, ALU.add)
                last.then_inc(S("ln_dve"), 1)
                if c:
                    empty(dve, "col", 4 * c - 4, 4 * c, move_col)
            empty(dve, "col", 4 * XC - 4, 4 * XC, move_col)
            link(TT(vr, row_var, ln_r, ALU.mult))
            link(TT(vr, vr, ln_r, ALU.mult))
            link(dve.tensor_reduce(s("v0"), vr, AX.X, ALU.add))
            link(TS(s("v0"), s("v0"), 1.0 / H, None, ALU.mult))
            dve.wait_ge(S("prm"), 16 * len(ROW_AT))
            inv_root(s("s1"), s("v0"), EPS, prm("norm1_g"))
            dve.tensor_copy(s("x0"), s("s1")).then_inc(S("s1"), 1)
            dve.wait_ge(S("gf_filled"), 1)
            dve.tensor_copy(gf, PS[:, 7, 0:NT]).then_inc(S("gf"), 1)
            dve.wait_ge(S("wt"), 1)
            wq, wk = prm("query_skip_w"), prm("key_skip_w")
            TT(wqk, wq, wk, ALU.mult)
            TT(aqk[:, 0, :], aqk[:, 0, :], wq, ALU.add)
            TT(pswv, prm("proj_skip_w"), prm("value_skip_w"), ALU.mult)
            link(TT(aqk[:, 2, :], aqk[:, 2, :], wk, ALU.add))
            for part, (p, q, op) in enumerate((((0, 2), (1, 3), ALU.add), ((0, 3), (1, 2), ALU.subtract))):
                link(TT(mqk[:, part, :], aqk[:, p[0], :], aqk[:, p[1], :], ALU.mult))
                link(TT(mqt, aqk[:, q[0], :], aqk[:, q[1], :], ALU.mult))
                link(TT(mqk[:, part, :], mqk[:, part, :], mqt, op))
            link(TT(mqk[:, 0, :], mqk[:, 0, :], wqk, ALU.subtract))
            link(TS(mqk[:, :, :], mqk[:, :, :], 128.0, None, ALU.mult))
            emptied(dve, "col", 32)
            for k in range(8):
                empty(dve, "p1", 2 * k, 2 * k + 2, move_p1)
                half = slice(64 * (k % 2), 64 * (k % 2) + 64)
                last = dve.tensor_reduce(row_sum[:, k // 2, half], x_w[:, k // 2::4, half].rearrange("w h t -> w t h"),
                                         AX.X, ALU.add)
            link(last)
            TT(edge_x[:, 0, :], row_sum[:, 0, :], row_sum[:, 2, :], ALU.subtract)
            TT(edge_x[:, 1, :], row_sum[:, 1, :], row_sum[:, 3, :], ALU.subtract).then_inc(S("edge_x"), 1)
            empty(dve, "p1", 16, len(P1_N), move_p1)
            dve.wait_ge(S("modes_filled"), 1)
            dve.tensor_copy(t0, modes_ps).then_inc(S("t0"), 1)
            dve.wait_ge(S("ts"), 1)
            dve.wait_ge(S("wy"), 4)
            tsm = modes(ts)
            for k, lo in enumerate((slice(0, 8), slice(24, 32))):
                last = dve.tensor_copy(xlow[:, :, :, 8 * k:8 * k + 8],
                                       tsm[:, 0:LW, :, lo].rearrange("t w v h -> t v w h"))
            last.then_inc(S("xlow"), 1)
            empty(dve, "rx", 0, 4, move_rx)
            dve.wait_ge(S("xlow_filled"), 1)
            dve.tensor_copy(xlow_t.rearrange("m v t -> m (v t)"), PS[:, 4, 0:256]).then_inc(S("m_low"), 1)
            empty(dve, "rx", 4, 8, move_rx)
            dve.wait_ge(S("edge_t_filled"), 1)
            dve.tensor_copy(edge_t, PS[0:64, 6, 256:384]).then_inc(S("edge_t"), 1)
            dve.wait_ge(S("m_low"), 1)
            mb = mqk[:, 0, :].unsqueeze(2).to_broadcast([128, NH, NT])
            xb = [xlow_t[:, k, :].unsqueeze(1).to_broadcast([128, NH, NT]) for k in range(2)]
            TT(u_re, mb, xb[0], ALU.mult)
            link(TT(u_im, mb, xb[1], ALU.mult))
            dve.wait_ge(S("g_filled"), 1)
            TS(g_s, PS[:, 7, 0:NT], s("s1"), None, ALU.mult).then_inc(S("g_s"), 1)
            dve.wait_ge(S("u_prod"), 1)
            TT(u_re, u_re, u_p, ALU.subtract)
            dve.wait_ge(S("u_prod"), 2)
            TT(u_im, u_im, u_q, ALU.add).then_inc(S("u"), 1)
            dve.wait_ge(S("g_t_filled"), 1)
            dve.memset(cbd, 0.0)
            for b in range(NB):
                tb = slice(TB * b, TB * b + TB)
                last = TS(g_c[tb, :], PS[tb, 6, 384 + TB * b:384 + TB * b + TB], sc[tb, scn["s1"]:scn["s1"] + 1],
                          None, ALU.mult)
            link(last)
            link(TT(stmp, wqk.unsqueeze(2).to_broadcast([128, NH, TB]),
                    g_c.unsqueeze(1).to_broadcast([128, NH, TB]), ALU.mult))
            dve.wait_ge(S("s_filled"), 1)
            link(TT(scr, stmp, PS[:, 5, :].rearrange("t (n s) -> t n s", s=TB), ALU.add))
            link(dve.tensor_reduce(smax, scr, AX.X, ALU.max))
            TT(scr, scr, smax.unsqueeze(2).to_broadcast([128, NH, TB]), ALU.subtract).then_inc(S("s_shift"), 1)

            def product_re(hg, b):
                n = 1 if b == 3 else 2
                TT(prod(4 * hg + b)[:, 0, :, 0:n], xrep[:, b, :, 0:n],
                   wr[:, hg, :, 0:1, :].to_broadcast([128, MW, n, MH]), ALU.mult).then_inc(S("prod_dve"), 1)

            dve.wait_ge(S("rep"), 16 * 32)
            product_re(0, 0)
            dve.wait_ge(S("s_exp"), 1)
            link(dve.tensor_reduce(ssum, prob, AX.X, ALU.add))
            link(dve.reciprocal(ssum, ssum))
            TT(prob, prob, ssum.unsqueeze(2).to_broadcast([128, NH, TB]), ALU.mult).then_inc(S("prob"), 1)
            dve.wait_ge(S("prob"), 1)

            def products(hg, b0=0):
                if hg >= 2:
                    dve.wait_ge(S("prod_used"), hg - 1)
                for b in range(b0, NB):
                    product_re(hg, b)
                for b in range(NB):
                    STT(prod(4 * hg + b)[:, 1, :, 0, :], xrep[:, b, :, 1, :], -1.0, wr[:, hg, :, 1, :],
                        ALU.mult, ALU.mult).then_inc(S("prod_dve"), 1)

            products(0, 1)
            link(TT(stmp, prob, pswv.unsqueeze(2).to_broadcast([128, NH, TB]), ALU.mult))
            link(dve.tensor_reduce(c32, stmp.rearrange("t n s -> t s n"), AX.X, ALU.add))
            for b in range(NB):
                tb = slice(TB * b, TB * b + TB)
                last = dve.tensor_copy(cbd[tb, tb], c32[tb, :])
            last.then_inc(S("cbd"), 1)
            products(1)
            dve.wait_ge(S("c_filled"), 1)
            STT(cft, PS[:, 6, 0:NT], s("s1"), ident, ALU.mult, ALU.add).then_inc(S("cft"), 1)
            dve.wait_ge(S("k1_filled"), 1)
            link(dve.tensor_copy(cf, PS[:, 6, 128:256]))
            link(TT(k1x, PS[:, 6, 256:384], cf, ALU.mult))
            link(dve.tensor_reduce(s("q"), k1x, AX.X, ALU.add))
            link(TS(s("q"), s("q"), 1.0 / PIX, None, ALU.mult))
            products(2)
            products(3)
            dve.wait_ge(S("p_cx"), 1)
            link(STT(s("q"), s("p_cx"), -2.0, s("q"), ALU.mult, ALU.add))
            dve.wait_ge(S("y_filled"), 1)
            TT(ma, cx, y_ps, ALU.add).then_inc(S("ma"), 1)
            link(dve.tensor_copy(y_m, y_ps))
            dve.wait_ge(S("ma"), 1)
            dve.wait_ge(S("p_ma"), 1)
            link(STT(s("va"), s("p_ma"), 2.0, s("q"), ALU.mult, ALU.add))
            inv_root(s("al"), s("va"), EPS, prm("attn_norm_g"))
            TS(dg, ident, s("al"), None, ALU.mult).then_inc(S("dg"), 1)
            link(TT(s("x0"), s("al"), s("al"), ALU.mult))
            link(TT(s("x0"), s("x0"), s("va"), ALU.mult))
            dve.wait_ge(S("bc_filled"), 1)
            TT(acft, cft, PS[:, 6, 384:512], ALU.mult).then_inc(S("acft"), 1)
            inv_root(s("rm"), s("x0"), EPS, prm("norm2_g"))
            link(TT(s("kappa"), s("rm"), prm("mixer_skip_w1"), ALU.mult))
            TS(dg, ident, s("kappa"), None, ALU.mult).then_inc(S("kap_dg"), 1)
            TT(s("sm"), s("rm"), s("al"), ALU.mult)
            w1 = prm("mixer_w1").rearrange("t (h w v) -> t v w h", v=2, w=17)[:, :, 1:17, :]
            mam, zwm, ztm, ym = modes(ma), modes(zw), modes(ztmp), modes(y_m)
            TT(zwm[:, :, 0, :], mam[:, :, 0, :], w1[:, 0], ALU.mult)
            TT(zwm[:, :, 1, :], mam[:, :, 0, :], w1[:, 1], ALU.mult)
            TT(ztm[:, :, 0, :], mam[:, :, 1, :], w1[:, 1], ALU.mult)
            link(TT(ztm[:, :, 1, :], mam[:, :, 1, :], w1[:, 0], ALU.mult))
            TT(zwm[:, :, 0, :], zwm[:, :, 0, :], ztm[:, :, 0, :], ALU.subtract)
            TT(zwm[:, :, 1, :], zwm[:, :, 1, :], ztm[:, :, 1, :], ALU.add).then_inc(S("zw"), 1)
            dve.wait_ge(S("zw"), 1)
            link(TS(y_m, y_m, s("al"), None, ALU.mult))
            dve.wait_ge(S("kap_filled"), 1)
            dve.tensor_copy(kap, PS[:, 3, 0:NT]).then_inc(S("kap"), 1)
            link(TT(s("x0"), s("sm"), s("sm"), ALU.mult))
            dve.wait_ge(S("p_z1"), 1)
            link(STT(s("x0"), s("p_z1"), 2.0, s("x0"), ALU.mult, ALU.mult))
            inv_root(s("r1"), s("x0"), EPS, prm("mixer_norm_g1"))
            link(TT(s("f1"), s("r1"), s("sm"), ALU.mult))
            link(TS(ztmp, y_m, s("kappa"), None, ALU.mult))
            o = z3_1.rearrange("t w k h -> t w (k h)")[:, :, MH:3 * MH]
            STT(o, zw.rearrange("t (w k) -> t w k", w=MW), s("f1"),
                ztmp.rearrange("t (w k) -> t w k", w=MW), ALU.mult, ALU.add).then_inc(S("z3_1"), 1)
            dve.wait_ge(S("z3_1"), 1)
            TS(z3_1[:, :, 0, :], z3_1[:, :, 2, :], -1.0, None, ALU.mult).then_inc(S("z3_1"), 1)
            link(TT(s("cu"), prm("mixer_skip_w1"), prm("norm2_b"), ALU.mult))
            link(TT(s("cu"), s("cu"), prm("mixer_norm_b1"), ALU.add))
            link(TT(s("cu"), s("cu"), prm("mixer_skip_b1"), ALU.add))
            for n in range(8):
                dve.wait_ge(S("zt1_filled"), n + 1)
                move_zt(0)(dve, n).then_inc(S("zt1"), 1)
            empty(dve, "ta1", 0, 8, move_ta(ta1, 0))
            for i in range(G4 + 3):
                if i < G4:
                    dve.wait_ge(S("ka0"), i + 1)
                    dve.wait_ge(S("b1_filled"), i + 1)
                    v = m1[:, 4 * i:4 * i + 4, :].rearrange("h t w -> h (t w)")
                    TT(v, bank(i % 6), v, ALU.add).then_inc(S("u_sum"), 1)
                if 0 <= i - 3 < G4:
                    dve.wait_ge(S("m1"), i - 2)
                    for n in range(4 * (i - 3), 4 * (i - 3) + 4):
                        last = dve.bn_stats(st2[:, n, :], m1[:, n, :])
            link(last)
            TT(kap, st2[:, :, 1], st2[:, :, 1], ALU.mult)
            TT(bet, st2[:, :, 4], st2[:, :, 4], ALU.mult)
            link(TT(dg, st2[:, :, 2], st2[:, :, 5], ALU.add))
            link(TT(kap, kap, bet, ALU.add))
            STT(dg, kap, float(W // 2), dg, ALU.mult, ALU.add).then_inc(S("rowsq"), 1)
            for bk, k0, n in ((0, 1, 7), (1, 8, 7), (2, 15, 1)):
                dve.wait_ge(S("x1_filled"), bk + 1)
                v = PS[:, bk, 0:68 * n].rearrange("t (k s w) -> t s k w", s=2, w=34)
                dve.tensor_copy(x1m[:, k0:k0 + n].rearrange("t h v w -> t h (v w)"), v[:, 0])
                dve.tensor_copy(x1m[:, 32 - k0:32 - k0 - n:-1].rearrange("t h v w -> t h (v w)"), v[:, 1])
            dve.tensor_copy(x1m[:, 0].rearrange("t v w -> t (v w)"), PS[:, 2, 68:102])
            link(dve.tensor_copy(x1m[:, 16].rearrange("t v w -> t (v w)"), PS[:, 2, 102:136]))
            w2 = prm("mixer_w2").rearrange("t (h w v) -> t v h w", v=2, w=17)
            TT(z2[:, :, 0, :], x1m[:, :, 0, :], w2[:, 0], ALU.mult)
            TT(z2[:, :, 1, :], x1m[:, :, 0, :], w2[:, 1], ALU.mult)
            TT(z2t[:, :, 0, :], x1m[:, :, 1, :], w2[:, 1], ALU.mult)
            link(TT(z2t[:, :, 1, :], x1m[:, :, 1, :], w2[:, 0], ALU.mult))
            TT(z2[:, :, 0, :], z2[:, :, 0, :], z2t[:, :, 0, :], ALU.subtract)
            TT(z2[:, :, 1, :], z2[:, :, 1, :], z2t[:, :, 1, :], ALU.add).then_inc(S("z2"), 1)
            dve.wait_ge(S("z2"), 1)
            gg = z2g
            TT(gg[:, 0:15], z2[:, 1:16, 0, 0], z2[:, 31:16:-1, 0, 0], ALU.add)
            TT(gg[:, 15:30], z2[:, 1:16, 1, 0], z2[:, 31:16:-1, 1, 0], ALU.subtract)
            link(dve.tensor_copy(gg[:, 30:32], z2[:, 16, :, 0]))
            link(TT(gg, gg, gg, ALU.mult))
            link(dve.tensor_reduce(s("g2"), gg, AX.X, ALU.add))
            link(TS(s("g2"), s("g2"), 0.5, None, ALU.mult))
            dve.wait_ge(S("p_z2"), 1)
            link(STT(s("v2"), s("p_z2"), 2.0, s("g2"), ALU.mult, ALU.add))
            ask_root(s("v2"), EPS)
            k2, mean1 = prm("mixer_skip_w2"), s("mean1")
            link(TT(z2t.rearrange("t h v w -> t (h v w)"), z2.rearrange("t h v w -> t (h v w)"),
                    x1m.rearrange("t h v w -> t (h v w)"), ALU.mult))
            dve.tensor_reduce(s("cov"), z2t.rearrange("t h v w -> t (h v) w")[:, :, 1:17], AX.XY, ALU.add)
            link(dve.tensor_reduce(s("cov0"), z2t[:, 1:32, :, 0], AX.XY, ALU.add))
            link(STT(s("cov"), s("cov"), 2.0, s("cov0"), ALU.mult, ALU.add))
            link(STT(s("kc"), s("cov"), 2.0, k2, ALU.mult, ALU.mult))
            dve.tensor_copy(mean1, x1m[:, 0, 0, 0:1])
            link(TT(s("m1sq"), x1m[:, 0, 0, 0:1], x1m[:, 0, 0, 0:1], ALU.mult))
            dve.wait_ge(S("sq_filled"), 1)
            link(STT(s("vm1"), PS[:, 3, 0:1], 1.0 / PIX, s("m1sq"), ALU.mult, ALU.subtract))
            link(TS(s("kv"), s("vm1"), k2, k2, ALU.mult, ALU.mult))
            TT(s("cb"), prm("mixer_out_b"), prm("attn_norm_b"), ALU.add)
            take_root(s("r2"), prm("mixer_norm_g2"))
            link(STT(s("x0"), s("v2"), s("r2"), s("kc"), ALU.mult, ALU.add))
            link(STT(s("x0"), s("x0"), s("r2"), s("kv"), ALU.mult, ALU.add))
            inv_root(s("ro"), s("x0"), EPS, prm("mixer_out_g"))
            link(TT(s("alpha"), s("ro"), s("r2"), ALU.mult))
            for part in range(2):
                last = STT(z3_2[:, :, 1 + part, :], z2[:, :, part, 1:17].rearrange("t h w -> t w h"), s("alpha"),
                           ym[:, :, part, :], ALU.mult, ALU.add)
            last.then_inc(S("z3_2"), 1)
            dve.wait_ge(S("z3_2"), 1)
            TS(z3_2[:, :, 0, :], z3_2[:, :, 2, :], -1.0, None, ALU.mult).then_inc(S("z3_2"), 1)
            TS(dg, ident, s("ro"), k2, ALU.mult, ALU.mult).then_inc(S("dg2"), 1)
            link(TT(s("bt"), s("ro"), k2, ALU.mult))
            link(TT(s("x1"), s("bt"), mean1, ALU.mult))
            TS(z0.rearrange("t (v h) -> t v h", v=2)[:, 0, :], z2[:, :, 0, 0], s("alpha"), None, ALU.mult)
            link(TS(z0.rearrange("t (v h) -> t v h", v=2)[:, 1, :], z2[:, :, 1, 0], s("alpha"), None, ALU.mult))
            TT(z0[:, 0:1], s("cb"), s("x1"), ALU.subtract).then_inc(S("z0"), 1)
            empty(dve, "zt2", 0, 6, move_zt(4))
            dve.wait_ge(S("z0t_filled"), 1)
            dve.tensor_copy(bet, PS[:, 3, 128:256]).then_inc(S("bet"), 1)
            dve.tensor_copy(z0t, PS[0:64, 3, 256:384]).then_inc(S("z0t"), 1)
            empty(dve, "zt2", 6, 8, move_zt(4))
            dve.wait_ge(S("g0_filled"), 1)
            dve.tensor_copy(g0, PS[:, 3, 384:512]).then_inc(S("g0"), 1)
            dve.wait_ge(S("xa"), G4)
            empty(dve, "ta2", 0, 8, move_ta(ta2, 0))

            for i in range(G4 + LAG_BN):
                g = i - 1
                if 0 <= g < G4:
                    v = a0[:, 4 * g:4 * g + 4, :].rearrange("h t w -> h (t w)")
                    dve.wait_ge(S("xm"), g + 1)
                    dve.wait_ge(S("b2_filled"), g + 1)
                    TT(v, v, bank(4 + g % 4), ALU.add).then_inc(S("x1"), 1)
                    dve.wait_ge(S("x1"), g + 1)
                    if g % 4 == 3:
                        ln_moments(g // 4, a0, 12, EPS, None)
                    else:
                        ln_rows(g // 4, a0, 4 * (g % 4), 4 * (g % 4) + 4)
                g = i - LAG_LN
                if 0 <= g < G4 and LN2_ACT[g % 2] < 4:
                    for n in range(4 * g + LN2_ACT[g % 2], 4 * g + 4):
                        last = TS(m1[:, n, :], a0[:, n, :], ln_r[:, n:n + 1], ln_b[:, n:n + 1], ALU.mult, ALU.add)
                    last.then_inc(S("ln2_dve"), 1)
                g = i - LAG_BN
                if g >= 0:
                    dve.wait_ge(S("wx"), g + 1)
                    dve.bn_stats(bn_st[:, g, :], wx(g)).then_inc(S("bn"), 1)
                if i % 4 == 1 and 0 <= i // 4 - 1 < XC:
                    ln_coefs(i // 4 - 1, "ln2_coef")
            dve.memset(start_a, 0.0).then_inc(S("start"), GR)
            dve.memset(start_b[:, 0, 0:NT:TB], 0.0)
            dve.wait_ge(S("bn"), G4)
            link(dve.bn_aggr(sc[:, 60:62], bn_st.rearrange("d g c -> d (g c)")))
            inv_root(s("bs"), sc[:, 61:62], EPS, s("gamma"))
            link(TT(s("x0"), sc[:, 60:61], s("bs"), ALU.mult))
            TT(s("bb"), s("beta"), s("x0"), ALU.subtract).then_inc(S("bn_ab"), 1)
            dve.wait_ge(S("bn_ab"), 1)

            def add_z(b, dj, j):
                STT(sums(b, dj), wx_step[:, b, :, bass.ds(j, 1), :], s("bs"), sums(b, dj),
                    ALU.mult, ALU.add).then_inc(S("vy_wx"), 1)

            def sweep(n, k0, j0):
                for dj in range(2):
                    for g in range(GR):
                        dve.wait_ge(S("vy"), GR * (k0 + dj) + g + 1)
                        add_z(g, dj, j0 + dj)
                with dve.Fori(1, (STEPS - j0) // 2) as i:
                    for dj in range(2):
                        for g in range(GR):
                            dve.wait_ge(S("vy"), i * (2 * GR) + (GR * (k0 + dj) + g + 1))
                            add_z(g, dj, i * 2 + (j0 + dj))

            def starts(k):
                for g in range(GR):
                    dve.wait_ge(S("state"), k * GR + (g + 1 - GR))
                    a, b = TB * g, TB * g + TB
                    last = y_s[:, :, STEPS - 1, a:b]
                    dve.tensor_copy(start_a[:, 1:Q, a:b], last[:, 0:Q - 1, :])
                    dve.tensor_copy(start_a[:, 0, a + 1:b], last[:, Q - 1, 0:TB - 1]).then_inc(S("start"), 1)

            def judge(k):
                dve.wait_ge(S("x1_g0"), G4)
                for g in range(GR):
                    dve.wait_ge(S("state"), k * GR + (g + 1 - GR))
                    a, b = TB * g, TB * g + TB
                    last = y_s[:, :, STEPS - 1, a:b]
                    TT(start_b[:, 1:Q, a:b], last[:, 0:Q - 1, :], start_a[:, 1:Q, a:b], ALU.subtract)
                    end = TT(start_b[:, 0, a + 1:b], last[:, Q - 1, 0:TB - 1], start_a[:, 0, a + 1:b],
                             ALU.subtract)
                link(end)
                link(TT(start_b, start_b, start_b, ALU.mult))
                dve.tensor_reduce(s("gap"), start_b, AX.XY, ALU.max).then_inc(S("gap"), 1)
                dve.wait_ge(S("gap_filled"), 1)
                link(dve.tensor_reduce(sc[0:1, 63:64], PS[0:1, 0, 0:NT], AX.X, ALU.max))
                link(TS(sc[0:1, 63:64], sc[0:1, 63:64], TOL * TOL, None, ALU.is_le))
                TS(FLAG[0:1, 0:1], sc[0:1, 63:64], -1.0, 1.0, ALU.mult, ALU.add).then_inc(S("judged"), 1)

            recur(dve, sweep, starts, judge)
            for g in range(G4):
                dve.wait_ge(S("yt_filled"), g + 1)
                dve.wait_ge(S("x1_g0"), g + 1)
                v = a0[:, 4 * g:4 * g + 4, :].rearrange("h t w -> h (t w)")
                TT(v, v, bank(g % 8), ALU.add).then_inc(S("result"), 1)


_NAMES = ["x", "L0_conv_key_w", "L0_conv_key_skip_w", "L0_conv_query_w", "L0_conv_query_skip_w",
          "L0_conv_value_w", "L0_conv_value_skip_w", "L0_conv_proj_w", "L0_conv_proj_skip_w",
          "L0_conv_norm1_g", "L0_conv_attn_norm_g", "L0_conv_attn_norm_b", "L0_conv_norm2_g",
          "L0_conv_norm2_b", "L0_conv_mixer_w1", "L0_conv_mixer_skip_w1", "L0_conv_mixer_skip_b1",
          "L0_conv_mixer_norm_g1", "L0_conv_mixer_norm_b1", "L0_conv_mixer_w2",
          "L0_conv_mixer_skip_w2", "L0_conv_mixer_norm_g2", "L0_conv_mixer_out_g",
          "L0_conv_mixer_out_b", "L0_ffn_W", "L0_ffn_V", "L0_ffn_gamma", "L0_ffn_beta"]


def kernel(**inputs):
    import concourse.bacc as bacc
    from concourse.bass_utils import run_bass_kernel_spmd as run

    nc = bacc.Bacc("TRN2", target_bir_lowering=False, num_devices=1)
    arrays, tensors = {}, {}
    for name in _NAMES + ["const"]:
        a = np.ascontiguousarray(CONST if name == "const" else inputs[name])
        arrays[f"in_{name}"] = a
        tensors[name.replace("L0_conv_", "").replace("L0_ffn_", "")] = nc.dram_tensor(
            f"in_{name}", a.shape, mybir.dt.from_np(a.dtype), kind="ExternalInput").ap()
    out = nc.dram_tensor("out_x", inputs["x"].shape, F32, kind="ExternalOutput").ap()
    metaformer(nc, tensors, out)
    r = run(nc, [arrays], core_ids=[0])
    return r.results[0]["out_x"]
```
